# Optimizing a Trainium2 kernel written in Bass

```python
import numpy as np
import jax
import jax.numpy as jnp

def _softmax(x, axis=-1):
    return jax.nn.softmax(x, axis=axis)

def _gelu(x):
    return jax.nn.gelu(x, approximate=True)

def _silu(x):
    return jax.nn.silu(x)

def _sigmoid(x):
    return jax.nn.sigmoid(x)

def _layernorm(x, axis=-1, eps=1e-05):
    m = jnp.mean(x, axis=axis, keepdims=True)
    v = jnp.var(x, axis=axis, keepdims=True)
    return (x - m) / jnp.sqrt(v + eps)

def _scatter_add(tgt, idx, src, axis=0):
    return tgt.at[idx].add(src)

def _segment_sum(src, seg, n):
    return jax.ops.segment_sum(src, seg, n)
kernel_name = 'mk_adaln_d2_jaxref_r4_744113'

def setup_inputs(seed: int=0):
    np.random.seed(seed)
    _w = jnp.asarray

    def _L0_attn_setup():
        import math
        import jax, jax.numpy as jnp
        import numpy as np
        D_MODEL = 256
        N_HEADS = 16
        HEAD_DIM = D_MODEL // N_HEADS
        B, L = (1, 1024)

        def _slopes(n_heads):
            ratio = 2.0 ** (-8.0 / n_heads)
            return jnp.asarray([ratio ** (i + 1) for i in range(n_heads)], dtype=jnp.float32)
        key = jax.random.key(seed)
        ks = jax.random.split(key, 5)
        scale = 1.0 / math.sqrt(D_MODEL)
        return {'x': jax.random.normal(ks[0], (B, L, D_MODEL), dtype=jnp.float32), 'q_w': jax.random.normal(ks[1], (D_MODEL, D_MODEL), dtype=jnp.float32) * scale, 'k_w': jax.random.normal(ks[2], (D_MODEL, D_MODEL), dtype=jnp.float32) * scale, 'v_w': jax.random.normal(ks[3], (D_MODEL, D_MODEL), dtype=jnp.float32) * scale, 'o_w': jax.random.normal(ks[4], (D_MODEL, D_MODEL), dtype=jnp.float32) * scale}
    _L0_attn_in = _L0_attn_setup()

    def _L0_ffn_setup():
        import jax, jax.numpy as jnp
        import numpy as np
        DIM = 256

        def _reference_tuple_inner(x, W_r, W_k, W_v, mu_r, mu_k):
            B, T, C = x.shape
            x_prev = jnp.concatenate([jnp.zeros((B, 1, C), x.dtype), x[:, :-1, :]], axis=1)
            xr = mu_r * x + (1.0 - mu_r) * x_prev
            xk = mu_k * x + (1.0 - mu_k) * x_prev
            r = jax.nn.sigmoid(jnp.einsum('btc,dc->btd', xr, W_r))
            k = jnp.einsum('btc,dc->btd', xk, W_k)
            k_act = jnp.square(jax.nn.relu(k))
            out = r * jnp.einsum('btc,dc->btd', k_act, W_v)
            new_state = x[:, -1, :]
            return (out, new_state)
        key = jax.random.key(seed)
        ks = jax.random.split(key, 6)
        B, T, C = (8, 512, DIM)
        x = jax.random.normal(ks[0], (B, T, C), dtype=jnp.float32)
        s = 1.0 / np.sqrt(C)
        W_r = jax.random.uniform(ks[1], (C, C), jnp.float32, -s, s)
        W_k = jax.random.uniform(ks[2], (C, C), jnp.float32, -s, s)
        W_v = jax.random.uniform(ks[3], (C, C), jnp.float32, -s, s)
        mu_r = jax.random.uniform(ks[4], (C,), jnp.float32)
        mu_k = jax.random.uniform(ks[5], (C,), jnp.float32)
        return {'x': x, 'W_r': W_r, 'W_k': W_k, 'W_v': W_v, 'mu_r': mu_r, 'mu_k': mu_k}
    _L0_ffn_in = _L0_ffn_setup()
    _L0_c = _w((lambda *s: np.random.randn(*s).astype(np.float32) * 0.05)(8, 256))
    _L0_wmod = _w((lambda *s: np.random.randn(*s).astype(np.float32) * 0.05)(256, 6 * 256) * 256 ** (-0.5))

    def _L1_attn_setup():
        import jax, jax.numpy as jnp
        import numpy as np
        B, T, DIM = (2, 1024, 256)
        DEPTH, HEADS = (4, 8)
        DH = DIM // HEADS
        NLOCAL, WINDOW, BUCKET = (4, 128, 64)
        MULT = 4

        def layer_norm(x, g, b, eps=1e-05):
            m = jnp.mean(x, -1, keepdims=True)
            v = jnp.mean(jnp.square(x - m), -1, keepdims=True)
            return (x - m) * jax.lax.rsqrt(v + eps) * g + b

        def causal_linear_attn(q, k, v):
            b, h, n, e = q.shape
            u = n // BUCKET
            q = jax.nn.softmax(q, axis=-1)
            k = jax.nn.elu(k) + 1.0
            bq = q.reshape(b, h, u, BUCKET, e)
            bk = k.reshape(b, h, u, BUCKET, e)
            bv = v.reshape(b, h, u, BUCKET, e)
            k_cum = jnp.cumsum(bk.sum(axis=-2), axis=-2)
            ctx = jnp.einsum('bhund,bhune->bhude', bk, bv)
            ctx = jnp.cumsum(ctx, axis=2)
            ctx = ctx / (k_cum[..., None] + 1e-06)
            ctx = jnp.pad(ctx, ((0, 0), (0, 0), (1, 0), (0, 0), (0, 0)))[:, :, :-1]
            out = jnp.einsum('bhund,bhude->bhune', bq, ctx)
            return out.reshape(b, h, n, e)

        def local_attn(q, k, v):
            b, lh, t, e = q.shape
            bh = b * lh
            nb = t // WINDOW
            bq = q.reshape(bh, nb, WINDOW, e)
            bk = k.reshape(bh, nb, WINDOW, e)
            bv = v.reshape(bh, nb, WINDOW, e)

            def look_around(x):
                padded = jnp.pad(x, ((0, 0), (1, 0), (0, 0), (0, 0)))
                return jnp.concatenate([padded[:, :-1], padded[:, 1:]], axis=2)
            bk2 = look_around(bk)
            bv2 = look_around(bv)
            tix = jnp.arange(t).reshape(1, nb, WINDOW)
            tpad = jnp.pad(tix, ((0, 0), (1, 0), (0, 0)), constant_values=-1)
            kix = jnp.concatenate([tpad[:, :-1], tpad[:, 1:]], axis=2)
            dots = jnp.einsum('bwie,bwje->bwij', bq, bk2) * e ** (-0.5)
            mask_value = -jnp.finfo(dots.dtype).max
            causal_mask = tix[:, :, :, None] < kix[:, :, None, :]
            pad_mask = (kix == -1)[:, :, None, :]
            dots = jnp.where(causal_mask | pad_mask, mask_value, dots)
            attn = jax.nn.softmax(dots, axis=-1)
            out = jnp.einsum('bwij,bwje->bwie', attn, bv2)
            return out.reshape(b, lh, t, e)

        def self_attention(x, Wq, Wk, Wv, Wo, bo):
            b, t, _ = x.shape
            mh = lambda z: z.reshape(b, t, HEADS, DH).transpose(0, 2, 1, 3)
            q, k, v = (mh(x @ Wq), mh(x @ Wk), mh(x @ Wv))
            lo = local_attn(q[:, :NLOCAL], k[:, :NLOCAL], v[:, :NLOCAL])
            go = causal_linear_attn(q[:, NLOCAL:], k[:, NLOCAL:], v[:, NLOCAL:])
            out = jnp.concatenate([lo, go], axis=1)
            out = out.transpose(0, 2, 1, 3).reshape(b, t, DIM)
            return out @ Wo + bo
        key = jax.random.key(seed)
        ks = jax.random.split(key, 8)
        s = 0.02
        rn = lambda k, shape: jax.random.normal(k, shape, dtype=jnp.float32) * s
        return {'x': jax.random.normal(ks[0], (B, T, DIM), dtype=jnp.float32), 'Wq': rn(ks[1], (DEPTH, DIM, DIM)), 'Wk': rn(ks[2], (DEPTH, DIM, DIM)), 'Wv': rn(ks[3], (DEPTH, DIM, DIM)), 'Wo': rn(ks[4], (DEPTH, DIM, DIM)), 'bo': jnp.zeros((DEPTH, DIM), jnp.float32), 'ln1_g': jnp.ones((DEPTH, DIM), jnp.float32), 'ln1_b': jnp.zeros((DEPTH, DIM), jnp.float32), 'W1': rn(ks[5], (DEPTH, DIM, DIM * MULT)), 'b1': jnp.zeros((DEPTH, DIM * MULT), jnp.float32), 'W2': rn(ks[6], (DEPTH, DIM * MULT, DIM)), 'b2': jnp.zeros((DEPTH, DIM), jnp.float32), 'ln2_g': jnp.ones((DEPTH, DIM), jnp.float32), 'ln2_b': jnp.zeros((DEPTH, DIM), jnp.float32)}
    _L1_attn_in = _L1_attn_setup()

    def _L1_ffn_setup():
        import jax, jax.numpy as jnp
        import numpy as np
        NH, NKV, E, K = (16, 4, 8, 2)
        CAP_FACTOR = 1.25
        LN_EPS = 1e-05

        def _layer_norm(x, w, b):
            mu = jnp.mean(x, axis=-1, keepdims=True)
            var = jnp.mean(jnp.square(x - mu), axis=-1, keepdims=True)
            return (x - mu) * jax.lax.rsqrt(var + LN_EPS) * w + b
        key = jax.random.key(seed)
        ks = jax.random.split(key, 6)
        S, B, H, F = (512, 1, 256, 512)
        HD = H // NH
        qkv_out = NKV * (NH // NKV + 2) * HD
        f32 = jnp.float32
        return {'hidden_states': jax.random.normal(ks[0], (S, B, H), f32), 'ln1_weight': jnp.ones((H,), f32), 'ln1_bias': jnp.zeros((H,), f32), 'ln2_weight': jnp.ones((H,), f32), 'ln2_bias': jnp.zeros((H,), f32), 'qkv_weight': jax.random.normal(ks[1], (qkv_out, H), f32) * 0.02, 'proj_weight': jax.random.normal(ks[2], (H, H), f32) * 0.02, 'router_weight': jax.random.normal(ks[3], (H, E), f32) * 0.02, 'moe_w1': jax.random.normal(ks[4], (E, H, F), f32) * 0.02, 'moe_w2': jax.random.normal(ks[5], (F and E, F, H), f32)[:E] * 0.02 if False else jax.random.normal(ks[5], (E, F, H), f32) * 0.02}
    _L1_ffn_in = _L1_ffn_setup()
    _L1_c = _w((lambda *s: np.random.randn(*s).astype(np.float32) * 0.05)(8, 256))
    _L1_wmod = _w((lambda *s: np.random.randn(*s).astype(np.float32) * 0.05)(256, 6 * 256) * 256 ** (-0.5))
    _d = {'L0_attn_x': _L0_attn_in['x'], 'L0_attn_q_w': _L0_attn_in['q_w'], 'L0_attn_k_w': _L0_attn_in['k_w'], 'L0_attn_v_w': _L0_attn_in['v_w'], 'L0_attn_o_w': _L0_attn_in['o_w'], 'L0_ffn_W_r': _L0_ffn_in['W_r'], 'L0_ffn_W_k': _L0_ffn_in['W_k'], 'L0_ffn_W_v': _L0_ffn_in['W_v'], 'L0_ffn_mu_r': _L0_ffn_in['mu_r'], 'L0_ffn_mu_k': _L0_ffn_in['mu_k'], 'L0_c': _L0_c, 'L0_wmod': _L0_wmod, 'L1_attn_Wq': _L1_attn_in['Wq'], 'L1_attn_Wk': _L1_attn_in['Wk'], 'L1_attn_Wv': _L1_attn_in['Wv'], 'L1_attn_Wo': _L1_attn_in['Wo'], 'L1_attn_bo': _L1_attn_in['bo'], 'L1_attn_ln1_g': _L1_attn_in['ln1_g'], 'L1_attn_ln1_b': _L1_attn_in['ln1_b'], 'L1_attn_W1': _L1_attn_in['W1'], 'L1_attn_b1': _L1_attn_in['b1'], 'L1_attn_W2': _L1_attn_in['W2'], 'L1_attn_b2': _L1_attn_in['b2'], 'L1_attn_ln2_g': _L1_attn_in['ln2_g'], 'L1_attn_ln2_b': _L1_attn_in['ln2_b'], 'L1_ffn_ln1_weight': _L1_ffn_in['ln1_weight'], 'L1_ffn_ln1_bias': _L1_ffn_in['ln1_bias'], 'L1_ffn_ln2_weight': _L1_ffn_in['ln2_weight'], 'L1_ffn_ln2_bias': _L1_ffn_in['ln2_bias'], 'L1_ffn_qkv_weight': _L1_ffn_in['qkv_weight'], 'L1_ffn_proj_weight': _L1_ffn_in['proj_weight'], 'L1_ffn_router_weight': _L1_ffn_in['router_weight'], 'L1_ffn_moe_w1': _L1_ffn_in['moe_w1'], 'L1_ffn_moe_w2': _L1_ffn_in['moe_w2'], 'L1_c': _L1_c, 'L1_wmod': _L1_wmod}
    _x0 = _d['L0_attn_x']
    _d['L0_attn_x'] = jax.random.normal(jax.random.fold_in(jax.random.key(seed), 1), (8, 512, 256), dtype=_x0.dtype)
    del _x0
    return _d

def reference(L0_attn_x, L0_attn_q_w, L0_attn_k_w, L0_attn_v_w, L0_attn_o_w, L0_ffn_W_r, L0_ffn_W_k, L0_ffn_W_v, L0_ffn_mu_r, L0_ffn_mu_k, L0_c, L0_wmod, L1_attn_Wq, L1_attn_Wk, L1_attn_Wv, L1_attn_Wo, L1_attn_bo, L1_attn_ln1_g, L1_attn_ln1_b, L1_attn_W1, L1_attn_b1, L1_attn_W2, L1_attn_b2, L1_attn_ln2_g, L1_attn_ln2_b, L1_ffn_ln1_weight, L1_ffn_ln1_bias, L1_ffn_ln2_weight, L1_ffn_ln2_bias, L1_ffn_qkv_weight, L1_ffn_proj_weight, L1_ffn_router_weight, L1_ffn_moe_w1, L1_ffn_moe_w2, L1_c, L1_wmod):

    def _L0_attn_ref(x, q_w, k_w, v_w, o_w):
        import math
        import jax, jax.numpy as jnp
        import numpy as np
        D_MODEL = 256
        N_HEADS = 16
        HEAD_DIM = D_MODEL // N_HEADS
        B, L = (1, 1024)

        def _slopes(n_heads):
            ratio = 2.0 ** (-8.0 / n_heads)
            return jnp.asarray([ratio ** (i + 1) for i in range(n_heads)], dtype=jnp.float32)
        b, l, _ = x.shape

        def proj(w):
            return (x @ w).reshape(b, l, N_HEADS, HEAD_DIM).transpose(0, 2, 1, 3)
        q, k, v = (proj(q_w), proj(k_w), proj(v_w))
        scale = math.sqrt(HEAD_DIM)
        scores = jnp.einsum('bhid,bhjd->bhij', q, k) / scale
        pos = jnp.arange(l)
        distance = jnp.abs(pos[None, :] - pos[:, None]).astype(jnp.float32)
        alibi = -distance[None, :, :] * _slopes(N_HEADS)[:, None, None]
        scores = scores + alibi[None]
        causal = pos[None, :] <= pos[:, None]
        scores = jnp.where(causal[None, None], scores, -jnp.inf)
        attn = jax.nn.softmax(scores, axis=-1)
        out = jnp.einsum('bhij,bhjd->bhid', attn, v)
        out = out.transpose(0, 2, 1, 3).reshape(b, l, D_MODEL)
        return out @ o_w

    def _L0_ffn_ref(x, W_r, W_k, W_v, mu_r, mu_k):
        import jax, jax.numpy as jnp
        import numpy as np
        DIM = 256

        def _reference_tuple_inner(x, W_r, W_k, W_v, mu_r, mu_k):
            B, T, C = x.shape
            x_prev = jnp.concatenate([jnp.zeros((B, 1, C), x.dtype), x[:, :-1, :]], axis=1)
            xr = mu_r * x + (1.0 - mu_r) * x_prev
            xk = mu_k * x + (1.0 - mu_k) * x_prev
            r = jax.nn.sigmoid(jnp.einsum('btc,dc->btd', xr, W_r))
            k = jnp.einsum('btc,dc->btd', xk, W_k)
            k_act = jnp.square(jax.nn.relu(k))
            out = r * jnp.einsum('btc,dc->btd', k_act, W_v)
            new_state = x[:, -1, :]
            return (out, new_state)
        return _reference_tuple_inner(x, W_r, W_k, W_v, mu_r, mu_k)[0]

    def _L1_attn_ref(x, Wq, Wk, Wv, Wo, bo, ln1_g, ln1_b, W1, b1, W2, b2, ln2_g, ln2_b):
        import jax, jax.numpy as jnp
        import numpy as np
        B, T, DIM = (2, 1024, 256)
        DEPTH, HEADS = (4, 8)
        DH = DIM // HEADS
        NLOCAL, WINDOW, BUCKET = (4, 128, 64)
        MULT = 4

        def layer_norm(x, g, b, eps=1e-05):
            m = jnp.mean(x, -1, keepdims=True)
            v = jnp.mean(jnp.square(x - m), -1, keepdims=True)
            return (x - m) * jax.lax.rsqrt(v + eps) * g + b

        def causal_linear_attn(q, k, v):
            b, h, n, e = q.shape
            u = n // BUCKET
            q = jax.nn.softmax(q, axis=-1)
            k = jax.nn.elu(k) + 1.0
            bq = q.reshape(b, h, u, BUCKET, e)
            bk = k.reshape(b, h, u, BUCKET, e)
            bv = v.reshape(b, h, u, BUCKET, e)
            k_cum = jnp.cumsum(bk.sum(axis=-2), axis=-2)
            ctx = jnp.einsum('bhund,bhune->bhude', bk, bv)
            ctx = jnp.cumsum(ctx, axis=2)
            ctx = ctx / (k_cum[..., None] + 1e-06)
            ctx = jnp.pad(ctx, ((0, 0), (0, 0), (1, 0), (0, 0), (0, 0)))[:, :, :-1]
            out = jnp.einsum('bhund,bhude->bhune', bq, ctx)
            return out.reshape(b, h, n, e)

        def local_attn(q, k, v):
            b, lh, t, e = q.shape
            bh = b * lh
            nb = t // WINDOW
            bq = q.reshape(bh, nb, WINDOW, e)
            bk = k.reshape(bh, nb, WINDOW, e)
            bv = v.reshape(bh, nb, WINDOW, e)

            def look_around(x):
                padded = jnp.pad(x, ((0, 0), (1, 0), (0, 0), (0, 0)))
                return jnp.concatenate([padded[:, :-1], padded[:, 1:]], axis=2)
            bk2 = look_around(bk)
            bv2 = look_around(bv)
            tix = jnp.arange(t).reshape(1, nb, WINDOW)
            tpad = jnp.pad(tix, ((0, 0), (1, 0), (0, 0)), constant_values=-1)
            kix = jnp.concatenate([tpad[:, :-1], tpad[:, 1:]], axis=2)
            dots = jnp.einsum('bwie,bwje->bwij', bq, bk2) * e ** (-0.5)
            mask_value = -jnp.finfo(dots.dtype).max
            causal_mask = tix[:, :, :, None] < kix[:, :, None, :]
            pad_mask = (kix == -1)[:, :, None, :]
            dots = jnp.where(causal_mask | pad_mask, mask_value, dots)
            attn = jax.nn.softmax(dots, axis=-1)
            out = jnp.einsum('bwij,bwje->bwie', attn, bv2)
            return out.reshape(b, lh, t, e)

        def self_attention(x, Wq, Wk, Wv, Wo, bo):
            b, t, _ = x.shape
            mh = lambda z: z.reshape(b, t, HEADS, DH).transpose(0, 2, 1, 3)
            q, k, v = (mh(x @ Wq), mh(x @ Wk), mh(x @ Wv))
            lo = local_attn(q[:, :NLOCAL], k[:, :NLOCAL], v[:, :NLOCAL])
            go = causal_linear_attn(q[:, NLOCAL:], k[:, NLOCAL:], v[:, NLOCAL:])
            out = jnp.concatenate([lo, go], axis=1)
            out = out.transpose(0, 2, 1, 3).reshape(b, t, DIM)
            return out @ Wo + bo
        for i in range(DEPTH):
            x = x + self_attention(layer_norm(x, ln1_g[i], ln1_b[i]), Wq[i], Wk[i], Wv[i], Wo[i], bo[i])
            h = layer_norm(x, ln2_g[i], ln2_b[i])
            x = x + (jax.nn.gelu(h @ W1[i] + b1[i], approximate=False) @ W2[i] + b2[i])
        return x

    def _L1_ffn_ref(hidden_states, ln1_weight, ln1_bias, ln2_weight, ln2_bias, qkv_weight, proj_weight, router_weight, moe_w1, moe_w2):
        import jax, jax.numpy as jnp
        import numpy as np
        NH, NKV, E, K = (16, 4, 8, 2)
        CAP_FACTOR = 1.25
        LN_EPS = 1e-05

        def _layer_norm(x, w, b):
            mu = jnp.mean(x, axis=-1, keepdims=True)
            var = jnp.mean(jnp.square(x - mu), axis=-1, keepdims=True)
            return (x - mu) * jax.lax.rsqrt(var + LN_EPS) * w + b
        S, B, H = hidden_states.shape
        HD = H // NH
        q_per_kv = NH // NKV
        ln1 = _layer_norm(hidden_states, ln1_weight, ln1_bias)
        qkv = jnp.einsum('sbh,oh->sbo', ln1, qkv_weight)
        qkv = qkv.reshape(S, B, NKV, (q_per_kv + 2) * HD)
        q = qkv[..., :q_per_kv * HD].reshape(S, B, NH, HD)
        k = qkv[..., q_per_kv * HD:(q_per_kv + 1) * HD]
        v = qkv[..., (q_per_kv + 1) * HD:]
        qb = jnp.transpose(q, (1, 2, 0, 3)).reshape(B, NKV, q_per_kv, S, HD)
        kb = jnp.transpose(k, (1, 2, 0, 3))
        vb = jnp.transpose(v, (1, 2, 0, 3))
        scale = 1.0 / np.sqrt(HD).astype(np.float32)
        scores = jnp.einsum('bgqsd,bgtd->bgqst', qb, kb) * scale
        causal = jnp.tril(jnp.ones((S, S), bool))
        scores = jnp.where(causal, scores, jnp.finfo(scores.dtype).min)
        attn = jax.nn.softmax(scores, axis=-1)
        ao = jnp.einsum('bgqst,bgtd->bgqsd', attn, vb)
        ao = ao.reshape(B, NH, S, HD)
        ao = jnp.transpose(ao, (2, 0, 1, 3)).reshape(S, B, H)
        proj = jnp.einsum('sbh,oh->sbo', ao, proj_weight)
        h1 = hidden_states + proj
        ln2 = _layer_norm(h1, ln2_weight, ln2_bias)
        x = ln2.reshape(-1, H)
        N = x.shape[0]
        logits = x @ router_weight
        probs = jax.nn.softmax(logits, axis=-1)
        top_p, top_i = jax.lax.top_k(probs, K)
        top_p = top_p / jnp.sum(top_p, axis=-1, keepdims=True)
        exp_idx = top_i.reshape(-1)
        exp_p = top_p.reshape(-1)
        order = jnp.argsort(exp_idx, stable=True)
        sorted_exp = exp_idx[order]
        counts = jnp.bincount(exp_idx, length=E)
        offsets = jnp.concatenate([jnp.zeros((1,), counts.dtype), jnp.cumsum(counts)[:-1]])
        within = jnp.arange(N * K) - offsets[sorted_exp]
        cap = int(np.ceil(N * K / E * CAP_FACTOR))
        T = E * cap
        valid = within < cap
        dst = jnp.where(valid, sorted_exp * cap + within, T)
        padded_tokens = jnp.zeros((T, H), x.dtype).at[dst].set(x[order // K], mode='drop')
        padded_probs = jnp.zeros((T,), exp_p.dtype).at[dst].set(exp_p[order], mode='drop')
        padded_tid = jnp.zeros((T,), jnp.int32).at[dst].set((order // K).astype(jnp.int32), mode='drop')
        xt = padded_tokens.reshape(E, cap, H)
        fc1 = jax.nn.gelu(jnp.einsum('ech,ehf->ecf', xt, moe_w1))
        fc2 = jnp.einsum('ecf,efh->ech', fc1, moe_w2).reshape(T, H)
        weighted = fc2 * padded_probs[:, None]
        moe_out = jnp.zeros((N, H), hidden_states.dtype).at[padded_tid].add(weighted)
        return h1 + moe_out.reshape(S, B, H)
    x = L0_attn_x
    mod = (_silu(L0_c) @ L0_wmod).reshape(L0_c.shape[0], 6, 1, -1)
    sa, ca, ga, sb, cb, gb = (mod[:, 0], mod[:, 1], mod[:, 2], mod[:, 3], mod[:, 4], mod[:, 5])
    ga = (2 * (ga >= 0) - 1) * jnp.maximum(jnp.abs(ga), 0.25)
    gb = (2 * (gb >= 0) - 1) * jnp.maximum(jnp.abs(gb), 0.25)
    h = _layernorm(x, axis=-1) * (1 + ca) + sa
    x = x + ga * _L0_attn_ref(h, L0_attn_q_w, L0_attn_k_w, L0_attn_v_w, L0_attn_o_w)
    h = _layernorm(x, axis=-1) * (1 + cb) + sb
    x = x + gb * _L0_ffn_ref(h, L0_ffn_W_r, L0_ffn_W_k, L0_ffn_W_v, L0_ffn_mu_r, L0_ffn_mu_k)
    mod = (_silu(L1_c) @ L1_wmod).reshape(L1_c.shape[0], 6, 1, -1)
    sa, ca, ga, sb, cb, gb = (mod[:, 0], mod[:, 1], mod[:, 2], mod[:, 3], mod[:, 4], mod[:, 5])
    ga = (2 * (ga >= 0) - 1) * jnp.maximum(jnp.abs(ga), 0.25)
    gb = (2 * (gb >= 0) - 1) * jnp.maximum(jnp.abs(gb), 0.25)
    h = _layernorm(x, axis=-1) * (1 + ca) + sa
    x = x + ga * _L1_attn_ref(h, L1_attn_Wq, L1_attn_Wk, L1_attn_Wv, L1_attn_Wo, L1_attn_bo, L1_attn_ln1_g, L1_attn_ln1_b, L1_attn_W1, L1_attn_b1, L1_attn_W2, L1_attn_b2, L1_attn_ln2_g, L1_attn_ln2_b)
    h = _layernorm(x, axis=-1) * (1 + cb) + sb
    x = x + gb * _L1_ffn_ref(h, L1_ffn_ln1_weight, L1_ffn_ln1_bias, L1_ffn_ln2_weight, L1_ffn_ln2_bias, L1_ffn_qkv_weight, L1_ffn_proj_weight, L1_ffn_router_weight, L1_ffn_moe_w1, L1_ffn_moe_w2)
    return x

_drawn_inputs = setup_inputs


def setup_inputs(seed=0):
    import zlib

    import numpy as np

    out = dict(_drawn_inputs(seed))
    spreads = {'L1_attn_bo': (0.0, 0.749),
     'L1_attn_ln1_g': (1.0, 0.6),
     'L1_attn_ln1_b': (0.0, 0.8),
     'L1_attn_b1': (0.0, 1.798),
     'L1_attn_b2': (0.0, 0.8),
     'L1_attn_ln2_g': (1.0, 0.6),
     'L1_attn_ln2_b': (0.0, 2.0),
     'L1_ffn_ln1_weight': (1.0, 0.6),
     'L1_ffn_ln1_bias': (0.0, 0.8),
     'L1_ffn_ln2_weight': (1.0, 0.6),
     'L1_ffn_ln2_bias': (0.0, 2.0)}
    factors = {'L0_ffn_W_r': 8.0,
     'L0_ffn_W_k': 3.015,
     'L0_ffn_W_v': 2.761,
     'L0_ffn_mu_r': 8.0,
     'L0_ffn_mu_k': 5.01,
     'L1_attn_Wq': 8.0,
     'L1_attn_Wk': 8.0,
     'L1_attn_Wv': 5.304,
     'L1_attn_Wo': 5.5,
     'L1_ffn_qkv_weight': 3.5,
     'L1_ffn_proj_weight': 3.355,
     'L1_ffn_router_weight': 4.741,
     'L1_ffn_moe_w1': 4.218,
     'L1_ffn_moe_w2': 4.104}
    for name, (base, spread) in spreads.items():
        noise = np.random.default_rng([zlib.crc32(name.encode()), seed]).standard_normal(out[name].shape)
        drawn = base * np.exp(spread * noise) if base else spread * noise
        out[name] = jnp.asarray(drawn.astype(out[name].dtype))
    for name, factor in factors.items():
        out[name] = (out[name] * factor).astype(out[name].dtype)
    return out
```

```python
from contextlib import ExitStack

import concourse.bass as bass
from concourse import mybir

F32 = mybir.dt.float32
I32 = mybir.dt.int32
U32 = mybir.dt.uint32
ALU = mybir.AluOpType
ACT = mybir.ActivationFunctionType
AX = mybir.AxisListType

P = 128
B = 8
T = 512
NT = T // P
D = 256
KD = D // P
EPS = 1e-5
BIG = 1e30
GATE_MIN = 0.25
H0, HD0 = 16, 16
G0 = H0 // 4
DEPTH = 4
H1, HD1 = 8, 32
BUCKET = 64
NU = T // BUCKET
FF = 4 * D
MF = FF // P
NH, NKV, E, TOPK = 16, 4, 8, 2
HDM = D // NH
QKV = NKV * (NH // NKV + 2) * HDM
FM = 512
CAP = -(-(B * T * TOPK * 5) // (E * 4))
SEMS = ("load aux store resid_ready mod_ready "
        "vbank_full vbank_empty pbank_full pbank_empty sbank_full sbank_empty obank_full obank_empty "
        "stats_ready rstd_ready normed_ready scores_exped probs_ready "
        "carry_ready mixed_ready squared_ready v_chain p_chain s_chain settled "
        "attn_weights mlp_weights biased lin_shifted lin_exped lin_inverted lin_q_ready lin_k_ready "
        "context_ready lin_full lin_out gated scaled shifted "
        "products_ready products_used cross_shifted cross_exped cross_probs "
        "logits_shifted logits_exped chosen finished stored").split()


class Span:

    def __init__(self, start, turn, i):
        self.start, self.turn, self.i = start, turn, i

    def __call__(self, name, k=0):
        return self.start.get(name, 0) + self.i * self.turn.get(name, 0) + k


def after(start, turn, n):
    return {k: start.get(k, 0) + n * turn.get(k, 0) for k in {*start, *turn}}


class Chip:
    pass


def alone(c, eng):
    eng.sem_inc(c.s["settled"], 1)


def chain(c, eng, sem, ins):
    ins.then_inc(sem, 1)
    eng.wait_ge(sem, 1)
    eng.sem_clear(sem)



def ln_stats(c, dve, n, src):
    nc = c.nc
    dve.wait_ge(c.s["normed_ready"], n)
    alone(c, dve)
    for t in range(NT):
        ins = nc.vector.bn_stats(c.bn[:, t, :], src[:, t, :])
    chain(c, dve, c.s["v_chain"], ins)
    for t in range(NT):
        ins = nc.vector.bn_aggr(c.mv[:, t, :], c.bn[:, t, :])
    ins.then_inc(c.s["stats_ready"], 1)


def ln_rstd(c, pool, n):
    nc = c.nc
    pool.wait_ge(c.s["stats_ready"], n + 1)
    alone(c, pool)
    chain(c, pool, c.s["p_chain"], nc.gpsimd.tensor_scalar(c.ve[:, :], c.mv[:, :, 1], EPS, None, ALU.add))
    nc.gpsimd.tensor_tensor(c.rstd[:, :], c.ve[:, :], c.mhalf[:, :], ALU.pow).then_inc(c.s["rstd_ready"], 1)


def ln_norm(c, dve, n, src, sbank_before, dst=None):
    nc = c.nc
    dve.wait_ge(c.s["rstd_ready"], n + 1)
    if dst is None:
        dst = c.xn
        dve.wait_ge(c.s["sbank_full"], sbank_before)
    for t in range(NT):
        ins = nc.vector.tensor_scalar(dst[:, t, :], src[:, t, :], c.mv[:, t, 0:1], c.rstd[:, t:t + 1],
                                      ALU.subtract, ALU.mult)
    ins.then_inc(c.s["normed_ready"], 1)


def ln_turn(c, pe, n, sb):
    nc = c.nc
    pe.wait_ge(c.s["normed_ready"], n + 1)
    for half in range(KD):
        pe.wait_ge(c.s["sbank_empty"], sb + half - 1)
        for t in range(NT):
            ins = nc.tensor.transpose(c.sbank[half][:, t * P:(t + 1) * P], c.xn[:, t, half * P:(half + 1) * P],
                                      c.ident[:, :])
        ins.then_inc(c.s["sbank_full"], 1)


def ln_gain(c, act, sb, gain, shift):
    nc = c.nc
    for half in range(KD):
        act.wait_ge(c.s["sbank_full"], sb + half + 1)
        alone(c, act)
        nc.scalar.activation(c.hT[:, half, 1:T + 1], c.sbank[half][:, :], ACT.Identity, bias=shift(half),
                             scale=gain(half)).then_inc(c.s["sbank_empty"], 1)



LAG_N, LAG_T, LAG_PT, LAG_AV = 5, 6, 7, 8


class Heads:

    def __init__(self, quads, q_of, k_of, keys_of, mask_of, v_of, out_of, vb, mid=None):
        self.quads, self.q_of, self.k_of, self.keys_of = quads, q_of, k_of, keys_of
        self.mask_of, self.v_of, self.out_of, self.vb = mask_of, v_of, out_of, vb
        self.items = 4 * quads
        self.steps = self.items + LAG_AV + 4


def heads_pe(c, pe, n, h, mid):
    nc = c.nc

    def score(k):
        q, j = divmod(k, 4)
        keys = h.keys_of(q)
        pe.wait_ge(c.s["vbank_empty"], n("vb", h.vb + k - 1))
        nc.tensor.matmul(c.vbank[k % 2][:, 0:P * len(keys)], h.q_of(q, j), h.k_of(q, j, keys[0], keys[-1] + 1),
                         start=True, stop=True).then_inc(c.s["vbank_full"], 1)

    def turn(k):
        q, j = divmod(k, 4)
        if k >= 2:
            pe.wait_ge(c.s["pbank_empty"], n("pb", k - 1))
        pe.wait_ge(c.s["probs_ready"], n("pb", k + 1))
        for m in range(len(h.keys_of(q))):
            ins = nc.tensor.transpose(c.pbank[k % 2][:, m * P:(m + 1) * P], c.prob[:, k % 8, m * P:(m + 1) * P],
                                      c.ident[:, :])
        ins.then_inc(c.s["pbank_full"], 1)

    def values(q):
        pe.wait_ge(c.s["pbank_empty"], n("pb", 4 * q + 4))
        keys = h.keys_of(q)
        bank, cols = h.out_of(q)
        for m, key in enumerate(keys):
            for j in range(4):
                ins = nc.tensor.matmul(bank[32 * j:32 * j + 32, cols], h.v_of(q, j, key),
                                       c.probT[:, (4 * q + j) % 8, m * P:(m + 1) * P],
                                       start=(m == 0), stop=(m == len(keys) - 1), tile_position=(0, 32 * j))
        ins.then_inc(c.s["obank_full"], 1)

    for t in range(h.steps):
        if t < h.items:
            score(t)
        if 0 <= t - LAG_T < h.items:
            turn(t - LAG_T)
        q, r = divmod(t - LAG_AV - 3, 4)
        if r == 0 and 0 <= q < h.quads:
            values(q)
        mid(t)


def heads_dve(c, dve, n, h, mid):
    nc = c.nc
    for t in range(h.steps):
        if t < h.items:
            q, j = divmod(t, 4)
            width = P * len(h.keys_of(q))
            if t >= 4:
                dve.wait_ge(c.s["scores_exped"], n("pb", t - 3))
            dve.wait_ge(c.s["vbank_full"], n("vb", h.vb + t + 1))
            alone(c, dve)
            nc.vector.tensor_tensor_reduce(out=c.score[:, t % 4, 0:width], in0=c.vbank[t % 2][:, 0:width],
                                           in1=h.mask_of(q, j), scale=1.0, scalar=3e38, op0=ALU.add, op1=ALU.min,
                                           accum_out=c.least[:, t % 8:t % 8 + 1]).then_inc(c.s["vbank_empty"], 1)
        q, r = divmod(t - LAG_N, 4)
        if r == 0 and 0 <= q < h.quads:
            dve.wait_ge(c.s["scores_exped"], n("pb", 4 * q + 4))
            lo = 4 * (q % 2)
            chain(c, dve, c.s["v_chain"], nc.vector.reciprocal(c.rsum[:, lo:lo + 4], c.psum_of[:, lo:lo + 4]))
        k = t - LAG_N
        if 0 <= k < h.items:
            width = P * len(h.keys_of(k // 4))
            nc.vector.tensor_scalar(c.prob[:, k % 8, 0:width], c.prob[:, k % 8, 0:width], c.rsum[:, k % 8:k % 8 + 1],
                                    None, ALU.mult).then_inc(c.s["probs_ready"], 1)
        k = t - LAG_PT
        if 0 <= k < h.items:
            q = k // 4
            width = P * len(h.keys_of(q))
            dve.wait_ge(c.s["pbank_full"], n("pb", k + 1))
            if q >= 2:
                dve.wait_ge(c.s["obank_full"], n("av", q - 1))
            nc.vector.tensor_copy(c.probT[:, k % 8, 0:width], c.pbank[k % 2][:, 0:width])\
              .then_inc(c.s["pbank_empty"], 1)
        mid(t)


def heads_act(c, act, n, h, mid):
    nc = c.nc
    for k in range(h.items):
        q, j = divmod(k, 4)
        width = P * len(h.keys_of(q))
        if k >= 8:
            act.wait_ge(c.s["pbank_full"], n("pb", k - 7))
        act.wait_ge(c.s["vbank_empty"], n("vb", h.vb + k + 1))
        nc.scalar.activation(c.prob[:, k % 8, 0:width], c.score[:, k % 4, 0:width], ACT.Exp,
                             bias=c.least[:, k % 8:k % 8 + 1], scale=-1.0,
                             accum_out=c.psum_of[:, k % 8:k % 8 + 1]).then_inc(c.s["scores_exped"], 1)
        mid(k)


def nothing(t):
    pass


def loop(c, eng, n, body):
    alone(c, eng)
    with eng.Fori(0, n - 1) as i:
        body(i, True)
    body(n - 1, False)



CHUNK = {"sa": 0, "ca": 1, "ga": 2, "sb": 3, "cb": 4, "gb": 5}
BEGIN = {"vb": 2, "sb": 2, "ln": 1}
OPENING = {"vb": BEGIN["vb"] + 8, "sb": BEGIN["sb"], "ln": BEGIN["ln"]}


def opening(c, d):
    nc = c.nc
    with ExitStack() as st:
        def sb(name, shape, dt=F32):
            return st.enter_context(nc.sbuf_tensor(name, shape, dt))

        cT = sb("cT", [P, 2, KD, B])
        wm = sb("wm", [P, 2, KD, 6 * D])
        rows = sb("rows", [B, 2, 6 * D])
        sign = sb("sign", [B, D])
        ones = sb("ones", [P, P])
        block = st.enter_context(nc.Block())

        @block.sync
        def _(sp):
            for name, count in (("vbank_full", BEGIN["vb"]), ("vbank_empty", BEGIN["vb"]), ("sbank_full", BEGIN["sb"]),
                                ("sbank_empty", BEGIN["sb"]), ("stats_ready", BEGIN["ln"]), ("rstd_ready", BEGIN["ln"]),
                                ("normed_ready", BEGIN["ln"])):
                sp.sem_inc(c.s[name], count)
            for l in range(2):
                sp.dma_start(cT[:, l, :, :], d[f"c{l}"].rearrange("(k p) b -> p k b", p=P)).then_inc(c.s["load"], 16)
                sp.dma_start(wm[:, l, :, :], d[f"wmod{l}"].rearrange("(k p) n -> p k n", p=P))\
                  .then_inc(c.s["load"], 16)
            for b in range(B):
                sp.dma_start(c.x[:, b, :, :], d["x"][b].rearrange("(t p) n -> p t n", p=P))\
                  .then_inc(c.s["resid_ready"], 16)
            sp.wait_ge(c.s["mod_ready"], 2)
            sp.dma_start(c.mod_dram.rearrange("l b n -> b l n"), rows[:, :, :]).then_inc(c.s["store"], 16)
            sp.wait_ge(c.s["store"], 16)
            sp.wait_ge(c.s["resid_ready"], 16 * B)

        @block.scalar
        def _(act):
            act.wait_ge(c.s["load"], 64)
            nc.scalar.activation(cT[:, :, :, :], cT[:, :, :, :], ACT.Silu).then_inc(c.s["aux"], 1)

        @block.gpsimd
        def _(pool):
            nc.gpsimd.memset(c.mhalf[:, :], -0.5)
            chain(c, pool, c.s["p_chain"], nc.gpsimd.memset(ones[:, :], 1.0))
            nc.gpsimd.affine_select(out=c.ident[:, :], in_=ones[:, :], compare_op=ALU.is_equal, fill=0.0, base=0,
                                    pattern=[[-1, P]], channel_multiplier=1).then_inc(c.s["aux"], 1)

        @block.tensor
        def _(pe):
            pe.wait_ge(c.s["aux"], 2)
            n = BEGIN["vb"]
            for l in range(2):
                for m in range(3):
                    pe.wait_ge(c.s["vbank_empty"], n - 1)
                    for k in range(KD):
                        ins = nc.tensor.matmul(c.vbank[n % 2][0:B, :], cT[:, l, k, :], wm[:, l, k, m * T:(m + 1) * T],
                                               start=(k == 0), stop=(k == KD - 1))
                    ins.then_inc(c.s["vbank_full"], 1)
                    n += 1
            pe.wait_ge(c.s["mod_ready"], 2)
            for pair in (("sa", "ca"), ("sb", "cb")):
                pe.wait_ge(c.s["vbank_empty"], n - 1)
                for i, name in enumerate(pair):
                    for k in range(KD):
                        at = CHUNK[name] * D + k * P
                        ins = nc.tensor.transpose(c.vbank[n % 2][:, (i * KD + k) * B:(i * KD + k + 1) * B],
                                                  rows[:, 0, at:at + P], c.ident[0:B, 0:B])
                ins.then_inc(c.s["vbank_full"], 1)
                n += 1

        @block.vector
        def _(dve):
            n = BEGIN["vb"]
            for l in range(2):
                for m in range(3):
                    dve.wait_ge(c.s["vbank_full"], n + 1)
                    ins = nc.vector.tensor_copy(rows[:, l, m * T:(m + 1) * T], c.vbank[n % 2][0:B, :])
                    ins.then_inc(c.s["vbank_empty"], 1)
                    n += 1
                dve.wait_ge(c.s["vbank_empty"], n)
                for name in ("ca", "cb"):
                    at = CHUNK[name] * D
                    v = rows[:, l, at:at + D]
                    chain(c, dve, c.s["v_chain"], nc.vector.tensor_scalar(v, v, 1.0, None, ALU.add))
                for name in ("ga", "gb"):
                    at = CHUNK[name] * D
                    v = rows[:, l, at:at + D]
                    chain(c, dve, c.s["v_chain"], nc.vector.tensor_scalar(sign[:, :], v, 0.0, 2.0, ALU.is_ge, ALU.mult))
                    chain(c, dve, c.s["v_chain"], nc.vector.tensor_scalar(sign[:, :], sign[:, :], -1.0, None, ALU.add))
                    chain(c, dve, c.s["v_chain"], nc.vector.tensor_tensor(v, v, sign[:, :], ALU.mult))
                    ins = nc.vector.scalar_tensor_tensor(out=v, in0=v, scalar=GATE_MIN, in1=sign[:, :], op0=ALU.max,
                                                         op1=ALU.mult)
                    if name == "gb":
                        ins.then_inc(c.s["mod_ready"], 1)
                        dve.wait_ge(c.s["mod_ready"], l + 1)
                    else:
                        chain(c, dve, c.s["v_chain"], ins)
            for i in range(2):
                dve.wait_ge(c.s["vbank_full"], n + 1)
                nc.vector.tensor_copy(c.modT[:, 2 * i:2 * i + 2, :, :],
                                      c.vbank[n % 2][:, 0:2 * KD * B].rearrange("p (i k b) -> p i k b", k=KD, b=B))\
                  .then_inc(c.s["vbank_empty"], 1)
                n += 1
            dve.wait_ge(c.s["vbank_empty"], n)


def mod_rows(c, l, name):
    at = CHUNK[name] * D
    return c.mod_dram[l, :, at:at + D].partition_broadcast(P)



ATTN0 = {"vb": 4 + 2 + 4 * 16 + 2, "sb": 4 + 2, "pb": 64, "av": 16, "ob": 4, "ln": 1}
FFN0 = {"vb": 2, "sb": 6, "ln": 1, "mx": 1}


def one(ap, i):
    return ap[:, i:i + 1] if isinstance(i, int) else ap[:, bass.ds(i, 1)]


def layer0(c, d, start):
    nc = c.nc
    with ExitStack() as st:
        def sb(name, shape, dt=F32):
            return st.enter_context(nc.sbuf_tensor(name, shape, dt))

        gates = sb("gates0", [P, 2, B, D])
        wqk = sb("wqk0", [P, 2, KD, H0, 32])
        wv = sb("wv0", [P, KD, D])
        wo = sb("wo0", [P, G0, D])
        wf = sb("wf0", [P, 3, KD, D])
        mu = sb("mu0", [P, 2, KD])
        omu = sb("omu0", [P, 2, KD])
        qT = sb("qT0", [P, G0, T])
        kT = sb("kT0", [P, G0, T])
        vt = sb("vt0", [P, NT, H0, 32])
        aoT = sb("aoT0", [P, G0, T])
        mixT = qT[:, :, :].rearrange("p (i k) t -> p i k t", k=KD)
        carry = kT[:, :, :].rearrange("p (i k) t -> p i k t", k=KD)
        krelu, kact = aoT[:, 0:KD, :], aoT[:, KD:2 * KD, :]
        rsig = vt[:, :, 0:D // 32, :].rearrange("p t h e -> p t (h e)")
        slope_mask = c.y[:, :, :, :].rearrange("p (h b) t n -> p h (b t n)", h=2)\
            .rearrange("p h (i n) -> p (h i) n", n=T)
        tmp = sb("tmp0", [P, 2, D])
        s0 = after(start, {"sb": 2, "ln": 1}, 1)
        s1 = after(s0, ATTN0, B)
        end = after(after(s1, FFN0, B), {"sb": -2, "ln": -1}, 1)

        block = st.enter_context(nc.Block())

        def mod(i, b):
            return lambda k: one(c.modT[:, i, k, :], b)

        h = Heads(
            quads=4 * G0,
            q_of=lambda q, j: qT[32 * j:32 * j + HD0, q // 4, (q % 4) * P:(q % 4 + 1) * P],
            k_of=lambda q, j, lo, hi: kT[32 * j:32 * j + HD0, q // 4, lo * P:hi * P],
            keys_of=lambda q: list(range(q % 4 + 1)),
            mask_of=lambda q, j: slope_mask[:, 4 * (q // 4) + j, (3 - q % 4) * P:T],
            v_of=lambda q, j, key: vt[:, key, 4 * (q // 4) + j, :],
            out_of=lambda q: (c.obank[(q // 4) % 2], slice((q % 4) * P, (q % 4 + 1) * P)),
            vb=6)
        L = c.loaded

        @block.sync
        def _(sp):
            sp.wait_ge(c.s["aux"], 3)
            for i, name in enumerate(("qw", "kw")):
                for k in range(KD):
                    sp.dma_start(wqk[:, i, k, :, 0:HD0],
                                 d[name][k * P:(k + 1) * P, :].rearrange("p (h e) -> p h e", e=HD0))\
                      .then_inc(c.s["load"], 16)
            for j in range(4):
                sp.dma_start(wo[32 * j:32 * j + HD0, :, :],
                             d["ow"].rearrange("(g j e) n -> j e g n", j=4, e=HD0)[j]).then_inc(c.s["load"], 16)
            sp.dma_start(wv[:, :, :], d["vw"].rearrange("(k p) n -> p k n", p=P)).then_inc(c.s["load"], 16)
            for i, name in enumerate(("Wr", "Wk", "Wv")):
                sp.dma_start(wf[:, i, :, :], d[name].rearrange("(k p) n -> p k n", p=P)).then_inc(c.s["load"], 16)
            for i, name in enumerate(("mu_r", "mu_k")):
                sp.dma_start(mu[:, i, :], d[name]).then_inc(c.s["load"], 16)
            for i, name in enumerate(("ga", "gb")):
                sp.dma_start(gates[:, i, :, :], mod_rows(c, 0, name)).then_inc(c.s["load"], 16)
        loaded0 = L + 16 * 16

        @block.gpsimd
        def _(pool):
            nc.gpsimd.memset(wqk[:, :, :, :, :], 0.0)
            nc.gpsimd.memset(wo[:, :, :], 0.0)
            nc.gpsimd.memset(vt[:, :, :, :], 0.0)
            nc.gpsimd.memset(c.hT[:, :, 0:1], 0.0).then_inc(c.s["aux"], 1)
            ln_rstd(c, pool, start["ln"])
            dist = slope_mask[:, H0 - 1, :]
            chain(c, pool, c.s["p_chain"], nc.gpsimd.iota(dist, pattern=[[-1, T]], base=T - P, channel_multiplier=1,
                                                          allow_small_or_imprecise_dtypes=True))
            chain(c, pool, c.s["p_chain"], nc.gpsimd.affine_select(out=dist, in_=dist, compare_op=ALU.is_ge, fill=BIG,
                                                                   base=T - P, pattern=[[-1, T]],
                                                                   channel_multiplier=1))
            for i in range(H0):
                slope = float((2.0 ** (-8.0 / H0)) ** (i + 1))
                ins = nc.gpsimd.tensor_scalar(slope_mask[:, i, :], dist, slope, None, ALU.mult)
            ins.then_inc(c.s["aux"], 1)

            def attn(b, more):
                ln_rstd(c, pool, Span(s0, ATTN0, b)("ln"))
            loop(c, pool, B, attn)
            pool.wait_ge(c.s["vbank_full"], s1["vb"])

            def ffn(b, more):
                n = Span(s1, FFN0, b)
                pool.wait_ge(c.s["sbank_empty"], n("sb"))
                alone(c, pool)
                for i in range(2):
                    for k in range(KD):
                        ins = nc.gpsimd.tensor_scalar(carry[:, i, k, :], c.hT[:, k, 0:T], omu[:, i, k:k + 1], None,
                                                      ALU.mult)
                ins.then_inc(c.s["carry_ready"], 1)
                if more:
                    ln_rstd(c, pool, n("ln"))
                pool.wait_ge(c.s["sbank_empty"], n("sb", 4))
                for k in range(KD):
                    ins = nc.gpsimd.tensor_tensor(kact[:, k, :], krelu[:, k, :], krelu[:, k, :], ALU.mult)
                ins.then_inc(c.s["squared_ready"], 1)
            loop(c, pool, B, ffn)

        @block.vector
        def _(dve):
            ln_stats(c, dve, start["ln"], c.x[:, 0])
            ln_norm(c, dve, start["ln"], c.x[:, 0], start["sb"])
            dve.wait_ge(c.s["load"], loaded0)
            chain(c, dve, c.s["v_chain"], nc.vector.tensor_scalar(omu[:, :, :], mu[:, :, :], -1.0, 1.0, ALU.mult,
                                                                  ALU.add))
            dve.wait_ge(c.s["aux"], 4)

            def attn(b, more):
                n = Span(s0, ATTN0, b)
                for g in range(G0):
                    dve.wait_ge(c.s["vbank_full"], n("vb", g + 1))
                    nc.vector.tensor_copy(kT[:, g, :], c.vbank[g % 2][:, :]).then_inc(c.s["vbank_empty"], 1)
                for i in range(2):
                    dve.wait_ge(c.s["vbank_full"], n("vb", 5 + i))
                    nc.vector.tensor_copy(vt[:, 2 * i:2 * i + 2, :, 0:HD0],
                                          c.vbank[i][:, :].rearrange("p (t h e) -> p t h e", t=2, e=HD0))\
                      .then_inc(c.s["vbank_empty"], 1)

                def mid(t):
                    nxt = c.x[:, b + 1] if more else c.x[:, 0]
                    if t == 16:
                        ln_stats(c, dve, n("ln"), nxt)
                    if t == 20:
                        ln_norm(c, dve, n("ln"), nxt, n("sb"))
                heads_dve(c, dve, n, h, mid)
                for i in range(2):
                    dve.wait_ge(c.s["vbank_full"], n("vb", 71 + i))
                    gate = one_row(gates[:, 0], b)
                    chain(c, dve, c.s["v_chain"],
                          nc.vector.tensor_tensor(tmp[:, :, :], c.vbank[i][:, :].rearrange("p (t n) -> p t n", t=2),
                                                  gate, ALU.mult))
                    xs = c.x[:, b, 2 * i:2 * i + 2, :]
                    nc.vector.tensor_tensor(xs, xs, tmp[:, :, :], ALU.add).then_inc(c.s["vbank_empty"], 1)
                    dve.wait_ge(c.s["vbank_empty"], n("vb", 71 + i))
            loop(c, dve, B, attn)

            def ffn(b, more):
                n = Span(s1, FFN0, b)
                dve.wait_ge(c.s["carry_ready"], n("mx", 1))
                for i in range(2):
                    for k in range(KD):
                        ins = nc.vector.scalar_tensor_tensor(out=mixT[:, i, k, :], in0=c.hT[:, k, 1:T + 1],
                                                             scalar=mu[:, i, k:k + 1], in1=carry[:, i, k, :],
                                                             op0=ALU.mult, op1=ALU.add)
                ins.then_inc(c.s["mixed_ready"], 1)
                if more:
                    ln_stats(c, dve, n("ln"), c.x[:, b + 1])
                    ln_norm(c, dve, n("ln"), c.x[:, b + 1], n("sb"))
                for i in range(2):
                    dve.wait_ge(c.s["vbank_full"], n("vb", 1 + i))
                    chain(c, dve, c.s["v_chain"],
                          nc.vector.tensor_tensor(tmp[:, :, :], c.vbank[i][:, :].rearrange("p (t n) -> p t n", t=2),
                                                  rsig[:, 2 * i:2 * i + 2, :], ALU.mult))
                    chain(c, dve, c.s["v_chain"], nc.vector.tensor_tensor(tmp[:, :, :], tmp[:, :, :],
                                                                          one_row(gates[:, 1], b), ALU.mult))
                    xs = c.x[:, b, 2 * i:2 * i + 2, :]
                    nc.vector.tensor_tensor(xs, xs, tmp[:, :, :], ALU.add).then_inc(c.s["vbank_empty"], 1)
                    dve.wait_ge(c.s["vbank_empty"], n("vb", 1 + i))
            loop(c, dve, B, ffn)

        @block.scalar
        def _(act):
            ln_gain(c, act, start["sb"], mod(1, 0), mod(0, 0))

            def attn(b, more):
                n = Span(s0, ATTN0, b)
                for g in range(G0):
                    act.wait_ge(c.s["sbank_full"], n("sb", g + 1))
                    nc.scalar.mul(qT[:, g, :], c.sbank[g % 2][:, :], -float(HD0) ** -0.5)\
                      .then_inc(c.s["sbank_empty"], 1)

                def out(g):
                    act.wait_ge(c.s["obank_full"], n("av", 4 * g + 4))
                    nc.scalar.copy(aoT[:, g, :], c.obank[g % 2][:, :]).then_inc(c.s["obank_empty"], 1)

                def mid(k):
                    if k in (24, 40, 56):
                        out((k - 24) // 16)
                    if k == 44:
                        if more:
                            ln_gain(c, act, n("sb", 4), mod(1, b + 1), mod(0, b + 1))
                        else:
                            ln_gain(c, act, n("sb", 4), mod(3, 0), mod(2, 0))
                heads_act(c, act, n, h, mid)
                out(G0 - 1)
            loop(c, act, B, attn)

            def ffn(b, more):
                n = Span(s1, FFN0, b)
                for i in range(2):
                    act.wait_ge(c.s["sbank_full"], n("sb", 1 + i))
                    nc.scalar.activation(rsig[:, 2 * i:2 * i + 2, :],
                                         c.sbank[i][:, :].rearrange("p (t n) -> p t n", t=2),
                                         ACT.Sigmoid).then_inc(c.s["sbank_empty"], 1)
                for i in range(KD):
                    act.wait_ge(c.s["sbank_full"], n("sb", 3 + i))
                    nc.scalar.activation(krelu[:, i, :], c.sbank[i][:, :], ACT.Relu).then_inc(c.s["sbank_empty"], 1)
                if more:
                    ln_gain(c, act, n("sb", 4), mod(3, b + 1), mod(2, b + 1))
            loop(c, act, B, ffn)

        @block.tensor
        def _(pe):
            ln_turn(c, pe, start["ln"], start["sb"])
            pe.wait_ge(c.s["load"], loaded0)

            def attn(b, more):
                n = Span(s0, ATTN0, b)
                pe.wait_ge(c.s["sbank_empty"], n("sb"))
                for g in range(G0):
                    for i, (bank, full, empty, job) in enumerate(
                            ((c.sbank, "sbank_full", "sbank_empty", "sb"), (c.vbank, "vbank_full", "vbank_empty", "vb"))):
                        pe.wait_ge(c.s[empty], n(job, g - 1))
                        for k in range(KD):
                            ins = nc.tensor.matmul(bank[g % 2][:, :],
                                                   wqk[:, i, k, 4 * g:4 * g + 4, :].rearrange("p h e -> p (h e)"),
                                                   c.hT[:, k, 1:T + 1], start=(k == 0), stop=(k == KD - 1))
                        ins.then_inc(c.s[full], 1)
                for i in range(2):
                    pe.wait_ge(c.s["vbank_empty"], n("vb", 3 + i))
                    for t in range(2 * i, 2 * i + 2):
                        for k in range(KD):
                            ins = nc.tensor.matmul(c.vbank[i][:, (t % 2) * D:(t % 2 + 1) * D],
                                                   c.hT[:, k, 1 + t * P:1 + (t + 1) * P], wv[:, k, :],
                                                   start=(k == 0), stop=(k == KD - 1))
                    ins.then_inc(c.s["vbank_full"], 1)
                pe.wait_ge(c.s["sbank_empty"], n("sb", 4))
                pe.wait_ge(c.s["vbank_empty"], n("vb", 6))

                def mid(t):
                    if t == 32:
                        ln_turn(c, pe, n("ln"), n("sb", 4))
                heads_pe(c, pe, n, h, mid)
                pe.wait_ge(c.s["obank_empty"], n("ob", G0))
                for i in range(2):
                    pe.wait_ge(c.s["vbank_empty"], n("vb", 69 + i))
                    for t in range(2 * i, 2 * i + 2):
                        for g in range(G0):
                            ins = nc.tensor.matmul(c.vbank[i][:, (t % 2) * D:(t % 2 + 1) * D],
                                                   aoT[:, g, t * P:(t + 1) * P], wo[:, g, :],
                                                   start=(g == 0), stop=(g == G0 - 1))
                    ins.then_inc(c.s["vbank_full"], 1)
            loop(c, pe, B, attn)

            def ffn(b, more):
                n = Span(s1, FFN0, b)
                pe.wait_ge(c.s["mixed_ready"], n("mx", 1))
                for i in range(2):
                    pe.wait_ge(c.s["sbank_empty"], n("sb", i - 1))
                    for t in range(2 * i, 2 * i + 2):
                        for k in range(KD):
                            ins = nc.tensor.matmul(c.sbank[i][:, (t % 2) * D:(t % 2 + 1) * D],
                                                   mixT[:, 0, k, t * P:(t + 1) * P], wf[:, 0, k, :],
                                                   start=(k == 0), stop=(k == KD - 1))
                    ins.then_inc(c.s["sbank_full"], 1)
                for i in range(KD):
                    pe.wait_ge(c.s["sbank_empty"], n("sb", 1 + i))
                    for k in range(KD):
                        ins = nc.tensor.matmul(c.sbank[i][:, :], wf[:, 1, k, i * P:(i + 1) * P], mixT[:, 1, k, :],
                                               start=(k == 0), stop=(k == KD - 1))
                    ins.then_inc(c.s["sbank_full"], 1)
                if more:
                    ln_turn(c, pe, n("ln"), n("sb", 4))
                pe.wait_ge(c.s["squared_ready"], n("mx", 1))
                for i in range(2):
                    pe.wait_ge(c.s["vbank_empty"], n("vb", i - 1))
                    for t in range(2 * i, 2 * i + 2):
                        for k in range(KD):
                            ins = nc.tensor.matmul(c.vbank[i][:, (t % 2) * D:(t % 2 + 1) * D],
                                                   kact[:, k, t * P:(t + 1) * P], wf[:, 2, k, :],
                                                   start=(k == 0), stop=(k == KD - 1))
                    ins.then_inc(c.s["vbank_full"], 1)
            loop(c, pe, B, ffn)
    c.loaded = loaded0
    return end


def one_row(rows, b):
    r = rows[:, b:b + 1, :] if isinstance(b, int) else rows[:, bass.ds(b, 1), :]
    return r.to_broadcast([P, 2, D])


def row_of(rows, b):
    return rows[:, b:b + 1, :] if isinstance(b, int) else rows[:, bass.ds(b, 1), :]



REMIX = {"ln": 1, "rx": 1}


def remix(c, d, start, gate, scale, shift):
    nc = c.nc
    end = after(start, REMIX, B)
    names = [gate, scale, shift] if gate else [scale, shift]
    with ExitStack() as st:
        rows = st.enter_context(nc.sbuf_tensor(f"rows_{scale}", [P, 3, B, D], F32))
        block = st.enter_context(nc.Block())
        loaded = c.loaded + 16 * len(names)

        @block.sync
        def _(sp):
            for i, name in enumerate(names):
                sp.dma_start(rows[:, i + (not gate), :, :], mod_rows(c, 1, name)).then_inc(c.s["load"], 16)

        @block.gpsimd
        def _(pool):
            pool.wait_ge(c.s["load"], loaded)

            def turn(b, more):
                n = Span(start, REMIX, b)
                if gate:
                    yb = c.y[:, b]
                    nc.gpsimd.tensor_tensor(yb, yb, row_of(rows[:, 0], b).to_broadcast([P, NT, D]), ALU.mult)\
                      .then_inc(c.s["gated"], 1)
                ln_rstd(c, pool, n("ln"))
                pool.wait_ge(c.s["normed_ready"], n("ln", 1))
                yb = c.y[:, b]
                nc.gpsimd.tensor_tensor(yb, yb, row_of(rows[:, 1], b).to_broadcast([P, NT, D]), ALU.mult)\
                  .then_inc(c.s["scaled"], 1)
            with pool.Fori(0, B) as b:
                turn(b, True)

        @block.vector
        def _(dve):
            dve.wait_ge(c.s["load"], loaded)
            with dve.Fori(0, B) as b:
                n = Span(start, REMIX, b)
                if gate:
                    dve.wait_ge(c.s["gated"], n("rx", 1 - start.get("rx", 0)))
                    chain(c, dve, c.s["v_chain"], nc.vector.tensor_tensor(c.x[:, b], c.x[:, b], c.y[:, b], ALU.add))
                ln_stats(c, dve, n("ln"), c.x[:, b])
                ln_norm(c, dve, n("ln"), c.x[:, b], 0, dst=c.y[:, b])
                dve.wait_ge(c.s["scaled"], n("rx", 1))
                nc.vector.tensor_tensor(c.y[:, b], c.y[:, b], row_of(rows[:, 2], b).to_broadcast([P, NT, D]), ALU.add)
    c.loaded = loaded
    return end



ATTN1 = {"vb": 26, "sb": 6, "pb": 16, "av": 4, "ob": 2, "ln": 1, "at": 1}
MLP1 = {"vb": 2, "sb": 10, "ln": 1, "ml": 1}
VL = 2 * P
LIN = VL + P
CTX = HD1 + 1
CTXW = P + 4


def plus(a, b):
    return {k: a.get(k, 0) + b.get(k, 0) for k in {*a, *b}}


def layer1(c, d, start):
    nc = c.nc
    one_depth = plus(after(plus({}, {}), ATTN1, B), after({}, MLP1, B))
    end = after(start, one_depth, DEPTH)
    with ExitStack() as st:
        def sb(name, shape, dt=F32):
            return st.enter_context(nc.sbuf_tensor(name, shape, dt))

        wq = sb("wq1", [P, KD, D])
        wk = sb("wk1", [P, KD, D])
        wv = sb("wv1", [P, KD, D])
        wtok = sb("wtok", [P, KD, 2 * P + D])
        wo = sb("wo1", [P, KD, D])
        w1 = sb("w1", [P, KD, FF])
        w2 = sb("w2", [P, MF, D])
        bo = sb("bo", [P, 1, D])
        b2 = sb("b2", [P, 1, D])
        vec = sb("vec", [P, DEPTH, 8 + MF])
        qT = sb("qT1", [P, T])
        kT = sb("kT1", [P, T])
        tok = sb("tok", [P, NT, LIN + P + 4])
        kneg = sb("kneg", [P, NT, P])
        qmax = sb("qmax", [P, NT, 4])
        qinv = sb("qinv", [P, NT, 4])
        qlT = sb("qlT", [P, T])
        ctx = sb("ctx", [P, NU - 1, CTX])
        kcum = sb("kcum", [P, NU - 1])
        bd = sb("bd", [P, NU - 1, P])
        mask = sb("mask", [P, 2 * P])
        aoT = sb("aoT1", [P, KD, T])
        gT = c.prob
        block = st.enter_context(nc.Block())

        def depth_start(e):
            return {k: start.get(k, 0) + e * one_depth.get(k, 0) for k in {*start, *one_depth}}

        def spans(e):
            s0 = depth_start(e)
            s0 = {**s0, "sb": s0["sb"] + KD, "ln": s0["ln"] + 1}
            s1 = {k: s0.get(k, 0) + B * ATTN1.get(k, 0) for k in {*s0, *ATTN1}}
            return s0, s1

        def vec_at(e, i):
            return one(c_vec(e), i)

        def c_vec(e):
            return vec[:, e, :]

        h = Heads(
            quads=4,
            q_of=lambda q, j: qT[32 * j:32 * j + 32, q * P:(q + 1) * P],
            k_of=lambda q, j, lo, hi: kT[32 * j:32 * j + 32, lo * P:hi * P],
            keys_of=lambda q: [q - 1, q] if q else [q],
            mask_of=lambda q, j: mask[:, 0:2 * P] if q else mask[:, P:2 * P],
            v_of=lambda q, j, key: tok[:, key, VL + 32 * j:VL + 32 * j + 32],
            out_of=lambda q: (c.obank[0], slice(q * P, (q + 1) * P)),
            vb=4)
        all_wa, all_wm = 5 * 16, 3 * 16

        @block.sync
        def _(sp):
            sp.dma_start(vec[:, :, :], d["vec"]).then_inc(c.s["load"], 16)
            with sp.Fori(0, DEPTH) as e:
                s0, s1 = spans(e)
                sp.wait_ge(c.s["vbank_empty"], s0["vb"])
                sp.dma_start(wtok[:, :, :], d["wtok"][e].rearrange("(k p) n -> p k n", p=P))\
                  .then_inc(c.s["attn_weights"], 16)
                for w, name in ((wq, "Aq"), (wk, "Ak")):
                    sp.dma_start(w[:, :, 0:P], d[name][e].rearrange("(k p) n -> p k n", p=P)[:, :, 0:P])\
                      .then_inc(c.s["attn_weights"], 16)
                sp.dma_start(wo[:, :, :], d["Ao"][e].rearrange("(k p) n -> p k n", p=P))\
                  .then_inc(c.s["attn_weights"], 16)
                sp.dma_start(bo[:, :, :], d["bo"][e:e + 1, :].partition_broadcast(P)
                             if isinstance(e, int) else d["bo"][bass.ds(e, 1), :].partition_broadcast(P))\
                  .then_inc(c.s["attn_weights"], 16)
                sp.dma_start(w1[:, :, :], d["W1"][e].rearrange("(k p) n -> p k n", p=P))\
                  .then_inc(c.s["mlp_weights"], 16)
                sp.dma_start(w2[:, :, :], d["W2"][e].rearrange("(k p) n -> p k n", p=P))\
                  .then_inc(c.s["mlp_weights"], 16)
                sp.dma_start(b2[:, :, :], d["b2"][bass.ds(e, 1), :].partition_broadcast(P))\
                  .then_inc(c.s["mlp_weights"], 16)

        @block.gpsimd
        def _(pool):
            nc.gpsimd.memset(bd[:, :, :], 0.0)
            nc.gpsimd.memset(aoT[:, 1, 0:BUCKET], 0.0)
            nc.gpsimd.memset(tok[:, :, LIN + P:LIN + P + 1], 1.0)
            chain(c, pool, c.s["p_chain"], nc.gpsimd.memset(mask[:, :], 0.0))
            cur = mask[:, P:2 * P]
            nc.gpsimd.affine_select(out=cur, in_=cur, compare_op=ALU.is_ge, fill=BIG, base=0, pattern=[[-1, P]],
                                    channel_multiplier=1).then_inc(c.s["aux"], 1)
            with pool.Fori(0, DEPTH) as e:
                s0, s1 = spans(e)
                ln_rstd(c, pool, depth_start(e)["ln"])
                pool.wait_ge(c.s["attn_weights"], (e + 1) * all_wa)
                alone(c, pool)

                def attn(b, more):
                    n = Span(s0, ATTN1, b)
                    pool.wait_ge(c.s["normed_ready"], n("ln"))
                    yb = c.y[:, b]
                    nc.gpsimd.tensor_tensor(yb, yb, bo[:, :, :].to_broadcast([P, NT, D]), ALU.add)\
                      .then_inc(c.s["biased"], 1)
                    pool.wait_ge(c.s["lin_inverted"], n("at", 1))
                    ql = tok[:, :, 0:P].rearrange("p t (h e) -> p t h e", e=HD1)
                    nc.gpsimd.tensor_tensor(ql, ql, qinv[:, :, :].unsqueeze(3).to_broadcast([P, NT, 4, HD1]),
                                            ALU.mult).then_inc(c.s["lin_q_ready"], 1)
                    ln_rstd(c, pool, n("ln"))
                with pool.Fori(0, B) as b:
                    attn(b, True)
                pool.wait_ge(c.s["mlp_weights"], (e + 1) * all_wm)

                def mlp(b, more):
                    n = Span(s1, MLP1, b)
                    pool.wait_ge(c.s["normed_ready"], n("ln"))
                    yb = c.y[:, b]
                    nc.gpsimd.tensor_tensor(yb, yb, b2[:, :, :].to_broadcast([P, NT, D]), ALU.add)\
                      .then_inc(c.s["biased"], 1)
                    if more:
                        ln_rstd(c, pool, n("ln"))
                loop(c, pool, B, mlp)

        @block.vector
        def _(dve):
            dve.wait_ge(c.s["aux"], 5)
            with dve.Fori(0, DEPTH) as e:
                s0, s1 = spans(e)
                n0 = depth_start(e)
                ln_stats(c, dve, n0["ln"], c.y[:, 0])
                ln_norm(c, dve, n0["ln"], c.y[:, 0], n0["sb"])

                def attn(b, more):
                    n = Span(s0, ATTN1, b)
                    for t in range(NT):
                        dve.wait_ge(c.s["vbank_full"], n("vb", t + 1))
                        nc.vector.tensor_copy(tok[:, t, 0:LIN + P], c.vbank[t % 2][:, :])\
                          .then_inc(c.s["vbank_empty"], 1)
                    dve.wait_ge(c.s["vbank_empty"], n("vb", NT))
                    ql = tok[:, :, 0:P].rearrange("p t (h e) -> p t h e", e=HD1)
                    kl = tok[:, :, P:2 * P]
                    nc.vector.tensor_scalar(kneg[:, :, :], kl, 0.0, None, ALU.min)
                    chain(c, dve, c.s["v_chain"],
                          nc.vector.tensor_reduce(qmax[:, :, :], ql, AX.X, ALU.max))
                    nc.vector.tensor_tensor(ql, ql, qmax[:, :, :].unsqueeze(3).to_broadcast([P, NT, 4, HD1]),
                                            ALU.subtract).then_inc(c.s["lin_shifted"], 1)

                    def context(i):
                        dve.wait_ge(c.s["vbank_full"], n("vb", 21 + i))
                        us = min(2, NU - 1 - 2 * i)
                        src = c.vbank[i % 2][:, 0:us * CTXW].rearrange("p (u n) -> p u n", u=us)
                        for j in range(4):
                            nc.vector.tensor_copy(ctx[32 * j:32 * j + 32, 2 * i:2 * i + us, 0:HD1],
                                                  src[32 * j:32 * j + 32, :, 32 * j:32 * j + 32])
                        nc.vector.tensor_copy(ctx[:, 2 * i:2 * i + us, HD1:CTX], src[:, :, P:P + 1])\
                          .then_inc(c.s["vbank_empty"], 1)

                    def mid(t):
                        if t == 2:
                            dve.wait_ge(c.s["lin_exped"], n("at", 0) * 2 + 1)
                            chain(c, dve, c.s["v_chain"],
                                  nc.vector.tensor_reduce(qmax[:, :, :], ql, AX.X, ALU.add))
                            nc.vector.reciprocal(qinv[:, :, :], qmax[:, :, :]).then_inc(c.s["lin_inverted"], 1)
                        if t == 4:
                            dve.wait_ge(c.s["lin_exped"], n("at", 0) * 2 + 2)
                            nc.vector.scalar_tensor_tensor(out=kl, in0=kl, scalar=0.0, in1=kneg[:, :, :],
                                                           op0=ALU.max, op1=ALU.add).then_inc(c.s["lin_k_ready"], 1)
                        if t == 9:
                            ln_stats(c, dve, n("ln"), c.y[:, b + 1] if more else c.y[:, 0])
                        if t == 12:
                            ln_norm(c, dve, n("ln"), c.y[:, b + 1] if more else c.y[:, 0], n("sb", 0))
                        if t >= 20 and t % 2 == 0 and t < 28:
                            context((t - 20) // 2)
                    heads_dve(c, dve, n, h, mid)
                    dve.wait_ge(c.s["vbank_empty"], n("vb", 24))
                    for u in range(2, NU - 1, 2):
                        to = slice(u, min(u + 2, NU - 1))
                        before = ctx[:, u - 1:u, :].to_broadcast([P, to.stop - to.start, CTX])
                        chain(c, dve, c.s["v_chain"], nc.vector.tensor_tensor(ctx[:, to, :], ctx[:, to, :], before,
                                                                              ALU.add))
                    chain(c, dve, c.s["v_chain"], nc.vector.tensor_scalar(kcum[:, :], ctx[:, :, HD1], 1e-6, None,
                                                                          ALU.add))
                    chain(c, dve, c.s["v_chain"], nc.vector.reciprocal(kcum[:, :], kcum[:, :]))
                    for j in range(4):
                        q = slice(32 * j, 32 * j + 32)
                        ins = nc.vector.tensor_tensor(bd[q, :, q], ctx[q, :, 0:HD1],
                                                      kcum[q, :].unsqueeze(2).to_broadcast([32, NU - 1, HD1]),
                                                      ALU.mult)
                    ins.then_inc(c.s["context_ready"], 1)
                    dve.wait_ge(c.s["biased"], 2 * e * B + b + 1)
                    for i in range(2):
                        dve.wait_ge(c.s["vbank_full"], n("vb", 25 + i))
                        ys = c.y[:, b, 2 * i:2 * i + 2, :]
                        nc.vector.tensor_tensor(ys, ys, c.vbank[i][:, :].rearrange("p (t n) -> p t n", t=2), ALU.add)\
                          .then_inc(c.s["vbank_empty"], 1)
                    dve.wait_ge(c.s["vbank_empty"], n("vb", 26))
                loop(c, dve, B, attn)

                def mlp(b, more):
                    n = Span(s1, MLP1, b)
                    if more:
                        ln_stats(c, dve, n("ln"), c.y[:, b + 1])
                        ln_norm(c, dve, n("ln"), c.y[:, b + 1], n("sb"))
                    dve.wait_ge(c.s["biased"], (2 * e + 1) * B + b + 1)
                    for i in range(2):
                        dve.wait_ge(c.s["vbank_full"], n("vb", 1 + i))
                        ys = c.y[:, b, 2 * i:2 * i + 2, :]
                        nc.vector.tensor_tensor(ys, ys, c.vbank[i][:, :].rearrange("p (t n) -> p t n", t=2), ALU.add)\
                          .then_inc(c.s["vbank_empty"], 1)
                    dve.wait_ge(c.s["vbank_empty"], n("vb", 2))
                loop(c, dve, B, mlp)

        @block.scalar
        def _(act):
            act.wait_ge(c.s["load"], c.loaded + 16)
            with act.Fori(0, DEPTH) as e:
                s0, s1 = spans(e)
                v = c_vec(e)
                ln_gain(c, act, depth_start(e)["sb"], lambda k: v[:, k:k + 1], lambda k: v[:, 2 + k:3 + k])

                def attn(b, more):
                    n = Span(s0, ATTN1, b)
                    act.wait_ge(c.s["sbank_full"], n("sb", 1))
                    nc.scalar.mul(qT[:, :], c.sbank[0][:, :], -float(HD1) ** -0.5).then_inc(c.s["sbank_empty"], 1)
                    act.wait_ge(c.s["sbank_full"], n("sb", 2))
                    nc.scalar.copy(kT[:, :], c.sbank[1][:, :]).then_inc(c.s["sbank_empty"], 1)
                    act.wait_ge(c.s["lin_shifted"], n("at", 1))
                    nc.scalar.activation(tok[:, :, 0:P], tok[:, :, 0:P], ACT.Exp).then_inc(c.s["lin_exped"], 1)
                    nc.scalar.activation(kneg[:, :, :], kneg[:, :, :], ACT.Exp).then_inc(c.s["lin_exped"], 1)

                    def mid(k):
                        if k == 10:
                            for i in range(2):
                                act.wait_ge(c.s["sbank_full"], n("sb", 3 + i))
                                nc.scalar.copy(qlT[:, 2 * i * P:2 * (i + 1) * P], c.sbank[i][:, 0:2 * P])\
                                  .then_inc(c.s["sbank_empty"], 1)
                    heads_act(c, act, n, h, mid)
                    w = (lambda k: v[:, k:k + 1], lambda k: v[:, 2 + k:3 + k]) if more else \
                        (lambda k: v[:, 4 + k:5 + k], lambda k: v[:, 6 + k:7 + k])
                    ln_gain(c, act, n("sb", 4), *w)
                    act.wait_ge(c.s["obank_full"], n("av", 4))
                    nc.scalar.copy(aoT[:, 0, :], c.obank[0][:, :]).then_inc(c.s["obank_empty"], 1)
                    act.wait_ge(c.s["lin_full"], n("at", 1))
                    nc.scalar.copy(aoT[:, 1, BUCKET:T], c.obank[1][:, BUCKET:T]).then_inc(c.s["obank_empty"], 1)
                loop(c, act, B, attn)

                def mlp(b, more):
                    n = Span(s1, MLP1, b)
                    for m in range(MF):
                        act.wait_ge(c.s["sbank_full"], n("sb", m + 1))
                        alone(c, act)
                        nc.scalar.activation(gT[:, m, :], c.sbank[m % 2][:, :], ACT.Gelu, bias=v[:, 8 + m:9 + m])\
                          .then_inc(c.s["sbank_empty"], 1)
                    if more:
                        ln_gain(c, act, n("sb", 8), lambda k: v[:, 4 + k:5 + k], lambda k: v[:, 6 + k:7 + k])
                loop(c, act, B, mlp)

        @block.tensor
        def _(pe):
            with pe.Fori(0, DEPTH) as e:
                s0, s1 = spans(e)
                n0 = depth_start(e)
                ln_turn(c, pe, n0["ln"], n0["sb"])
                pe.wait_ge(c.s["attn_weights"], (e + 1) * all_wa)

                def attn(b, more):
                    n = Span(s0, ATTN1, b)
                    pe.wait_ge(c.s["sbank_empty"], n("sb"))
                    for t in range(NT):
                        pe.wait_ge(c.s["vbank_empty"], n("vb", t - 1))
                        for k in range(KD):
                            ins = nc.tensor.matmul(c.vbank[t % 2][:, :], c.hT[:, k, 1 + t * P:1 + (t + 1) * P],
                                                   wtok[:, k, :], start=(k == 0), stop=(k == KD - 1))
                        ins.then_inc(c.s["vbank_full"], 1)
                    for i, w in enumerate((wq, wk)):
                        pe.wait_ge(c.s["sbank_empty"], n("sb", i - 1))
                        for k in range(KD):
                            ins = nc.tensor.matmul(c.sbank[i][:, :], w[:, k, 0:P], c.hT[:, k, 1:T + 1],
                                                   start=(k == 0), stop=(k == KD - 1))
                        ins.then_inc(c.s["sbank_full"], 1)
                    pe.wait_ge(c.s["sbank_empty"], n("sb", 2))

                    def context(i):
                        pe.wait_ge(c.s["vbank_empty"], n("vb", 19 + i))
                        for u in range(2 * i, min(2 * i + 2, NU - 1)):
                            rows = slice(0, BUCKET if u % 2 == 0 else P)
                            at = (u % 2) * CTXW
                            ins = nc.tensor.matmul(c.vbank[i % 2][:, at:at + P + 1], tok[rows, u // 2, P:2 * P],
                                                   tok[rows, u // 2, LIN:LIN + P + 1], start=True, stop=True)
                        ins.then_inc(c.s["vbank_full"], 1)

                    def mid(t):
                        if t == 8:
                            pe.wait_ge(c.s["lin_q_ready"], n("at", 1))
                            for i in range(2):
                                pe.wait_ge(c.s["sbank_empty"], n("sb", 1 + i))
                                for r in range(2):
                                    ins = nc.tensor.transpose(c.sbank[i][:, r * P:(r + 1) * P],
                                                              tok[:, 2 * i + r, 0:P], c.ident[:, :])
                                ins.then_inc(c.s["sbank_full"], 1)
                        if t == 16:
                            pe.wait_ge(c.s["lin_k_ready"], n("at", 1))
                            context(0)
                            context(1)
                        if t == 22:
                            context(2)
                        if t == 24:
                            context(3)
                        if t == 18:
                            ln_turn(c, pe, n("ln"), n("sb", 4))
                    heads_pe(c, pe, n, h, mid)
                    pe.wait_ge(c.s["context_ready"], n("at", 1))
                    for u in range(NU - 1):
                        cols = slice(BUCKET * (u + 1), BUCKET * (u + 2))
                        ins = nc.tensor.matmul(c.obank[1][:, cols], bd[:, u, :], qlT[:, cols], start=True, stop=True)
                    ins.then_inc(c.s["lin_full"], 1)
                    pe.wait_ge(c.s["obank_empty"], n("ob", 2))
                    for i in range(2):
                        pe.wait_ge(c.s["vbank_empty"], n("vb", 23 + i))
                        for t in range(2 * i, 2 * i + 2):
                            for k in range(KD):
                                ins = nc.tensor.matmul(c.vbank[i][:, (t % 2) * D:(t % 2 + 1) * D],
                                                       aoT[:, k, t * P:(t + 1) * P], wo[:, k, :],
                                                       start=(k == 0), stop=(k == KD - 1))
                        ins.then_inc(c.s["vbank_full"], 1)
                loop(c, pe, B, attn)
                pe.wait_ge(c.s["mlp_weights"], (e + 1) * all_wm)

                def mlp(b, more):
                    n = Span(s1, MLP1, b)
                    pe.wait_ge(c.s["sbank_empty"], n("sb"))
                    for m in range(MF):
                        pe.wait_ge(c.s["sbank_empty"], n("sb", m - 1))
                        for k in range(KD):
                            ins = nc.tensor.matmul(c.sbank[m % 2][:, :], w1[:, k, m * P:(m + 1) * P],
                                                   c.hT[:, k, 1:T + 1], start=(k == 0), stop=(k == KD - 1))
                        ins.then_inc(c.s["sbank_full"], 1)
                    for i in range(2):
                        pe.wait_ge(c.s["vbank_empty"], n("vb", i - 1))
                        pe.wait_ge(c.s["sbank_empty"], n("sb", MF))
                        for t in range(2 * i, 2 * i + 2):
                            for m in range(MF):
                                ins = nc.tensor.matmul(c.vbank[i][:, (t % 2) * D:(t % 2 + 1) * D],
                                                       gT[:, m, t * P:(t + 1) * P], w2[:, m, :],
                                                       start=(m == 0), stop=(m == MF - 1))
                        ins.then_inc(c.s["vbank_full"], 1)
                        if i == 0 and more:
                            ln_turn(c, pe, n("ln"), n("sb", 8))
                loop(c, pe, B, mlp)
    c.loaded += 16
    return end



CROSS = {"vb": B + 4, "sb": 8, "ln": 2, "cr": 1, "pr": 16, "ab": 1}
GW = QKV // NKV
QH = NH // NKV


def cross(c, d, start):
    nc = c.nc
    end = after(start, CROSS, NT)
    with ExitStack() as st:
        def sb(name, shape, dt=F32):
            return st.enter_context(nc.sbuf_tensor(name, shape, dt))

        wqkv = sb("wqkv", [P, KD, QKV])
        wp = sb("wproj", [P, KD, D])
        g1 = sb("cross_gain", [P, 2 * KD])
        qkv = sb("qkv", [P, B, QKV])
        prod = sb("prod", [P, 2, NKV * B * QH * HDM])
        sc = sb("cross_scores", [P, NH, B, B])
        pr = sb("cross_probs", [P, NH, B, B])
        mx = sb("cross_max", [P, NH, B])
        ao = sb("cross_out", [P, B, D])
        aoT = sb("cross_outT", [P, KD, B, P])
        block = st.enter_context(nc.Block())
        loaded = c.loaded + 3 * 16

        def part(s, g, at, n):
            return qkv[:, s, g * GW + at:g * GW + at + n]

        @block.sync
        def _(sp):
            sp.dma_start(wqkv[:, :, :], d["wqkv"].rearrange("(k p) n -> p k n", p=P)).then_inc(c.s["load"], 16)
            sp.dma_start(wp[:, :, :], d["wproj"].rearrange("(k p) n -> p k n", p=P)).then_inc(c.s["load"], 16)
            sp.dma_start(g1[:, :], d["cross_ln"]).then_inc(c.s["load"], 16)

        @block.gpsimd
        def _(pool):
            nc.gpsimd.memset(sc[:, :, :, :], -BIG).then_inc(c.s["aux"], 1)
            with pool.Fori(0, NT) as p:
                n = Span(start, CROSS, p)
                ln_rstd(c, pool, n("ln"))
                ln_rstd(c, pool, n("ln", 1))
                pool.wait_ge(c.s["vbank_empty"], n("vb", B))
                for s in range(B):
                    pool.wait_ge(c.s["products_used"], n("pr", s + 1))
                    for g in range(NKV):
                        out = prod[:, s % 2, g * (s + 1) * QH * HDM:(g + 1) * (s + 1) * QH * HDM]\
                            .rearrange("p (t h e) -> p t h e", h=QH, e=HDM)
                        q = part(s, g, 0, QH * HDM).rearrange("p (h e) -> p h e", h=QH).unsqueeze(1)\
                            .to_broadcast([P, s + 1, QH, HDM])
                        k = part(slice(0, s + 1), g, QH * HDM, HDM).unsqueeze(2).to_broadcast([P, s + 1, QH, HDM])
                        ins = nc.gpsimd.tensor_tensor(out, q, k, ALU.mult)
                    ins.then_inc(c.s["products_ready"], 1)
                pool.wait_ge(c.s["cross_probs"], n("cr", 1))
                for s in range(B):
                    pool.wait_ge(c.s["products_used"], n("pr", B + s + 1))
                    for g in range(NKV):
                        out = prod[:, s % 2, g * (s + 1) * QH * HDM:(g + 1) * (s + 1) * QH * HDM]\
                            .rearrange("p (h e t) -> p h e t", h=QH, e=HDM)
                        a = pr[:, g * QH:(g + 1) * QH, s, 0:s + 1].unsqueeze(2).to_broadcast([P, QH, HDM, s + 1])
                        v = part(slice(0, s + 1), g, (QH + 1) * HDM, HDM).rearrange("p t e -> p e t").unsqueeze(1)\
                            .to_broadcast([P, QH, HDM, s + 1])
                        ins = nc.gpsimd.tensor_tensor(out, a, v, ALU.mult)
                    ins.then_inc(c.s["products_ready"], 1)

        @block.vector
        def _(dve):
            dve.wait_ge(c.s["aux"], 6)
            dve.sem_inc(c.s["products_used"], 2)
            with dve.Fori(0, NT) as p:
                n = Span(start, CROSS, p)
                for half in range(2):
                    src = c.y[:, 4 * half:4 * half + 4, p, :]
                    ln_stats(c, dve, n("ln", half), src)
                    ln_norm(c, dve, n("ln", half), src, n("sb", 2 * half))
                for s in range(B):
                    dve.wait_ge(c.s["vbank_full"], n("vb", s + 1))
                    nc.vector.tensor_copy(qkv[:, s, :], c.vbank[s % 2][:, 0:QKV]).then_inc(c.s["vbank_empty"], 1)
                for s in range(B):
                    dve.wait_ge(c.s["products_ready"], n("pr", s + 1))
                    src = prod[:, s % 2, 0:(s + 1) * D].rearrange("p (g t h e) -> p g t h e", g=NKV, h=QH, e=HDM)
                    to = sc[:, :, s, 0:s + 1].rearrange("p (g h) t -> p g t h", g=NKV)
                    if s == 0:
                        src, to = src[:, :, 0], to[:, :, 0]
                    nc.vector.tensor_reduce(to, src, AX.X, ALU.add).then_inc(c.s["products_used"], 1)
                dve.wait_ge(c.s["products_used"], n("pr", B + 2))
                chain(c, dve, c.s["v_chain"], nc.vector.tensor_reduce(mx[:, :, :], sc[:, :, :, :], AX.X, ALU.max))
                nc.vector.tensor_tensor(pr[:, :, :, :], sc[:, :, :, :], mx[:, :, :].unsqueeze(3)
                                        .to_broadcast([P, NH, B, B]), ALU.subtract).then_inc(c.s["cross_shifted"], 1)
                dve.wait_ge(c.s["cross_exped"], n("cr", 1))
                chain(c, dve, c.s["v_chain"], nc.vector.tensor_reduce(mx[:, :, :], pr[:, :, :, :], AX.X, ALU.add))
                chain(c, dve, c.s["v_chain"], nc.vector.reciprocal(mx[:, :, :], mx[:, :, :]))
                nc.vector.tensor_tensor(pr[:, :, :, :], pr[:, :, :, :], mx[:, :, :].unsqueeze(3)
                                        .to_broadcast([P, NH, B, B]), ALU.mult).then_inc(c.s["cross_probs"], 1)
                for s in range(B):
                    dve.wait_ge(c.s["products_ready"], n("pr", B + s + 1))
                    src = prod[:, s % 2, 0:(s + 1) * D].rearrange("p (n t) -> p n t", t=s + 1)
                    nc.vector.tensor_reduce(ao[:, s, :], src, AX.X, ALU.add).then_inc(c.s["products_used"], 1)
                for i in range(4):
                    dve.wait_ge(c.s["vbank_full"], n("vb", B + i + 1))
                    ys = c.y[:, 2 * i:2 * i + 2, p, :]
                    nc.vector.tensor_tensor(ys, ys, c.vbank[i % 2][:, :].rearrange("p (t n) -> p t n", t=2), ALU.add)\
                      .then_inc(c.s["vbank_empty"], 1)

        @block.scalar
        def _(act):
            act.wait_ge(c.s["load"], loaded)
            with act.Fori(0, NT) as p:
                n = Span(start, CROSS, p)
                for half in range(2):
                    if half:
                        act.wait_ge(c.s["vbank_full"], n("vb", 4))
                    ln_gain(c, act, n("sb", 2 * half), lambda k: g1[:, k:k + 1], lambda k: g1[:, 2 + k:3 + k])
                act.wait_ge(c.s["cross_shifted"], n("cr", 1))
                nc.scalar.activation(pr[:, :, :, :], pr[:, :, :, :], ACT.Exp, scale=float(HDM) ** -0.5)\
                  .then_inc(c.s["cross_exped"], 1)
                for i in range(4):
                    act.wait_ge(c.s["sbank_full"], n("sb", 5 + i))
                    nc.scalar.copy(aoT[:, i // 2, 4 * (i % 2):4 * (i % 2) + 4, :].rearrange("p s t -> p (s t)"),
                                   c.sbank[i % 2][:, :]).then_inc(c.s["sbank_empty"], 1)

        @block.tensor
        def _(pe):
            pe.wait_ge(c.s["load"], loaded)
            with pe.Fori(0, NT) as p:
                n = Span(start, CROSS, p)
                for half in range(2):
                    ln_turn(c, pe, n("ln", half), n("sb", 2 * half))
                    pe.wait_ge(c.s["sbank_empty"], n("sb", 2 * half + 2))
                    for t in range(4):
                        pe.wait_ge(c.s["vbank_empty"], n("vb", 4 * half + t - 1))
                        for k in range(KD):
                            ins = nc.tensor.matmul(c.vbank[t % 2][:, 0:QKV], c.hT[:, k, 1 + t * P:1 + (t + 1) * P],
                                                   wqkv[:, k, :], start=(k == 0), stop=(k == KD - 1))
                        ins.then_inc(c.s["vbank_full"], 1)
                pe.wait_ge(c.s["products_used"], n("pr", 2 * B + 2))
                for i in range(4):
                    pe.wait_ge(c.s["sbank_empty"], n("sb", 3 + i))
                    for r in range(4):
                        s = 4 * (i % 2) + r
                        ins = nc.tensor.transpose(c.sbank[i % 2][:, r * P:(r + 1) * P],
                                                  ao[:, s, (i // 2) * P:(i // 2 + 1) * P], c.ident[:, :])
                    ins.then_inc(c.s["sbank_full"], 1)
                pe.wait_ge(c.s["sbank_empty"], n("sb", 8))
                for i in range(4):
                    pe.wait_ge(c.s["vbank_empty"], n("vb", B + i - 1))
                    for r in range(2):
                        for k in range(KD):
                            ins = nc.tensor.matmul(c.vbank[i % 2][:, r * D:(r + 1) * D], aoT[:, k, 2 * i + r, :],
                                                   wp[:, k, :], start=(k == 0), stop=(k == KD - 1))
                    ins.then_inc(c.s["vbank_full"], 1)
    c.loaded = loaded
    return end



MOE = {"vb": 2 + 2 * E, "sb": 4 * E + 2, "ln": 1, "mo": 1}
KF = FM // P


def moe(c, d, start, out):
    nc = c.nc
    start = dict(start)
    with ExitStack() as st:
        def sb(name, shape, dt=F32):
            return st.enter_context(nc.sbuf_tensor(name, shape, dt))

        w1 = sb("we1", [P, E, KD, FM])
        w2 = sb("we2", [P, E, KF, D])
        wr = sb("wrouter", [P, KD, E])
        gains = sb("moe_gain", [P, 2 * KD])
        gate = sb("gate1", [P, B, D])
        tri = sb("tri", [P, P])
        ones = sb("ones_moe", [P, P])
        expert = sb("expert", [P, 1, E])
        lg = sb("logits", [P, NT, E])
        top = sb("top", [P, NT, 8])
        index = sb("index", [P, NT, 8], U32)
        indexf = sb("indexf", [P, NT, 2])
        total = sb("total", [P, NT])
        hot = sb("hot", [P, 2, NT, E])
        chosen = sb("chosen", [P, NT, E])
        rank = sb("rank", [P, NT, E])
        base = sb("base", [P, NT + 1, E])
        w = sb("weight", [P, NT, E])
        tmp = c.probT[:, 0:2, :].rearrange("p i (t n) -> p (i t) n", t=2)
        gT = c.prob
        s0 = after(start, {"sb": KD, "ln": 1}, 1)
        block = st.enter_context(nc.Block())
        loaded = c.loaded + 5 * 16

        @block.sync
        def _(sp):
            sp.dma_start(wr[:, :, :], d["wrouter"].rearrange("(k p) n -> p k n", p=P)).then_inc(c.s["load"], 16)
            sp.dma_start(gains[:, :], d["moe_ln"]).then_inc(c.s["load"], 16)
            sp.dma_start(w1[:, :, :, :], d["we1"].rearrange("e (k p) n -> p e k n", p=P)).then_inc(c.s["load"], 16)
            sp.dma_start(w2[:, :, :, :], d["we2"].rearrange("e (k p) n -> p e k n", p=P)).then_inc(c.s["load"], 16)
            sp.dma_start(gate[:, :, :], mod_rows(c, 1, "gb")).then_inc(c.s["load"], 16)
            with sp.Fori(0, B) as b:
                sp.wait_ge(c.s["finished"], b + 1)
                sp.dma_start(out[b].rearrange("(t p) n -> p t n", p=P), c.x[:, b]).then_inc(c.s["stored"], 16)
            sp.wait_ge(c.s["stored"], 16 * B)

        @block.gpsimd
        def _(pool):
            ln_rstd(c, pool, start["ln"])
            chain(c, pool, c.s["p_chain"], nc.gpsimd.memset(ones[:, :], 1.0))
            nc.gpsimd.memset(base[:, 0:1, :], 0.0)
            nc.gpsimd.affine_select(out=tri[:, :], in_=ones[:, :], compare_op=ALU.is_gt, fill=0.0, base=0,
                                    pattern=[[1, P]], channel_multiplier=-1)
            nc.gpsimd.iota(expert[:, 0, :], pattern=[[1, E]], base=0, channel_multiplier=0,
                           allow_small_or_imprecise_dtypes=True).then_inc(c.s["aux"], 1)
            pool.wait_ge(c.s["load"], loaded)

            def turn(b, more):
                n = Span(s0, MOE, b)
                if more:
                    ln_rstd(c, pool, n("ln"))
                pool.wait_ge(c.s["vbank_empty"], n("vb", MOE["vb"]))
                nc.gpsimd.tensor_tensor(tmp, c.y[:, b], row_of(gate, b).to_broadcast([P, NT, D]), ALU.mult)\
                  .then_inc(c.s["gated"], 1)
            loop(c, pool, B, turn)

        @block.vector
        def _(dve):
            v = c.s["v_chain"]
            ln_stats(c, dve, start["ln"], c.y[:, 0])
            ln_norm(c, dve, start["ln"], c.y[:, 0], start["sb"])
            dve.wait_ge(c.s["aux"], 7)

            def over_experts(x):
                return x.unsqueeze(2).to_broadcast([P, NT, E])

            def turn(b, more):
                n = Span(s0, MOE, b)
                dve.wait_ge(c.s["vbank_full"], n("vb", 1))
                nc.vector.tensor_copy(lg[:, :, :], c.vbank[0][:, 0:NT * E].rearrange("p (t e) -> p t e", e=E))\
                  .then_inc(c.s["vbank_empty"], 1)
                dve.wait_ge(c.s["vbank_empty"], n("vb", 1))
                chain(c, dve, v, nc.vector.tensor_reduce(total[:, :], lg[:, :, :], AX.X, ALU.max))
                nc.vector.tensor_tensor(lg[:, :, :], lg[:, :, :], over_experts(total[:, :]), ALU.subtract)\
                  .then_inc(c.s["logits_shifted"], 1)
                dve.wait_ge(c.s["logits_exped"], n("mo", 1))
                chain(c, dve, v, nc.vector.tensor_reduce(total[:, :], lg[:, :, :], AX.X, ALU.add))
                chain(c, dve, v, nc.vector.reciprocal(total[:, :], total[:, :]))
                chain(c, dve, v, nc.vector.tensor_tensor(lg[:, :, :], lg[:, :, :], over_experts(total[:, :]),
                                                         ALU.mult))
                for t in range(NT):
                    ins = nc.vector.max(top[:, t, :], lg[:, t, :])
                chain(c, dve, v, ins)
                for t in range(NT):
                    ins = nc.vector.max_index(index[:, t, :], top[:, t, :], lg[:, t, :])
                chain(c, dve, v, ins)
                chain(c, dve, v, nc.vector.tensor_copy(indexf[:, :, :], index[:, :, 0:2]))
                for i in range(TOPK):
                    ins = nc.vector.tensor_tensor(hot[:, i, :, :], expert[:, :, :].to_broadcast([P, NT, E]),
                                                  over_experts(indexf[:, :, i]), ALU.is_equal)
                chain(c, dve, v, ins)
                nc.vector.tensor_tensor(chosen[:, :, :], hot[:, 0], hot[:, 1], ALU.add)\
                  .then_inc(c.s["chosen"], 1)
                chain(c, dve, v, nc.vector.tensor_tensor(total[:, :], top[:, :, 0], top[:, :, 1], ALU.add))
                chain(c, dve, v, nc.vector.reciprocal(total[:, :], total[:, :]))
                for i in range(TOPK):
                    ins = nc.vector.tensor_tensor(indexf[:, :, i], top[:, :, i], total[:, :], ALU.mult)
                chain(c, dve, v, ins)
                for i in range(TOPK):
                    ins = nc.vector.tensor_tensor(hot[:, i], hot[:, i], over_experts(indexf[:, :, i]), ALU.mult)
                chain(c, dve, v, ins)
                nc.vector.tensor_tensor(w[:, :, :], hot[:, 0], hot[:, 1], ALU.add)
                dve.wait_ge(c.s["vbank_full"], n("vb", 2))
                for t in range(NT):
                    at = NT * E + t * E
                    chain(c, dve, v, nc.vector.tensor_tensor(base[:, t + 1, :], base[:, t, :],
                                                             c.vbank[1][:, at:at + E], ALU.add))
                nc.vector.tensor_tensor(rank[:, :, :], base[:, 0:NT, :],
                                        c.vbank[1][:, 0:NT * E].rearrange("p (t e) -> p t e", e=E), ALU.add)\
                  .then_inc(c.s["vbank_empty"], 1)
                dve.wait_ge(c.s["vbank_empty"], n("vb", 2))
                chain(c, dve, v, nc.vector.tensor_copy(base[:, 0, :], base[:, NT, :]))
                chain(c, dve, v, nc.vector.scalar_tensor_tensor(out=w[:, :, :], in0=rank[:, :, :], scalar=float(CAP),
                                                                in1=w[:, :, :], op0=ALU.is_lt, op1=ALU.mult))
                if more:
                    ln_stats(c, dve, n("ln"), c.y[:, b + 1])
                    ln_norm(c, dve, n("ln"), c.y[:, b + 1], n("sb"))
                for e in range(E):
                    for i in range(2):
                        dve.wait_ge(c.s["vbank_full"], n("vb", 2 * e + i + 3))
                        for t in range(2):
                            y = c.y[:, b, 2 * i + t, :]
                            ins = nc.vector.scalar_tensor_tensor(out=y, in0=c.vbank[i][:, t * D:(t + 1) * D],
                                                                 scalar=w[:, 2 * i + t, e:e + 1], in1=y,
                                                                 op0=ALU.mult, op1=ALU.add)
                        ins.then_inc(c.s["vbank_empty"], 1)
                    dve.wait_ge(c.s["vbank_empty"], n("vb", 2 * e + 4))
                dve.wait_ge(c.s["gated"], gated0 + 1 + b)
                nc.vector.tensor_tensor(c.x[:, b], c.x[:, b], tmp, ALU.add).then_inc(c.s["finished"], 1)
            gated0 = B
            loop(c, dve, B, turn)

        @block.scalar
        def _(act):
            act.wait_ge(c.s["load"], loaded)
            g = (lambda k: gains[:, k:k + 1], lambda k: gains[:, 2 + k:3 + k])
            ln_gain(c, act, start["sb"], *g)

            def turn(b, more):
                n = Span(s0, MOE, b)
                act.wait_ge(c.s["logits_shifted"], n("mo", 1))
                nc.scalar.activation(lg[:, :, :], lg[:, :, :], ACT.Exp).then_inc(c.s["logits_exped"], 1)
                for e in range(E):
                    for m in range(KF):
                        act.wait_ge(c.s["sbank_full"], n("sb", KF * e + m + 1))
                        if e >= 2:
                            act.wait_ge(c.s["vbank_full"], n("vb", 2 * e))
                        nc.scalar.activation(gT[:, KF * (e % 2) + m, :], c.sbank[m % 2][:, :],
                                             ACT.Gelu_apprx_tanh).then_inc(c.s["sbank_empty"], 1)
                if more:
                    ln_gain(c, act, n("sb", KF * E), *g)
            loop(c, act, B, turn)

        @block.tensor
        def _(pe):
            pe.wait_ge(c.s["load"], loaded)
            pe.wait_ge(c.s["aux"], 7)
            ln_turn(c, pe, start["ln"], start["sb"])

            def turn(b, more):
                n = Span(s0, MOE, b)
                pe.wait_ge(c.s["sbank_empty"], n("sb"))
                pe.wait_ge(c.s["vbank_empty"], n("vb", -1))
                for t in range(NT):
                    for k in range(KD):
                        ins = nc.tensor.matmul(c.vbank[0][:, t * E:(t + 1) * E], c.hT[:, k, 1 + t * P:1 + (t + 1) * P],
                                               wr[:, k, :], start=(k == 0), stop=(k == KD - 1))
                ins.then_inc(c.s["vbank_full"], 1)

                def up(e):
                    for m in range(KF):
                        pe.wait_ge(c.s["sbank_empty"], n("sb", KF * e + m - 1))
                        for k in range(KD):
                            ins = nc.tensor.matmul(c.sbank[m % 2][:, :], w1[:, e, k, m * P:(m + 1) * P],
                                                   c.hT[:, k, 1:T + 1], start=(k == 0), stop=(k == KD - 1))
                        ins.then_inc(c.s["sbank_full"], 1)

                def down(e):
                    pe.wait_ge(c.s["sbank_empty"], n("sb", KF * (e + 1)))
                    for i in range(2):
                        pe.wait_ge(c.s["vbank_empty"], n("vb", 2 * e + 1 + i))
                        for t in range(2 * i, 2 * i + 2):
                            for k in range(KF):
                                ins = nc.tensor.matmul(c.vbank[i][:, (t % 2) * D:(t % 2 + 1) * D],
                                                       gT[:, KF * (e % 2) + k, t * P:(t + 1) * P], w2[:, e, k, :],
                                                       start=(k == 0), stop=(k == KF - 1))
                        ins.then_inc(c.s["vbank_full"], 1)

                up(0)
                pe.wait_ge(c.s["chosen"], n("mo", 1))
                pe.wait_ge(c.s["vbank_empty"], n("vb", 0))
                for i, m in enumerate((tri, ones)):
                    ins = nc.tensor.matmul(c.vbank[1][:, i * NT * E:(i + 1) * NT * E], m[:, :],
                                           chosen[:, :, :].rearrange("p t e -> p (t e)"), start=True, stop=True)
                ins.then_inc(c.s["vbank_full"], 1)
                for e in range(1, E):
                    up(e)
                    down(e - 1)
                if more:
                    ln_turn(c, pe, n("ln"), n("sb", KF * E))
                down(E - 1)
            loop(c, pe, B, turn)


def build(nc, d, outs):
    with ExitStack() as st:
        c = Chip()
        c.nc = nc
        c.s = {name: st.enter_context(nc.semaphore(name)) for name in SEMS}

        def sb(name, shape, dt=F32):
            return st.enter_context(nc.sbuf_tensor(name, shape, dt))

        def pair(name):
            return [st.enter_context(nc.psum_tensor(f"{name}{i}", [P, T], F32)) for i in range(2)]

        c.x = sb("x", [P, B, NT, D])
        c.y = sb("y", [P, B, NT, D])
        c.hT = sb("hT", [P, KD, T + 1])
        c.xn = sb("xn", [P, NT, D])
        c.ident = sb("ident", [P, P])
        c.modT = sb("modT", [P, 4, KD, B])
        c.bn = sb("bn", [P, NT, 6])
        c.mv = sb("mv", [P, NT, 2])
        c.ve = sb("ve", [P, NT])
        c.rstd = sb("rstd", [P, NT])
        c.mhalf = sb("mhalf", [P, NT])
        c.score = sb("score", [P, 4, T])
        c.prob = sb("prob", [P, 8, T])
        c.probT = sb("probT", [P, 8, T])
        c.least = sb("least", [P, 8])
        c.psum_of = sb("psum_of", [P, 8])
        c.rsum = sb("rsum", [P, 8])
        c.vbank, c.pbank, c.sbank, c.obank = pair("vbank"), pair("pbank"), pair("sbank"), pair("obank")
        c.mod_dram = nc.dram_tensor("modulation", (2, B, 6 * D), F32).ap()
        c.loaded = 64
        opening(c, d)
        n = layer0(c, d, dict(OPENING))
        n = remix(c, d, n, None, "ca", "sa")
        n = layer1(c, d, n)
        n = remix(c, d, n, "ga", "cb", "sb")
        n = cross(c, d, n)
        moe(c, d, n, outs[0])


def kernel(**inputs):
    import numpy as np
    import concourse.bacc as bacc
    from concourse.bass_utils import run_bass_kernel_spmd

    inputs = {k: np.asarray(v) for k, v in inputs.items()}
    arrays = {"x": inputs["L0_attn_x"]}
    for short, name in (("qw", "q_w"), ("kw", "k_w"), ("vw", "v_w"), ("ow", "o_w")):
        arrays[short] = inputs[f"L0_attn_{name}"]
    for l in range(2):
        arrays[f"c{l}"] = inputs[f"L{l}_c"].T
        arrays[f"wmod{l}"] = inputs[f"L{l}_wmod"]
    for short, name in (("Wr", "W_r"), ("Wk", "W_k"), ("Wv", "W_v")):
        arrays[short] = inputs[f"L0_ffn_{name}"].T
    for name in ("mu_r", "mu_k"):
        arrays[name] = inputs[f"L0_ffn_{name}"].reshape(KD, P).T
    for short, name in (("Aq", "Wq"), ("Ak", "Wk"), ("Ao", "Wo"), ("W1", "W1"), ("W2", "W2"), ("bo", "bo"), ("b2", "b2")):
        arrays[short] = inputs[f"L1_attn_{name}"]
    wide = [inputs[f"L1_attn_{name}"] for name in ("Wq", "Wk", "Wv")]
    arrays["wtok"] = np.concatenate([wide[0][:, :, P:], wide[1][:, :, P:], wide[2]], axis=2)
    by_feature = [inputs[f"L1_attn_{name}"].reshape(DEPTH, -1, P) for name in ("ln1_g", "ln1_b", "ln2_g", "ln2_b", "b1")]
    arrays["vec"] = np.concatenate(by_feature, axis=1).transpose(2, 0, 1)
    for short, name in (("wqkv", "qkv_weight"), ("wproj", "proj_weight")):
        arrays[short] = inputs[f"L1_ffn_{name}"].T
    for short, ln in (("cross_ln", "ln1"), ("moe_ln", "ln2")):
        both = [inputs[f"L1_ffn_{ln}_{name}"].reshape(KD, P) for name in ("weight", "bias")]
        arrays[short] = np.concatenate(both).T
    for short, name in (("wrouter", "router_weight"), ("we1", "moe_w1"), ("we2", "moe_w2")):
        arrays[short] = inputs[f"L1_ffn_{name}"]
    arrays = {k: np.ascontiguousarray(v) for k, v in arrays.items()}
    nc = bacc.Bacc("TRN2", target_bir_lowering=False, num_devices=1)
    d = {k: nc.dram_tensor(f"in_{k}", v.shape, mybir.dt.from_np(v.dtype), kind="ExternalInput").ap()
         for k, v in arrays.items()}
    out = nc.dram_tensor("out_x", (B, T, D), F32, kind="ExternalOutput").ap()
    build(nc, d, [out])
    r = run_bass_kernel_spmd(nc, [{f"in_{k}": v for k, v in arrays.items()}], core_ids=[0])
    return r.results[0]["out_x"]
```

```python
from contextlib import ExitStack

import concourse.bass as bass
from concourse import mybir

F32 = mybir.dt.float32
I32 = mybir.dt.int32
U32 = mybir.dt.uint32
ALU = mybir.AluOpType
ACT = mybir.ActivationFunctionType
AX = mybir.AxisListType

P = 128
B = 8
T = 512
NT = T // P
D = 256
KD = D // P
EPS = 1e-5
BIG = 1e30
GATE_MIN = 0.25
H0, HD0 = 16, 16
DEPTH = 4
H1, HD1 = 8, 32
BUCKET = 64
NU = T // BUCKET
FF = 4 * D
MF = FF // P
NH, NKV, E, TOPK = 16, 4, 8, 2
HDM = D // NH
QKV = NKV * (NH // NKV + 2) * HDM
FM = 512
CAP = -(-(B * T * TOPK * 5) // (E * 4))
SEMS = ("load aux store resid_ready mod_ready "
        "vbank_full vbank_empty pbank_full pbank_empty sbank_full sbank_empty obank_full obank_empty "
        "stats_ready rstd_ready normed_ready scores_exped sums_inverted q_ready probs_ready "
        "carry_ready mixed_ready squared_ready v_chain p_chain s_chain settled "
        "attn_weights mlp_weights attn_biased mlp_biased mlp_full mlp_added lin_turned lin_qT_ready "
        "lin_shifted lin_exped lin_inverted lin_q_ready lin_k_ready "
        "context_ready lin_full lin_out gated scaled shifted "
        "products_ready products_used cross_shifted cross_exped cross_probs "
        "logits_shifted logits_exped chosen finished stored").split()


class Span:

    def __init__(self, start, turn, i):
        self.start, self.turn, self.i = start, turn, i

    def __call__(self, name, k=0):
        return self.start.get(name, 0) + self.i * self.turn.get(name, 0) + k


def after(start, turn, n):
    return {k: start.get(k, 0) + n * turn.get(k, 0) for k in {*start, *turn}}


class Chip:
    pass


def alone(c, eng):
    eng.sem_inc(c.s["settled"], 1)


def chain(c, eng, sem, ins):
    ins.then_inc(sem, 1)
    eng.wait_ge(sem, 1)
    eng.sem_clear(sem)



def ln_stats(c, dve, n, src):
    nc = c.nc
    dve.wait_ge(c.s["normed_ready"], n)
    alone(c, dve)
    for t in range(NT):
        ins = nc.vector.bn_stats(c.bn[:, t, :], src[:, t, :])
    chain(c, dve, c.s["v_chain"], ins)
    for t in range(NT):
        ins = nc.vector.bn_aggr(c.mv[:, t, :], c.bn[:, t, :])
    ins.then_inc(c.s["stats_ready"], 1)


def ln_rstd(c, pool, n):
    nc = c.nc
    pool.wait_ge(c.s["stats_ready"], n + 1)
    alone(c, pool)
    chain(c, pool, c.s["p_chain"], nc.gpsimd.tensor_scalar(c.ve[:, :], c.mv[:, :, 1], EPS, None, ALU.add))
    nc.gpsimd.tensor_tensor(c.rstd[:, :], c.ve[:, :], c.mhalf[:, :], ALU.pow).then_inc(c.s["rstd_ready"], 1)


def ln_norm(c, dve, n, src, sbank_before, dst=None):
    nc = c.nc
    dve.wait_ge(c.s["rstd_ready"], n + 1)
    if dst is None:
        dst = c.xn
        dve.wait_ge(c.s["sbank_full"], sbank_before)
    for t in range(NT):
        ins = nc.vector.tensor_scalar(dst[:, t, :], src[:, t, :], c.mv[:, t, 0:1], c.rstd[:, t:t + 1],
                                      ALU.subtract, ALU.mult)
    ins.then_inc(c.s["normed_ready"], 1)


def ln_turn(c, pe, n, sb):
    nc = c.nc
    pe.wait_ge(c.s["normed_ready"], n + 1)
    for half in range(KD):
        pe.wait_ge(c.s["sbank_empty"], sb + half - 1)
        for t in range(NT):
            ins = nc.tensor.transpose(c.sbank[half][:, t * P:(t + 1) * P], c.xn[:, t, half * P:(half + 1) * P],
                                      c.ident[:, :])
        ins.then_inc(c.s["sbank_full"], 1)


def ln_gain(c, act, sb, gain, shift, dst=None):
    nc = c.nc
    dst = c.hT if dst is None else dst
    for half in range(KD):
        act.wait_ge(c.s["sbank_full"], sb + half + 1)
        alone(c, act)
        nc.scalar.activation(dst[:, half, 1:T + 1], c.sbank[half][:, :], ACT.Identity, bias=shift(half),
                             scale=gain(half)).then_inc(c.s["sbank_empty"], 1)



LAG_N, LAG_T, LAG_PT, LAG_AV = 5, 8, 9, 10


class Heads:

    def __init__(self, quads, q_of, k_of, keys_of, mask_of, v_of, out_of, vb, opens=lambda q: True,
                 closes=lambda q: True, q_needed=lambda q, j: None):
        self.quads, self.q_of, self.k_of, self.keys_of = quads, q_of, k_of, keys_of
        self.mask_of, self.v_of, self.out_of, self.vb = mask_of, v_of, out_of, vb
        self.opens, self.closes, self.q_needed = opens, closes, q_needed
        self.items = 4 * quads
        self.steps = self.items + LAG_AV + 4


def heads_pe(c, pe, n, h, mid):
    nc = c.nc

    def score(k):
        q, j = divmod(k, 4)
        keys = h.keys_of(q)
        needed = h.q_needed(q, j)
        if needed is not None:
            pe.wait_ge(c.s["q_ready"], n("qr", needed))
        pe.wait_ge(c.s["vbank_empty"], n("vb", h.vb + k - 1))
        nc.tensor.matmul(c.vbank[k % 2][:, 0:P * len(keys)], h.q_of(q, j), h.k_of(q, j, keys[0], keys[-1] + 1),
                         start=True, stop=True).then_inc(c.s["vbank_full"], 1)

    def turn(k):
        q, j = divmod(k, 4)
        if k >= 2:
            pe.wait_ge(c.s["pbank_empty"], n("pb", k - 1))
        pe.wait_ge(c.s["probs_ready"], n("pb", k + 1))
        for m in range(len(h.keys_of(q))):
            ins = nc.tensor.transpose(c.pbank[k % 2][:, m * P:(m + 1) * P], c.prob[:, k % 8, m * P:(m + 1) * P],
                                      c.ident[:, :])
        ins.then_inc(c.s["pbank_full"], 1)

    def values(q):
        pe.wait_ge(c.s["pbank_empty"], n("pb", 4 * q + 4))
        keys = h.keys_of(q)
        bank, cols = h.out_of(q)
        for m, key in enumerate(keys):
            for j in range(4):
                ins = nc.tensor.matmul(bank[32 * j:32 * j + 32, cols], h.v_of(q, j, key),
                                       c.probT[:, (4 * q + j) % 8, m * P:(m + 1) * P],
                                       start=(m == 0 and h.opens(q)), stop=(m == len(keys) - 1 and h.closes(q)),
                                       tile_position=(0, 32 * j))
        ins.then_inc(c.s["obank_full"], 1)

    for t in range(h.steps):
        if t < h.items:
            score(t)
        if 0 <= t - LAG_T < h.items:
            turn(t - LAG_T)
        q, r = divmod(t - LAG_AV - 3, 4)
        if r == 0 and 0 <= q < h.quads:
            values(q)
        mid(t)


def heads_dve(c, dve, n, h, mid):
    nc = c.nc
    for t in range(h.steps):
        if t < h.items:
            q, j = divmod(t, 4)
            width = P * len(h.keys_of(q))
            if t >= 4:
                dve.wait_ge(c.s["scores_exped"], n("pb", t - 3))
            dve.wait_ge(c.s["vbank_full"], n("vb", h.vb + t + 1))
            alone(c, dve)
            nc.vector.tensor_tensor_reduce(out=c.score[:, t % 4, 0:width], in0=c.vbank[t % 2][:, 0:width],
                                           in1=h.mask_of(q, j), scale=1.0, scalar=3e38, op0=ALU.add, op1=ALU.min,
                                           accum_out=c.least[:, t % 8:t % 8 + 1]).then_inc(c.s["vbank_empty"], 1)
        q, r = divmod(t - LAG_N, 4)
        if r == 0 and 0 <= q < h.quads:
            dve.wait_ge(c.s["scores_exped"], n("pb", 4 * q + 4))
            lo = 4 * (q % 2)
            nc.vector.reciprocal(c.rsum[:, lo:lo + 4], c.psum_of[:, lo:lo + 4]).then_inc(c.s["sums_inverted"], 1)
        k = t - LAG_PT
        if 0 <= k < h.items:
            q = k // 4
            width = P * len(h.keys_of(q))
            dve.wait_ge(c.s["pbank_full"], n("pb", k + 1))
            if q >= 2:
                dve.wait_ge(c.s["obank_full"], n("av", q - 1))
            nc.vector.tensor_copy(c.probT[:, k % 8, 0:width], c.pbank[k % 2][:, 0:width])\
              .then_inc(c.s["pbank_empty"], 1)
        mid(t)


def heads_pool(c, pool, n, h, mid):
    nc = c.nc
    for q in range(h.quads):
        width = P * len(h.keys_of(q))
        pool.wait_ge(c.s["sums_inverted"], n("av", q + 1))
        for lo in (4 * (q % 2), 4 * (q % 2) + 2):
            two = c.prob[:, lo:lo + 2, 0:width]
            nc.gpsimd.tensor_tensor(two, two, c.rsum[:, lo:lo + 2].unsqueeze(2).to_broadcast([P, 2, width]), ALU.mult)\
              .then_inc(c.s["probs_ready"], 2)
        mid(q)


def heads_act(c, act, n, h, mid):
    nc = c.nc
    for k in range(h.items):
        q, j = divmod(k, 4)
        width = P * len(h.keys_of(q))
        if k >= 8:
            act.wait_ge(c.s["pbank_full"], n("pb", k - 7))
        act.wait_ge(c.s["vbank_empty"], n("vb", h.vb + k + 1))
        nc.scalar.activation(c.prob[:, k % 8, 0:width], c.score[:, k % 4, 0:width], ACT.Exp,
                             bias=c.least[:, k % 8:k % 8 + 1], scale=-1.0,
                             accum_out=c.psum_of[:, k % 8:k % 8 + 1]).then_inc(c.s["scores_exped"], 1)
        mid(k)


def nothing(t):
    pass


def loop(c, eng, n, body):
    alone(c, eng)
    with eng.Fori(0, n - 1) as i:
        body(i, True)
    body(n - 1, False)



CHUNK = {"sa": 0, "ca": 1, "ga": 2, "sb": 3, "cb": 4, "gb": 5}
BEGIN = {"vb": 2, "sb": 2, "ln": 1}
OPENING = {"vb": BEGIN["vb"] + 8, "sb": BEGIN["sb"], "ln": BEGIN["ln"]}


def opening(c, d):
    nc = c.nc
    with ExitStack() as st:
        def sb(name, shape, dt=F32):
            return st.enter_context(nc.sbuf_tensor(name, shape, dt))

        cT = sb("cT", [P, 2, KD, B])
        wm = sb("wm", [P, 2, KD, 6 * D])
        rows = sb("rows", [B, 2, 6 * D])
        sign = sb("sign", [B, D])
        ones = sb("ones", [P, P])
        block = st.enter_context(nc.Block())

        @block.sync
        def _(sp):
            for name, count in (("vbank_full", BEGIN["vb"]), ("vbank_empty", BEGIN["vb"]), ("sbank_full", BEGIN["sb"]),
                                ("sbank_empty", BEGIN["sb"]), ("stats_ready", BEGIN["ln"]), ("rstd_ready", BEGIN["ln"]),
                                ("normed_ready", BEGIN["ln"])):
                sp.sem_inc(c.s[name], count)
            for l in range(2):
                sp.dma_start(cT[:, l, :, :], d[f"c{l}"].rearrange("(k p) b -> p k b", p=P)).then_inc(c.s["load"], 16)
                sp.dma_start(wm[:, l, :, :], d[f"wmod{l}"].rearrange("(k p) n -> p k n", p=P))\
                  .then_inc(c.s["load"], 16)
            for b in range(B):
                sp.dma_start(c.x[:, b, :, :], d["x"][b].rearrange("(t p) n -> p t n", p=P))\
                  .then_inc(c.s["resid_ready"], 16)
            sp.wait_ge(c.s["mod_ready"], 2)
            sp.dma_start(c.mod_dram.rearrange("l b n -> b l n"), rows[:, :, :]).then_inc(c.s["store"], 16)
            sp.wait_ge(c.s["store"], 16)
            sp.wait_ge(c.s["resid_ready"], 16 * B)

        @block.scalar
        def _(act):
            act.wait_ge(c.s["load"], 64)
            nc.scalar.activation(cT[:, :, :, :], cT[:, :, :, :], ACT.Silu).then_inc(c.s["aux"], 1)

        @block.gpsimd
        def _(pool):
            nc.gpsimd.memset(c.mhalf[:, :], -0.5)
            chain(c, pool, c.s["p_chain"], nc.gpsimd.memset(ones[:, :], 1.0))
            nc.gpsimd.affine_select(out=c.ident[:, :], in_=ones[:, :], compare_op=ALU.is_equal, fill=0.0, base=0,
                                    pattern=[[-1, P]], channel_multiplier=1).then_inc(c.s["aux"], 1)

        @block.tensor
        def _(pe):
            pe.wait_ge(c.s["aux"], 2)
            n = BEGIN["vb"]
            for l in range(2):
                for m in range(3):
                    pe.wait_ge(c.s["vbank_empty"], n - 1)
                    for k in range(KD):
                        ins = nc.tensor.matmul(c.vbank[n % 2][0:B, :], cT[:, l, k, :], wm[:, l, k, m * T:(m + 1) * T],
                                               start=(k == 0), stop=(k == KD - 1))
                    ins.then_inc(c.s["vbank_full"], 1)
                    n += 1
            pe.wait_ge(c.s["mod_ready"], 2)
            for pair in (("sa", "ca"), ("sb", "cb")):
                pe.wait_ge(c.s["vbank_empty"], n - 1)
                for i, name in enumerate(pair):
                    for k in range(KD):
                        at = CHUNK[name] * D + k * P
                        ins = nc.tensor.transpose(c.vbank[n % 2][:, (i * KD + k) * B:(i * KD + k + 1) * B],
                                                  rows[:, 0, at:at + P], c.ident[0:B, 0:B])
                ins.then_inc(c.s["vbank_full"], 1)
                n += 1

        @block.vector
        def _(dve):
            n = BEGIN["vb"]
            for l in range(2):
                for m in range(3):
                    dve.wait_ge(c.s["vbank_full"], n + 1)
                    ins = nc.vector.tensor_copy(rows[:, l, m * T:(m + 1) * T], c.vbank[n % 2][0:B, :])
                    ins.then_inc(c.s["vbank_empty"], 1)
                    n += 1
                dve.wait_ge(c.s["vbank_empty"], n)
                for name in ("ca", "cb"):
                    at = CHUNK[name] * D
                    v = rows[:, l, at:at + D]
                    chain(c, dve, c.s["v_chain"], nc.vector.tensor_scalar(v, v, 1.0, None, ALU.add))
                for name in ("ga", "gb"):
                    at = CHUNK[name] * D
                    v = rows[:, l, at:at + D]
                    chain(c, dve, c.s["v_chain"], nc.vector.tensor_scalar(sign[:, :], v, 0.0, 2.0, ALU.is_ge, ALU.mult))
                    chain(c, dve, c.s["v_chain"], nc.vector.tensor_scalar(sign[:, :], sign[:, :], -1.0, None, ALU.add))
                    chain(c, dve, c.s["v_chain"], nc.vector.tensor_tensor(v, v, sign[:, :], ALU.mult))
                    ins = nc.vector.scalar_tensor_tensor(out=v, in0=v, scalar=GATE_MIN, in1=sign[:, :], op0=ALU.max,
                                                         op1=ALU.mult)
                    if name == "gb":
                        ins.then_inc(c.s["mod_ready"], 1)
                        dve.wait_ge(c.s["mod_ready"], l + 1)
                    else:
                        chain(c, dve, c.s["v_chain"], ins)
            for i in range(2):
                dve.wait_ge(c.s["vbank_full"], n + 1)
                nc.vector.tensor_copy(c.modT[:, 2 * i:2 * i + 2, :, :],
                                      c.vbank[n % 2][:, 0:2 * KD * B].rearrange("p (i k b) -> p i k b", k=KD, b=B))\
                  .then_inc(c.s["vbank_empty"], 1)
                n += 1
            dve.wait_ge(c.s["vbank_empty"], n)


def mod_rows(c, l, name):
    at = CHUNK[name] * D
    return c.mod_dram[l, :, at:at + D].partition_broadcast(P)



PROJ0 = {"vb": KD + 2, "sb": KD}
HEADS0 = {"vb": 4 * 16 + 2, "sb": 2, "pb": 64, "av": 16, "ob": KD, "ln": 1, "qr": H0}
ATTN0 = after(HEADS0, PROJ0, 1)
FFN0 = {"vb": 2, "sb": 6, "ln": 1, "mx": 1}


def one(ap, i):
    return ap[:, i:i + 1] if isinstance(i, int) else ap[:, bass.ds(i, 1)]


def layer0(c, d, start):
    nc = c.nc
    with ExitStack() as st:
        def sb(name, shape, dt=F32):
            return st.enter_context(nc.sbuf_tensor(name, shape, dt))

        gates = sb("gates0", [P, 2, B, D])
        wqkv = sb("wqkv0", [P, 3, KD, D])
        wo = sb("wo0", [P, KD, D])
        wf = sb("wf0", [P, 3, KD, D])
        mu = sb("mu0", [P, 2, KD])
        omu = sb("omu0", [P, 2, KD])
        scale = sb("scale0", [P, H0 // KD])
        qT = sb("qT0", [P, H0, T])
        kT = sb("kT0", [P, KD, T])
        vt = sb("vt0", [P, NT, H0 // 2, 2, 32])
        aoT = sb("aoT0", [P, KD, T])
        mixT = qT[:, 0:2 * KD, :].rearrange("p (i k) t -> p i k t", k=KD)
        carry = qT[:, 2 * KD:4 * KD, :].rearrange("p (i k) t -> p i k t", k=KD)
        krelu, kact = qT[:, 4 * KD:5 * KD, :], qT[:, 5 * KD:6 * KD, :]
        rsig = qT[:, 6 * KD:7 * KD, :].rearrange("p i (t n) -> p (i t) n", n=D)
        slope_mask = c.y[:, :, :, :].rearrange("p (h b) t n -> p h (b t n)", h=2)\
            .rearrange("p h (i n) -> p (h i) n", n=T)
        tmp = sb("tmp0", [P, 2, D])
        norm = after(start, {"sb": 2, "ln": 1}, 1)
        s0 = after(after(norm, PROJ0, 1), {"qr": 4}, 1)
        s1 = after(after(after(s0, ATTN0, B - 1), HEADS0, 1), {"qr": -4}, 1)
        end = after(after(s1, FFN0, B), {"sb": -2, "ln": -1}, 1)

        block = st.enter_context(nc.Block())

        def mod(i, b):
            return lambda k: one(c.modT[:, i, k, :], b)

        def head(s, j):
            return 8 * (s // 2) + 2 * j + s % 2

        def place(q):
            return 2 * (q // 8) + q % 2, (q % 8) // 2

        def of(f):
            return lambda q, *rest: f(*place(q), *rest)

        h = Heads(
            quads=H0,
            q_of=of(lambda s, tile, j: qT[:, head(s, j), tile * P:(tile + 1) * P]),
            k_of=of(lambda s, tile, j, lo, hi: kT[:, s // 2, lo * P:hi * P]),
            keys_of=of(lambda s, tile: list(range(tile + 1))),
            mask_of=of(lambda s, tile, j: slope_mask[:, head(s, j), (3 - tile) * P:T]),
            v_of=of(lambda s, tile, j, key: vt[:, key, head(s, j) // 2, s % 2, :]),
            out_of=of(lambda s, tile: (c.obank[s // 2], slice(tile * P, (tile + 1) * P))),
            vb=0,
            opens=lambda q: q % 2 == 0,
            closes=lambda q: q % 2 == 1,
            q_needed=of(lambda s, tile, j: 4 * (s - 1) + j + 1 if tile == 0 else None))
        L = c.loaded

        @block.sync
        def _(sp):
            for i, name in enumerate(("qw", "kw", "vw")):
                sp.dma_start(wqkv[:, i, :, :], d[name].rearrange("(k p) n -> p k n", p=P)).then_inc(c.s["load"], 16)
            sp.dma_start(wo[:, :, :], d["ow"].rearrange("(k p) n -> p k n", p=P)).then_inc(c.s["load"], 16)
            for i, name in enumerate(("Wr", "Wk", "Wv")):
                sp.dma_start(wf[:, i, :, :], d[name].rearrange("(k p) n -> p k n", p=P)).then_inc(c.s["load"], 16)
            for i, name in enumerate(("mu_r", "mu_k")):
                sp.dma_start(mu[:, i, :], d[name]).then_inc(c.s["load"], 16)
            for i, name in enumerate(("ga", "gb")):
                sp.dma_start(gates[:, i, :, :], mod_rows(c, 0, name)).then_inc(c.s["load"], 16)
        loaded0 = L + 11 * 16

        @block.gpsimd
        def _(pool):
            nc.gpsimd.memset(vt[:, :, :, :, :], 0.0)
            nc.gpsimd.memset(c.hT[:, :, 0:1], 0.0)
            chain(c, pool, c.s["p_chain"], nc.gpsimd.memset(scale[:, :], -float(HD0) ** -0.5))
            for base, step in ((0, 1), (HD0 - 1, -1)):
                ins = nc.gpsimd.affine_select(out=scale[:, :], in_=scale[:, :], compare_op=ALU.is_ge, fill=0.0,
                                              base=base, pattern=[[-HD0 * step, H0 // KD]], channel_multiplier=step)
                if step == 1:
                    chain(c, pool, c.s["p_chain"], ins)
            ins.then_inc(c.s["aux"], 1)
            ln_rstd(c, pool, start["ln"])
            dist = slope_mask[:, H0 - 1, :]
            chain(c, pool, c.s["p_chain"], nc.gpsimd.iota(dist, pattern=[[-1, T]], base=T - P, channel_multiplier=1,
                                                          allow_small_or_imprecise_dtypes=True))
            chain(c, pool, c.s["p_chain"], nc.gpsimd.affine_select(out=dist, in_=dist, compare_op=ALU.is_ge, fill=BIG,
                                                                   base=T - P, pattern=[[-1, T]],
                                                                   channel_multiplier=1))
            for i in range(H0):
                slope = float((2.0 ** (-8.0 / H0)) ** (i + 1))
                ins = nc.gpsimd.tensor_scalar(slope_mask[:, i, :], dist, slope, None, ALU.mult)
            ins.then_inc(c.s["aux"], 1)

            def attn(b, more):
                n = Span(s0, ATTN0, b)

                def mid(q):
                    if q == 2:
                        ln_rstd(c, pool, n("ln"))
                heads_pool(c, pool, n, h, mid)
            loop(c, pool, B, attn)
            pool.wait_ge(c.s["vbank_full"], s1["vb"])

            def ffn(b, more):
                n = Span(s1, FFN0, b)
                pool.wait_ge(c.s["sbank_empty"], n("sb"))
                alone(c, pool)
                for i in range(2):
                    for k in range(KD):
                        ins = nc.gpsimd.tensor_scalar(carry[:, i, k, :], c.hT[:, k, 0:T], omu[:, i, k:k + 1], None,
                                                      ALU.mult)
                ins.then_inc(c.s["carry_ready"], 1)
                if more:
                    ln_rstd(c, pool, n("ln"))
                pool.wait_ge(c.s["sbank_empty"], n("sb", 4))
                for k in range(KD):
                    ins = nc.gpsimd.tensor_tensor(kact[:, k, :], krelu[:, k, :], krelu[:, k, :], ALU.mult)
                ins.then_inc(c.s["squared_ready"], 1)
            loop(c, pool, B, ffn)

        @block.vector
        def _(dve):
            ln_stats(c, dve, start["ln"], c.x[:, 0])
            ln_norm(c, dve, start["ln"], c.x[:, 0], start["sb"])
            dve.wait_ge(c.s["load"], loaded0)
            chain(c, dve, c.s["v_chain"], nc.vector.tensor_scalar(omu[:, :, :], mu[:, :, :], -1.0, 1.0, ALU.mult,
                                                                  ALU.add))
            dve.wait_ge(c.s["aux"], 4)

            def keys_out(n, k, vb):
                dve.wait_ge(c.s["vbank_full"], n("vb", vb + k + 1))
                nc.vector.tensor_copy(kT[:, k, :], c.vbank[k][:, :]).then_inc(c.s["vbank_empty"], 1)

            def values_out(n, vb):
                for i in range(2):
                    dve.wait_ge(c.s["vbank_full"], n("vb", vb + i + 1))
                    for odd in range(2):
                        src = c.vbank[i][:, :].rearrange("p (t h z e) -> p t h z e", t=2, z=2, e=HD0)
                        ins = nc.vector.tensor_copy(vt[:, 2 * i:2 * i + 2, :, odd, HD0 * odd:HD0 * odd + HD0],
                                                    src[:, :, :, odd, :])
                    ins.then_inc(c.s["vbank_empty"], 1)

            first = Span(norm, PROJ0, 0)
            for k in range(KD):
                keys_out(first, k, 0)
            values_out(first, KD)

            def attn(b, more):
                n = Span(s0, ATTN0, b)

                def mid(t):
                    nxt = c.x[:, b + 1] if more else c.x[:, 0]
                    if t == 16:
                        ln_stats(c, dve, n("ln"), nxt)
                    if t == 20:
                        ln_norm(c, dve, n("ln"), nxt, n("sb"))
                    if more and t in (66, 68):
                        keys_out(n, (t - 66) // 2, 64)
                heads_dve(c, dve, n, h, mid)
                if more:
                    dve.wait_ge(c.s["obank_full"], n("av", 16))
                    values_out(n, 66)
                out = 68 if more else 64
                for i in range(2):
                    dve.wait_ge(c.s["vbank_full"], n("vb", out + 1 + i))
                    gate = one_row(gates[:, 0], b)
                    chain(c, dve, c.s["v_chain"],
                          nc.vector.tensor_tensor(tmp[:, :, :], c.vbank[i][:, :].rearrange("p (t n) -> p t n", t=2),
                                                  gate, ALU.mult))
                    xs = c.x[:, b, 2 * i:2 * i + 2, :]
                    nc.vector.tensor_tensor(xs, xs, tmp[:, :, :], ALU.add).then_inc(c.s["vbank_empty"], 1)
                    dve.wait_ge(c.s["vbank_empty"], n("vb", out + 1 + i))
            loop(c, dve, B, attn)

            def ffn(b, more):
                n = Span(s1, FFN0, b)
                dve.wait_ge(c.s["carry_ready"], n("mx", 1))
                for i in range(2):
                    for k in range(KD):
                        ins = nc.vector.scalar_tensor_tensor(out=mixT[:, i, k, :], in0=c.hT[:, k, 1:T + 1],
                                                             scalar=mu[:, i, k:k + 1], in1=carry[:, i, k, :],
                                                             op0=ALU.mult, op1=ALU.add)
                ins.then_inc(c.s["mixed_ready"], 1)
                if more:
                    ln_stats(c, dve, n("ln"), c.x[:, b + 1])
                    ln_norm(c, dve, n("ln"), c.x[:, b + 1], n("sb"))
                for i in range(2):
                    dve.wait_ge(c.s["vbank_full"], n("vb", 1 + i))
                    chain(c, dve, c.s["v_chain"],
                          nc.vector.tensor_tensor(tmp[:, :, :], c.vbank[i][:, :].rearrange("p (t n) -> p t n", t=2),
                                                  rsig[:, 2 * i:2 * i + 2, :], ALU.mult))
                    chain(c, dve, c.s["v_chain"], nc.vector.tensor_tensor(tmp[:, :, :], tmp[:, :, :],
                                                                          one_row(gates[:, 1], b), ALU.mult))
                    xs = c.x[:, b, 2 * i:2 * i + 2, :]
                    nc.vector.tensor_tensor(xs, xs, tmp[:, :, :], ALU.add).then_inc(c.s["vbank_empty"], 1)
                    dve.wait_ge(c.s["vbank_empty"], n("vb", 1 + i))
            loop(c, dve, B, ffn)

        @block.scalar
        def _(act):
            ln_gain(c, act, start["sb"], mod(1, 0), mod(0, 0))

            def q_out(k, full):
                hd = head(k // 4, k % 4)
                if k % 8 == 0:
                    act.wait_ge(c.s["sbank_full"], full)
                    alone(c, act)
                nc.scalar.activation(qT[:, hd, :], c.sbank[k // 8][:, :], ACT.Identity,
                                     scale=scale[:, hd % 8:hd % 8 + 1]).then_inc(c.s["q_ready"], 1)

            for k in range(4):
                q_out(k, norm["sb"] + 1)

            def attn(b, more):
                n = Span(s0, ATTN0, b)

                def out(g):
                    act.wait_ge(c.s["obank_full"], n("av", 8 * g + 8))
                    nc.scalar.copy(aoT[:, g, :], c.obank[g][:, :]).then_inc(c.s["obank_empty"], 1)

                def mid(k):
                    if k < 12:
                        q_out(k + 4, n("sb"))
                        if k + 4 in (7, 15):
                            act.wait_ge(c.s["q_ready"], n("qr", k + 1))
                            act.sem_inc(c.s["sbank_empty"], 1)
                    if k == 48:
                        out(0)
                    if k == 44:
                        if more:
                            ln_gain(c, act, n("sb"), mod(1, b + 1), mod(0, b + 1))
                        else:
                            ln_gain(c, act, n("sb"), mod(3, 0), mod(2, 0))
                heads_act(c, act, n, h, mid)
                if more:
                    for k in range(4):
                        q_out(k, n("sb", 3))
                out(1)
            loop(c, act, B, attn)

            def ffn(b, more):
                n = Span(s1, FFN0, b)
                for i in range(2):
                    act.wait_ge(c.s["sbank_full"], n("sb", 1 + i))
                    nc.scalar.activation(rsig[:, 2 * i:2 * i + 2, :],
                                         c.sbank[i][:, :].rearrange("p (t n) -> p t n", t=2),
                                         ACT.Sigmoid).then_inc(c.s["sbank_empty"], 1)
                for i in range(KD):
                    act.wait_ge(c.s["sbank_full"], n("sb", 3 + i))
                    nc.scalar.activation(krelu[:, i, :], c.sbank[i][:, :], ACT.Relu).then_inc(c.s["sbank_empty"], 1)
                if more:
                    ln_gain(c, act, n("sb", 4), mod(3, b + 1), mod(2, b + 1))
            loop(c, act, B, ffn)

        @block.tensor
        def _(pe):
            ln_turn(c, pe, start["ln"], start["sb"])
            pe.wait_ge(c.s["load"], loaded0)

            def queries_and_keys(n, g, sb, vb):
                for i, (bank, full, empty, job) in enumerate(
                        ((c.sbank, "sbank_full", "sbank_empty", n("sb", sb)),
                         (c.vbank, "vbank_full", "vbank_empty", n("vb", vb)))):
                    pe.wait_ge(c.s[empty], job + g - 1)
                    for k in range(KD):
                        ins = nc.tensor.matmul(bank[g][:, :], wqkv[:, i, k, g * P:(g + 1) * P],
                                               c.hT[:, k, 1:T + 1], start=(k == 0), stop=(k == KD - 1))
                    ins.then_inc(c.s[full], 1)

            def values(n, i, vb):
                pe.wait_ge(c.s["vbank_empty"], n("vb", vb + i - 1))
                for t in range(2 * i, 2 * i + 2):
                    for k in range(KD):
                        ins = nc.tensor.matmul(c.vbank[i][:, (t % 2) * D:(t % 2 + 1) * D],
                                               c.hT[:, k, 1 + t * P:1 + (t + 1) * P], wqkv[:, 2, k, :],
                                               start=(k == 0), stop=(k == KD - 1))
                ins.then_inc(c.s["vbank_full"], 1)

            first = Span(norm, PROJ0, 0)
            pe.wait_ge(c.s["sbank_empty"], norm["sb"])
            for g in range(KD):
                queries_and_keys(first, g, 0, 0)
            for i in range(2):
                values(first, i, KD)
            pe.wait_ge(c.s["vbank_empty"], s0["vb"])

            def attn(b, more):
                n = Span(s0, ATTN0, b)

                def mid(t):
                    if t == 32:
                        ln_turn(c, pe, n("ln"), n("sb"))
                    if more and t in (64, 66):
                        if t == 64:
                            pe.wait_ge(c.s["sbank_empty"], n("sb", 2))
                        queries_and_keys(n, (t - 64) // 2, 2, 64)
                    if more and t in (69, 71):
                        values(n, (t - 69) // 2, 66)
                heads_pe(c, pe, n, h, mid)
                pe.wait_ge(c.s["obank_empty"], n("ob", KD))
                out = 68 if more else 64
                for i in range(2):
                    pe.wait_ge(c.s["vbank_empty"], n("vb", out - 1 + i))
                    for t in range(2 * i, 2 * i + 2):
                        for g in range(KD):
                            ins = nc.tensor.matmul(c.vbank[i][:, (t % 2) * D:(t % 2 + 1) * D],
                                                   aoT[:, g, t * P:(t + 1) * P], wo[:, g, :],
                                                   start=(g == 0), stop=(g == KD - 1))
                    ins.then_inc(c.s["vbank_full"], 1)
            loop(c, pe, B, attn)

            def ffn(b, more):
                n = Span(s1, FFN0, b)
                pe.wait_ge(c.s["mixed_ready"], n("mx", 1))
                for i in range(2):
                    pe.wait_ge(c.s["sbank_empty"], n("sb", i - 1))
                    for t in range(2 * i, 2 * i + 2):
                        for k in range(KD):
                            ins = nc.tensor.matmul(c.sbank[i][:, (t % 2) * D:(t % 2 + 1) * D],
                                                   mixT[:, 0, k, t * P:(t + 1) * P], wf[:, 0, k, :],
                                                   start=(k == 0), stop=(k == KD - 1))
                    ins.then_inc(c.s["sbank_full"], 1)
                for i in range(KD):
                    pe.wait_ge(c.s["sbank_empty"], n("sb", 1 + i))
                    for k in range(KD):
                        ins = nc.tensor.matmul(c.sbank[i][:, :], wf[:, 1, k, i * P:(i + 1) * P], mixT[:, 1, k, :],
                                               start=(k == 0), stop=(k == KD - 1))
                    ins.then_inc(c.s["sbank_full"], 1)
                if more:
                    ln_turn(c, pe, n("ln"), n("sb", 4))
                pe.wait_ge(c.s["squared_ready"], n("mx", 1))
                for i in range(2):
                    pe.wait_ge(c.s["vbank_empty"], n("vb", i - 1))
                    for t in range(2 * i, 2 * i + 2):
                        for k in range(KD):
                            ins = nc.tensor.matmul(c.vbank[i][:, (t % 2) * D:(t % 2 + 1) * D],
                                                   kact[:, k, t * P:(t + 1) * P], wf[:, 2, k, :],
                                                   start=(k == 0), stop=(k == KD - 1))
                    ins.then_inc(c.s["vbank_full"], 1)
            loop(c, pe, B, ffn)
    c.loaded = loaded0
    return end


def one_row(rows, b):
    r = rows[:, b:b + 1, :] if isinstance(b, int) else rows[:, bass.ds(b, 1), :]
    return r.to_broadcast([P, 2, D])


def row_of(rows, b):
    return rows[:, b:b + 1, :] if isinstance(b, int) else rows[:, bass.ds(b, 1), :]



REMIX = {"ln": 1, "rx": 1}


def remix(c, d, start, gate, scale, shift):
    nc = c.nc
    end = after(start, REMIX, B)
    names = [gate, scale, shift] if gate else [scale, shift]
    with ExitStack() as st:
        rows = st.enter_context(nc.sbuf_tensor(f"rows_{scale}", [P, 3, B, D], F32))
        block = st.enter_context(nc.Block())
        loaded = c.loaded + 16 * len(names)

        @block.sync
        def _(sp):
            for i, name in enumerate(names):
                sp.dma_start(rows[:, i + (not gate), :, :], mod_rows(c, 1, name)).then_inc(c.s["load"], 16)

        @block.gpsimd
        def _(pool):
            pool.wait_ge(c.s["load"], loaded)

            def turn(b, more):
                n = Span(start, REMIX, b)
                if gate:
                    yb = c.y[:, b]
                    nc.gpsimd.tensor_tensor(yb, yb, row_of(rows[:, 0], b).to_broadcast([P, NT, D]), ALU.mult)\
                      .then_inc(c.s["gated"], 1)
                ln_rstd(c, pool, n("ln"))
                pool.wait_ge(c.s["normed_ready"], n("ln", 1))
                yb = c.y[:, b]
                nc.gpsimd.tensor_tensor(yb, yb, row_of(rows[:, 1], b).to_broadcast([P, NT, D]), ALU.mult)\
                  .then_inc(c.s["scaled"], 1)
            with pool.Fori(0, B) as b:
                turn(b, True)

        @block.vector
        def _(dve):
            dve.wait_ge(c.s["load"], loaded)
            with dve.Fori(0, B) as b:
                n = Span(start, REMIX, b)
                if gate:
                    dve.wait_ge(c.s["gated"], n("rx", 1 - start.get("rx", 0)))
                    chain(c, dve, c.s["v_chain"], nc.vector.tensor_tensor(c.x[:, b], c.x[:, b], c.y[:, b], ALU.add))
                ln_stats(c, dve, n("ln"), c.x[:, b])
                ln_norm(c, dve, n("ln"), c.x[:, b], 0, dst=c.y[:, b])
                dve.wait_ge(c.s["scaled"], n("rx", 1))
                nc.vector.tensor_tensor(c.y[:, b], c.y[:, b], row_of(rows[:, 2], b).to_broadcast([P, NT, D]), ALU.add)
    c.loaded = loaded
    return end



ATTN1 = {"vb": 26, "pb": 16, "av": 4, "ob": 2, "at": 1}
VL = 2 * P
LIN = VL + P
CTX = HD1 + 1
CTXW = P + 4


KEPT = 8


class Turn:

    def __init__(self, attn, mlp, more):
        self.attn, self.mlp, self.more = attn, mlp, more
        self.qk = 0
        self.mlp_norm = 2 * attn
        self.hidden = self.mlp_norm + 2 * mlp
        self.next_norm = self.hidden + MF * mlp
        self.adds = {"sb": self.next_norm + 2 * more, "ln": mlp + more, "ml": mlp}
        if attn:
            self.adds.update(ATTN1)


FIRST, INNER, LAST, TAIL = Turn(1, 0, 1), Turn(1, 1, 1), Turn(1, 1, 0), Turn(0, 1, 1)
DEPTH_ADDS = {}
for _turn, _times in ((FIRST, 1), (INNER, B - 2), (LAST, 1), (TAIL, 1)):
    DEPTH_ADDS = after(DEPTH_ADDS, _turn.adds, _times)


def depth_turns(c, eng, start, body):
    body(0, FIRST, Span(start, FIRST.adds, 0))
    start = after(start, FIRST.adds, 1)
    alone(c, eng)
    with eng.Fori(0, B - 2) as i:
        body(i + 1, INNER, Span(start, INNER.adds, i))
    start = after(start, INNER.adds, B - 2)
    body(B - 1, LAST, Span(start, LAST.adds, 0))
    start = after(start, LAST.adds, 1)
    body(B, TAIL, Span(start, TAIL.adds, 0))


def layer1(c, d, start):
    nc = c.nc
    begin = after(start, {"sb": KD, "ln": 1}, 1)
    end = after(begin, DEPTH_ADDS, DEPTH)
    with ExitStack() as st:
        def sb(name, shape, dt=F32):
            return st.enter_context(nc.sbuf_tensor(name, shape, dt))

        wq = sb("wq1", [P, KD, P])
        wk = sb("wk1", [P, KD, P])
        wtok = sb("wtok", [P, KD, 2 * P + D])
        wo = sb("wo1", [P, KD, D])
        w1 = sb("w1", [P, KD, FF])
        w2 = sb("w2", [P, MF, D])
        bo = sb("bo", [P, 1, D])
        b2 = sb("b2", [P, 1, D])
        vec = sb("vec", [P, DEPTH + 1, 8 + MF])
        qT = sb("qT1", [P, T])
        kT = sb("kT1", [P, T])
        tok = sb("tok", [P, NT, LIN + P + 4])
        kneg = sb("kneg", [P, NT, P])
        qmax = sb("qmax", [P, NT, 4])
        qinv = sb("qinv", [P, NT, 4])
        qlT = sb("qlT", [P, T])
        ctx = sb("ctx", [P, NU - 1, CTX])
        kcum = sb("kcum", [P, NU - 1])
        bd = sb("bd", [P, NU - 1, P])
        mask = sb("mask", [P, 2 * P])
        aoT = sb("aoT1", [P, KD, T])
        h2T = sb("h2T", [P, KD, T + 1])
        gT = sb("gT", [P, MF, T])
        block = st.enter_context(nc.Block())

        def depth_start(e):
            return {k: begin.get(k, 0) + e * DEPTH_ADDS.get(k, 0) for k in {*begin, *DEPTH_ADDS}}

        h = Heads(
            quads=4,
            q_of=lambda q, j: qT[32 * j:32 * j + 32, q * P:(q + 1) * P],
            k_of=lambda q, j, lo, hi: kT[32 * j:32 * j + 32, lo * P:hi * P],
            keys_of=lambda q: [q - 1, q] if q else [q],
            mask_of=lambda q, j: mask[:, 0:2 * P] if q else mask[:, P:2 * P],
            v_of=lambda q, j, key: tok[:, key, VL + 32 * j:VL + 32 * j + 32],
            out_of=lambda q: (c.obank[0], slice(q * P, (q + 1) * P)),
            vb=4)
        all_wa, all_wm = 5 * 16, 3 * 16

        @block.sync
        def _(sp):
            sp.dma_start(vec[:, 0:DEPTH, :], d["vec"]).then_inc(c.s["load"], 16)

            def attn_weights(e):
                sp.dma_start(wtok[:, :, :], d["wtok"][e].rearrange("(k p) n -> p k n", p=P))\
                  .then_inc(c.s["attn_weights"], 16)
                for w, name in ((wq, "Aq"), (wk, "Ak")):
                    sp.dma_start(w[:, :, :], d[name][e].rearrange("(k p) n -> p k n", p=P)[:, :, 0:P])\
                      .then_inc(c.s["attn_weights"], 16)
                sp.dma_start(wo[:, :, :], d["Ao"][e].rearrange("(k p) n -> p k n", p=P))\
                  .then_inc(c.s["attn_weights"], 16)
                sp.dma_start(bo[:, :, :], row(d["bo"], e)).then_inc(c.s["attn_weights"], 16)

            def mlp_weights(e):
                sp.dma_start(w1[:, :, :], d["W1"][e].rearrange("(k p) n -> p k n", p=P))\
                  .then_inc(c.s["mlp_weights"], 16)
                sp.dma_start(w2[:, :, :], d["W2"][e].rearrange("(k p) n -> p k n", p=P))\
                  .then_inc(c.s["mlp_weights"], 16)
                sp.dma_start(b2[:, :, :], row(d["b2"], e)).then_inc(c.s["mlp_weights"], 16)

            def row(bias, e):
                return (bias[e:e + 1, :] if isinstance(e, int) else bias[bass.ds(e, 1), :]).partition_broadcast(P)

            attn_weights(0)
            mlp_weights(0)
            with sp.Fori(0, DEPTH - 1) as e:
                n = Span(begin, DEPTH_ADDS, e)
                sp.wait_ge(c.s["vbank_empty"], n("vb", DEPTH_ADDS["vb"]))
                attn_weights(e + 1)
                sp.wait_ge(c.s["mlp_added"], 2 * B * (e + 1))
                mlp_weights(e + 1)

        @block.gpsimd
        def _(pool):
            nc.gpsimd.memset(bd[:, :, :], 0.0)
            nc.gpsimd.memset(aoT[:, 1, 0:BUCKET], 0.0)
            nc.gpsimd.memset(tok[:, :, LIN + P:LIN + P + 1], 1.0)
            nc.gpsimd.memset(vec[:, DEPTH, :], 0.0)
            chain(c, pool, c.s["p_chain"], nc.gpsimd.memset(mask[:, :], 0.0))
            cur = mask[:, P:2 * P]
            nc.gpsimd.affine_select(out=cur, in_=cur, compare_op=ALU.is_ge, fill=BIG, base=0, pattern=[[-1, P]],
                                    channel_multiplier=1).then_inc(c.s["aux"], 1)
            ln_rstd(c, pool, start["ln"])
            with pool.Fori(0, DEPTH) as e:
                pool.wait_ge(c.s["attn_weights"], (e + 1) * all_wa)
                alone(c, pool)
                pool.wait_ge(c.s["mlp_weights"], (e + 1) * all_wm)
                alone(c, pool)

                def body(b, turn, n):
                    if turn.mlp:
                        ln_rstd(c, pool, n("ln"))
                    if turn.attn:
                        pool.wait_ge(c.s["normed_ready"], n("ln"))
                        yb = c.y[:, b]
                        nc.gpsimd.tensor_tensor(yb, yb, bo[:, :, :].to_broadcast([P, NT, D]), ALU.add)\
                          .then_inc(c.s["attn_biased"], 1)
                    if turn.mlp:
                        pool.wait_ge(c.s["normed_ready"], n("ln", 1))
                        yb = c.y[:, b - 1]
                        nc.gpsimd.tensor_tensor(yb, yb, b2[:, :, :].to_broadcast([P, NT, D]), ALU.add)\
                          .then_inc(c.s["mlp_biased"], 1)
                    if turn.attn:
                        pool.wait_ge(c.s["lin_inverted"], n("at", 1))
                        ql = tok[:, :, 0:P].rearrange("p t (h e) -> p t h e", e=HD1)
                        nc.gpsimd.tensor_tensor(ql, ql, qinv[:, :, :].unsqueeze(3).to_broadcast([P, NT, 4, HD1]),
                                                ALU.mult).then_inc(c.s["lin_q_ready"], 1)

                        def mid(q):
                            if q == 1 and turn.more:
                                ln_rstd(c, pool, n("ln", turn.mlp))
                        heads_pool(c, pool, n, h, mid)
                    elif turn.more:
                        ln_rstd(c, pool, n("ln", turn.mlp))
                depth_turns(c, pool, depth_start(e), body)

        @block.vector
        def _(dve):
            ln_stats(c, dve, start["ln"], c.y[:, 0])
            ln_norm(c, dve, start["ln"], c.y[:, 0], start["sb"])
            dve.wait_ge(c.s["aux"], 5)
            with dve.Fori(0, DEPTH) as e:

                def body(b, turn, n):
                    if turn.mlp:
                        ln_stats(c, dve, n("ln"), c.y[:, b - 1])
                    if turn.attn:
                        for t in range(NT):
                            dve.wait_ge(c.s["vbank_full"], n("vb", t + 1))
                            nc.vector.tensor_copy(tok[:, t, 0:LIN + P], c.vbank[t % 2][:, :])\
                              .then_inc(c.s["vbank_empty"], 1)
                            if t == 1 and turn.mlp:
                                ln_norm(c, dve, n("ln"), c.y[:, b - 1], n("sb"))
                        dve.wait_ge(c.s["vbank_empty"], n("vb", NT))
                        attention(b, turn, n)
                    else:
                        ln_norm(c, dve, n("ln"), c.y[:, b - 1], n("sb"))
                        ln_stats(c, dve, n("ln", 1), c.y[:, 0])
                        ln_norm(c, dve, n("ln", 1), c.y[:, 0], n("sb", turn.hidden))
                        mlp_sum(b, n, 0)
                        mlp_sum(b, n, 1)

                def mlp_sum(b, n, i):
                    dve.wait_ge(c.s["mlp_biased"], n("ml", 1))
                    dve.wait_ge(c.s["mlp_full"], 2 * n("ml") + i + 1)
                    ys = c.y[:, b - 1, 2 * i:2 * i + 2, :]
                    nc.vector.tensor_tensor(ys, ys, c.sbank[i][:, :].rearrange("p (t n) -> p t n", t=2), ALU.add)\
                      .then_inc(c.s["mlp_added"], 1)

                def attention(b, turn, n):
                    ql = tok[:, :, 0:P].rearrange("p t (h e) -> p t h e", e=HD1)
                    kl = tok[:, :, P:2 * P]
                    nc.vector.tensor_scalar(kneg[:, :, :], kl, 0.0, None, ALU.min)
                    chain(c, dve, c.s["v_chain"],
                          nc.vector.tensor_reduce(qmax[:, :, :], ql, AX.X, ALU.max))
                    nc.vector.tensor_tensor(ql, ql, qmax[:, :, :].unsqueeze(3).to_broadcast([P, NT, 4, HD1]),
                                            ALU.subtract).then_inc(c.s["lin_shifted"], 1)

                    def context(i):
                        dve.wait_ge(c.s["vbank_full"], n("vb", 21 + i))
                        us = min(2, NU - 1 - 2 * i)
                        src = c.vbank[i % 2][:, 0:us * CTXW].rearrange("p (u n) -> p u n", u=us)
                        for j in range(4):
                            nc.vector.tensor_copy(ctx[32 * j:32 * j + 32, 2 * i:2 * i + us, 0:HD1],
                                                  src[32 * j:32 * j + 32, :, 32 * j:32 * j + 32])
                        nc.vector.tensor_copy(ctx[:, 2 * i:2 * i + us, HD1:CTX], src[:, :, P:P + 1])\
                          .then_inc(c.s["vbank_empty"], 1)

                    def mid(t):
                        if t == 2:
                            dve.wait_ge(c.s["lin_exped"], n("at", 0) * 2 + 1)
                            chain(c, dve, c.s["v_chain"],
                                  nc.vector.tensor_reduce(qmax[:, :, :], ql, AX.X, ALU.add))
                            nc.vector.reciprocal(qinv[:, :, :], qmax[:, :, :]).then_inc(c.s["lin_inverted"], 1)
                        if t == 4:
                            dve.wait_ge(c.s["lin_exped"], n("at", 0) * 2 + 2)
                            nc.vector.scalar_tensor_tensor(out=kl, in0=kl, scalar=0.0, in1=kneg[:, :, :],
                                                           op0=ALU.max, op1=ALU.add).then_inc(c.s["lin_k_ready"], 1)
                        if turn.more and t == 9:
                            ln_stats(c, dve, n("ln", turn.mlp), c.y[:, b + 1])
                        if turn.more and t == 12:
                            ln_norm(c, dve, n("ln", turn.mlp), c.y[:, b + 1], n("sb", turn.hidden))
                        if t >= 20 and t % 2 == 0 and t < 28:
                            context((t - 20) // 2)
                    heads_dve(c, dve, n, h, mid)
                    dve.wait_ge(c.s["vbank_empty"], n("vb", 24))
                    for u in range(2, NU - 1, 2):
                        to = slice(u, min(u + 2, NU - 1))
                        before = ctx[:, u - 1:u, :].to_broadcast([P, to.stop - to.start, CTX])
                        chain(c, dve, c.s["v_chain"], nc.vector.tensor_tensor(ctx[:, to, :], ctx[:, to, :], before,
                                                                              ALU.add))
                    chain(c, dve, c.s["v_chain"], nc.vector.tensor_scalar(kcum[:, :], ctx[:, :, HD1], 1e-6, None,
                                                                          ALU.add))
                    chain(c, dve, c.s["v_chain"], nc.vector.reciprocal(kcum[:, :], kcum[:, :]))
                    for j in range(4):
                        q = slice(32 * j, 32 * j + 32)
                        ins = nc.vector.tensor_tensor(bd[q, :, q], ctx[q, :, 0:HD1],
                                                      kcum[q, :].unsqueeze(2).to_broadcast([32, NU - 1, HD1]),
                                                      ALU.mult)
                    ins.then_inc(c.s["context_ready"], 1)
                    if turn.mlp:
                        mlp_sum(b, n, 0)
                        mlp_sum(b, n, 1)
                    dve.wait_ge(c.s["attn_biased"], n("at", 1))
                    for i in range(2):
                        dve.wait_ge(c.s["vbank_full"], n("vb", 25 + i))
                        ys = c.y[:, b, 2 * i:2 * i + 2, :]
                        nc.vector.tensor_tensor(ys, ys, c.vbank[i][:, :].rearrange("p (t n) -> p t n", t=2), ALU.add)\
                          .then_inc(c.s["vbank_empty"], 1)
                    dve.wait_ge(c.s["vbank_empty"], n("vb", 26))
                depth_turns(c, dve, depth_start(e), body)

        @block.scalar
        def _(act):
            act.wait_ge(c.s["load"], c.loaded + 16)
            ln_gain(c, act, start["sb"], lambda k: vec[:, 0, k:k + 1], lambda k: vec[:, 0, 2 + k:3 + k])
            with act.Fori(0, DEPTH) as e:
                v = vec[:, e, :]

                def body(b, turn, n):
                    if turn.attn:
                        act.wait_ge(c.s["sbank_full"], n("sb", 1))
                        nc.scalar.mul(qT[:, :], c.sbank[0][:, :], -float(HD1) ** -0.5).then_inc(c.s["sbank_empty"], 1)
                        act.wait_ge(c.s["sbank_full"], n("sb", 2))
                        nc.scalar.copy(kT[:, :], c.sbank[1][:, :]).then_inc(c.s["sbank_empty"], 1)
                    if turn.mlp:
                        ln_gain(c, act, n("sb", turn.mlp_norm), lambda k: v[:, 4 + k:5 + k],
                                lambda k: v[:, 6 + k:7 + k], h2T)
                        for m in range(MF):
                            act.wait_ge(c.s["sbank_full"], n("sb", turn.hidden + m + 1))
                            alone(c, act)
                            nc.scalar.activation(gT[:, m, :], c.sbank[m % 2][:, :], ACT.Gelu, bias=v[:, 8 + m:9 + m])\
                              .then_inc(c.s["sbank_empty"], 1)
                    if turn.attn:
                        act.wait_ge(c.s["lin_shifted"], n("at", 1))
                        nc.scalar.activation(tok[:, :, 0:P], tok[:, :, 0:P], ACT.Exp).then_inc(c.s["lin_exped"], 1)
                        nc.scalar.activation(kneg[:, :, :], kneg[:, :, :], ACT.Exp).then_inc(c.s["lin_exped"], 1)

                        def mid(k):
                            if k == 11:
                                act.wait_ge(c.s["lin_turned"], n("at", 1))
                                nc.scalar.copy(qlT[:, :], c.obank[1][:, :]).then_inc(c.s["lin_qT_ready"], 1)
                        heads_act(c, act, n, h, mid)
                        act.wait_ge(c.s["obank_full"], n("av", 4))
                        nc.scalar.copy(aoT[:, 0, :], c.obank[0][:, :]).then_inc(c.s["obank_empty"], 1)
                        act.wait_ge(c.s["lin_full"], n("at", 1))
                        nc.scalar.copy(aoT[:, 1, BUCKET:T], c.obank[1][:, BUCKET:T]).then_inc(c.s["obank_empty"], 1)
                    if turn.more:
                        w = v if turn.attn else vec[:, e + 1, :]
                        ln_gain(c, act, n("sb", turn.next_norm), lambda k: w[:, k:k + 1], lambda k: w[:, 2 + k:3 + k])
                depth_turns(c, act, depth_start(e), body)

        @block.tensor
        def _(pe):
            ln_turn(c, pe, start["ln"], start["sb"])
            with pe.Fori(0, DEPTH) as e:
                pe.wait_ge(c.s["attn_weights"], (e + 1) * all_wa)
                alone(c, pe)

                def body(b, turn, n):
                    if turn.attn:
                        project(n)
                    if turn.mlp:
                        pe.wait_ge(c.s["mlp_weights"], (e + 1) * all_wm)
                        ln_turn(c, pe, n("ln"), n("sb", turn.mlp_norm))
                        pe.wait_ge(c.s["sbank_empty"], n("sb", turn.hidden))
                        for m in range(MF):
                            pe.wait_ge(c.s["sbank_empty"], n("sb", turn.hidden + m - 1))
                            for k in range(KD):
                                ins = nc.tensor.matmul(c.sbank[m % 2][:, :], w1[:, k, m * P:(m + 1) * P],
                                                       h2T[:, k, 1:T + 1], start=(k == 0), stop=(k == KD - 1))
                            ins.then_inc(c.s["sbank_full"], 1)
                    pieces = [(i, t, m) for i in range(2) for t in (2 * i, 2 * i + 1) for m in range(MF)] \
                        if turn.mlp else []

                    def down(count, kept=0):
                        count = min(count, max(0, len(pieces) - kept))
                        for i, t, m in pieces[:count]:
                            if m == 0 and t == 2 * i:
                                pe.wait_ge(c.s["sbank_empty"], n("sb", turn.next_norm + i - 1))
                                if i == 0:
                                    pe.wait_ge(c.s["sbank_empty"], n("sb", turn.next_norm))
                            ins = nc.tensor.matmul(c.sbank[i][:, (t % 2) * D:(t % 2 + 1) * D],
                                                   gT[:, m, t * P:(t + 1) * P], w2[:, m, :],
                                                   start=(m == 0), stop=(m == MF - 1))
                            if m == MF - 1 and t == 2 * i + 1:
                                ins.then_inc(c.s["mlp_full"], 1)
                        del pieces[:count]

                    if turn.attn:
                        attention(turn, n, down)
                    else:
                        down(4 * MF)
                        next_norm(turn, n)

                def next_norm(turn, n):
                    if turn.mlp:
                        pe.wait_ge(c.s["mlp_added"], 2 * n("ml", 1))
                    ln_turn(c, pe, n("ln", turn.mlp), n("sb", turn.next_norm))

                def project(n):
                    pe.wait_ge(c.s["sbank_empty"], n("sb"))
                    for t in range(NT):
                        pe.wait_ge(c.s["vbank_empty"], n("vb", t - 1))
                        for k in range(KD):
                            ins = nc.tensor.matmul(c.vbank[t % 2][:, :], c.hT[:, k, 1 + t * P:1 + (t + 1) * P],
                                                   wtok[:, k, :], start=(k == 0), stop=(k == KD - 1))
                        ins.then_inc(c.s["vbank_full"], 1)
                        if t % 2 == 1:
                            i = t // 2
                            pe.wait_ge(c.s["sbank_empty"], n("sb", i - 1))
                            for k in range(KD):
                                ins = nc.tensor.matmul(c.sbank[i][:, :], (wq, wk)[i][:, k, :], c.hT[:, k, 1:T + 1],
                                                       start=(k == 0), stop=(k == KD - 1))
                            ins.then_inc(c.s["sbank_full"], 1)

                def attention(turn, n, down):
                    pe.wait_ge(c.s["sbank_empty"], n("sb", 2))

                    def context(i):
                        pe.wait_ge(c.s["vbank_empty"], n("vb", 19 + i))
                        for u in range(2 * i, min(2 * i + 2, NU - 1)):
                            rows = slice(0, BUCKET if u % 2 == 0 else P)
                            at = (u % 2) * CTXW
                            ins = nc.tensor.matmul(c.vbank[i % 2][:, at:at + P + 1], tok[rows, u // 2, P:2 * P],
                                                   tok[rows, u // 2, LIN:LIN + P + 1], start=True, stop=True)
                        ins.then_inc(c.s["vbank_full"], 1)

                    def mid(t):
                        if t >= 2:
                            down(2, KEPT)
                        if t == 9:
                            pe.wait_ge(c.s["lin_q_ready"], n("at", 1))
                            for r in range(NT):
                                ins = nc.tensor.transpose(c.obank[1][:, r * P:(r + 1) * P], tok[:, r, 0:P],
                                                          c.ident[:, :])
                            ins.then_inc(c.s["lin_turned"], 1)
                        if t == 16:
                            pe.wait_ge(c.s["lin_k_ready"], n("at", 1))
                            context(0)
                            context(1)
                        if t == 22:
                            context(2)
                        if t == 24:
                            context(3)
                    heads_pe(c, pe, n, h, mid)
                    down(4 * MF)
                    pe.wait_ge(c.s["lin_qT_ready"], n("at", 1))
                    pe.wait_ge(c.s["context_ready"], n("at", 1))
                    for u in range(NU - 1):
                        cols = slice(BUCKET * (u + 1), BUCKET * (u + 2))
                        ins = nc.tensor.matmul(c.obank[1][:, cols], bd[:, u, :], qlT[:, cols], start=True, stop=True)
                    ins.then_inc(c.s["lin_full"], 1)
                    if turn.more:
                        next_norm(turn, n)
                    pe.wait_ge(c.s["obank_empty"], n("ob", 2))
                    for i in range(2):
                        pe.wait_ge(c.s["vbank_empty"], n("vb", 23 + i))
                        for t in range(2 * i, 2 * i + 2):
                            for k in range(KD):
                                ins = nc.tensor.matmul(c.vbank[i][:, (t % 2) * D:(t % 2 + 1) * D],
                                                       aoT[:, k, t * P:(t + 1) * P], wo[:, k, :],
                                                       start=(k == 0), stop=(k == KD - 1))
                        ins.then_inc(c.s["vbank_full"], 1)
                depth_turns(c, pe, depth_start(e), body)
    c.loaded += 16
    return end



CROSS = {"vb": B + 4, "sb": 8, "ln": 2, "cr": 1, "pr": 16, "ab": 1}
GW = QKV // NKV
QH = NH // NKV


def cross(c, d, start):
    nc = c.nc
    end = after(start, CROSS, NT)
    with ExitStack() as st:
        def sb(name, shape, dt=F32):
            return st.enter_context(nc.sbuf_tensor(name, shape, dt))

        wqkv = sb("wqkv", [P, KD, QKV])
        wp = sb("wproj", [P, KD, D])
        g1 = sb("cross_gain", [P, 2 * KD])
        qkv = sb("qkv", [P, B, QKV])
        prod = sb("prod", [P, 2, NKV * B * QH * HDM])
        sc = sb("cross_scores", [P, NH, B, B])
        pr = sb("cross_probs", [P, NH, B, B])
        mx = sb("cross_max", [P, NH, B])
        ao = sb("cross_out", [P, B, D])
        aoT = sb("cross_outT", [P, KD, B, P])
        block = st.enter_context(nc.Block())
        loaded = c.loaded + 3 * 16

        def part(s, g, at, n):
            return qkv[:, s, g * GW + at:g * GW + at + n]

        @block.sync
        def _(sp):
            sp.dma_start(wqkv[:, :, :], d["wqkv"].rearrange("(k p) n -> p k n", p=P)).then_inc(c.s["load"], 16)
            sp.dma_start(wp[:, :, :], d["wproj"].rearrange("(k p) n -> p k n", p=P)).then_inc(c.s["load"], 16)
            sp.dma_start(g1[:, :], d["cross_ln"]).then_inc(c.s["load"], 16)

        @block.gpsimd
        def _(pool):
            nc.gpsimd.memset(sc[:, :, :, :], -BIG).then_inc(c.s["aux"], 1)
            with pool.Fori(0, NT) as p:
                n = Span(start, CROSS, p)
                ln_rstd(c, pool, n("ln"))
                ln_rstd(c, pool, n("ln", 1))
                pool.wait_ge(c.s["vbank_empty"], n("vb", B))
                for s in range(B):
                    pool.wait_ge(c.s["products_used"], n("pr", s + 1))
                    for g in range(NKV):
                        out = prod[:, s % 2, g * (s + 1) * QH * HDM:(g + 1) * (s + 1) * QH * HDM]\
                            .rearrange("p (t h e) -> p t h e", h=QH, e=HDM)
                        q = part(s, g, 0, QH * HDM).rearrange("p (h e) -> p h e", h=QH).unsqueeze(1)\
                            .to_broadcast([P, s + 1, QH, HDM])
                        k = part(slice(0, s + 1), g, QH * HDM, HDM).unsqueeze(2).to_broadcast([P, s + 1, QH, HDM])
                        ins = nc.gpsimd.tensor_tensor(out, q, k, ALU.mult)
                    ins.then_inc(c.s["products_ready"], 1)
                pool.wait_ge(c.s["cross_probs"], n("cr", 1))
                for s in range(B):
                    pool.wait_ge(c.s["products_used"], n("pr", B + s + 1))
                    for g in range(NKV):
                        out = prod[:, s % 2, g * (s + 1) * QH * HDM:(g + 1) * (s + 1) * QH * HDM]\
                            .rearrange("p (h e t) -> p h e t", h=QH, e=HDM)
                        a = pr[:, g * QH:(g + 1) * QH, s, 0:s + 1].unsqueeze(2).to_broadcast([P, QH, HDM, s + 1])
                        v = part(slice(0, s + 1), g, (QH + 1) * HDM, HDM).rearrange("p t e -> p e t").unsqueeze(1)\
                            .to_broadcast([P, QH, HDM, s + 1])
                        ins = nc.gpsimd.tensor_tensor(out, a, v, ALU.mult)
                    ins.then_inc(c.s["products_ready"], 1)

        @block.vector
        def _(dve):
            dve.wait_ge(c.s["aux"], 6)
            dve.sem_inc(c.s["products_used"], 2)
            with dve.Fori(0, NT) as p:
                n = Span(start, CROSS, p)
                for half in range(2):
                    src = c.y[:, 4 * half:4 * half + 4, p, :]
                    ln_stats(c, dve, n("ln", half), src)
                    ln_norm(c, dve, n("ln", half), src, n("sb", 2 * half))
                for s in range(B):
                    dve.wait_ge(c.s["vbank_full"], n("vb", s + 1))
                    nc.vector.tensor_copy(qkv[:, s, :], c.vbank[s % 2][:, 0:QKV]).then_inc(c.s["vbank_empty"], 1)
                for s in range(B):
                    dve.wait_ge(c.s["products_ready"], n("pr", s + 1))
                    src = prod[:, s % 2, 0:(s + 1) * D].rearrange("p (g t h e) -> p g t h e", g=NKV, h=QH, e=HDM)
                    to = sc[:, :, s, 0:s + 1].rearrange("p (g h) t -> p g t h", g=NKV)
                    if s == 0:
                        src, to = src[:, :, 0], to[:, :, 0]
                    nc.vector.tensor_reduce(to, src, AX.X, ALU.add).then_inc(c.s["products_used"], 1)
                dve.wait_ge(c.s["products_used"], n("pr", B + 2))
                chain(c, dve, c.s["v_chain"], nc.vector.tensor_reduce(mx[:, :, :], sc[:, :, :, :], AX.X, ALU.max))
                nc.vector.tensor_tensor(pr[:, :, :, :], sc[:, :, :, :], mx[:, :, :].unsqueeze(3)
                                        .to_broadcast([P, NH, B, B]), ALU.subtract).then_inc(c.s["cross_shifted"], 1)
                dve.wait_ge(c.s["cross_exped"], n("cr", 1))
                chain(c, dve, c.s["v_chain"], nc.vector.tensor_reduce(mx[:, :, :], pr[:, :, :, :], AX.X, ALU.add))
                chain(c, dve, c.s["v_chain"], nc.vector.reciprocal(mx[:, :, :], mx[:, :, :]))
                nc.vector.tensor_tensor(pr[:, :, :, :], pr[:, :, :, :], mx[:, :, :].unsqueeze(3)
                                        .to_broadcast([P, NH, B, B]), ALU.mult).then_inc(c.s["cross_probs"], 1)
                for s in range(B):
                    dve.wait_ge(c.s["products_ready"], n("pr", B + s + 1))
                    src = prod[:, s % 2, 0:(s + 1) * D].rearrange("p (n t) -> p n t", t=s + 1)
                    nc.vector.tensor_reduce(ao[:, s, :], src, AX.X, ALU.add).then_inc(c.s["products_used"], 1)
                for i in range(4):
                    dve.wait_ge(c.s["vbank_full"], n("vb", B + i + 1))
                    ys = c.y[:, 2 * i:2 * i + 2, p, :]
                    nc.vector.tensor_tensor(ys, ys, c.vbank[i % 2][:, :].rearrange("p (t n) -> p t n", t=2), ALU.add)\
                      .then_inc(c.s["vbank_empty"], 1)

        @block.scalar
        def _(act):
            act.wait_ge(c.s["load"], loaded)
            with act.Fori(0, NT) as p:
                n = Span(start, CROSS, p)
                for half in range(2):
                    if half:
                        act.wait_ge(c.s["vbank_full"], n("vb", 4))
                    ln_gain(c, act, n("sb", 2 * half), lambda k: g1[:, k:k + 1], lambda k: g1[:, 2 + k:3 + k])
                act.wait_ge(c.s["cross_shifted"], n("cr", 1))
                nc.scalar.activation(pr[:, :, :, :], pr[:, :, :, :], ACT.Exp, scale=float(HDM) ** -0.5)\
                  .then_inc(c.s["cross_exped"], 1)
                for i in range(4):
                    act.wait_ge(c.s["sbank_full"], n("sb", 5 + i))
                    nc.scalar.copy(aoT[:, i // 2, 4 * (i % 2):4 * (i % 2) + 4, :].rearrange("p s t -> p (s t)"),
                                   c.sbank[i % 2][:, :]).then_inc(c.s["sbank_empty"], 1)

        @block.tensor
        def _(pe):
            pe.wait_ge(c.s["load"], loaded)
            with pe.Fori(0, NT) as p:
                n = Span(start, CROSS, p)
                for half in range(2):
                    ln_turn(c, pe, n("ln", half), n("sb", 2 * half))
                    pe.wait_ge(c.s["sbank_empty"], n("sb", 2 * half + 2))
                    for t in range(4):
                        pe.wait_ge(c.s["vbank_empty"], n("vb", 4 * half + t - 1))
                        for k in range(KD):
                            ins = nc.tensor.matmul(c.vbank[t % 2][:, 0:QKV], c.hT[:, k, 1 + t * P:1 + (t + 1) * P],
                                                   wqkv[:, k, :], start=(k == 0), stop=(k == KD - 1))
                        ins.then_inc(c.s["vbank_full"], 1)
                pe.wait_ge(c.s["products_used"], n("pr", 2 * B + 2))
                for i in range(4):
                    pe.wait_ge(c.s["sbank_empty"], n("sb", 3 + i))
                    for r in range(4):
                        s = 4 * (i % 2) + r
                        ins = nc.tensor.transpose(c.sbank[i % 2][:, r * P:(r + 1) * P],
                                                  ao[:, s, (i // 2) * P:(i // 2 + 1) * P], c.ident[:, :])
                    ins.then_inc(c.s["sbank_full"], 1)
                pe.wait_ge(c.s["sbank_empty"], n("sb", 8))
                for i in range(4):
                    pe.wait_ge(c.s["vbank_empty"], n("vb", B + i - 1))
                    for r in range(2):
                        for k in range(KD):
                            ins = nc.tensor.matmul(c.vbank[i % 2][:, r * D:(r + 1) * D], aoT[:, k, 2 * i + r, :],
                                                   wp[:, k, :], start=(k == 0), stop=(k == KD - 1))
                    ins.then_inc(c.s["vbank_full"], 1)
    c.loaded = loaded
    return end



MOE = {"vb": 2 + 2 * E, "sb": 4 * E + 2, "ln": 1, "mo": 1}
KF = FM // P


def moe(c, d, start, out):
    nc = c.nc
    start = dict(start)
    with ExitStack() as st:
        def sb(name, shape, dt=F32):
            return st.enter_context(nc.sbuf_tensor(name, shape, dt))

        w1 = sb("we1", [P, E, KD, FM])
        w2 = sb("we2", [P, E, KF, D])
        wr = sb("wrouter", [P, KD, E])
        gains = sb("moe_gain", [P, 2 * KD])
        gate = sb("gate1", [P, B, D])
        tri = sb("tri", [P, P])
        ones = sb("ones_moe", [P, P])
        expert = sb("expert", [P, 1, E])
        lg = sb("logits", [P, NT, E])
        top = sb("top", [P, NT, 8])
        index = sb("index", [P, NT, 8], U32)
        indexf = sb("indexf", [P, NT, 2])
        total = sb("total", [P, NT])
        hot = sb("hot", [P, 2, NT, E])
        chosen = sb("chosen", [P, NT, E])
        rank = sb("rank", [P, NT, E])
        base = sb("base", [P, NT + 1, E])
        w = sb("weight", [P, NT, E])
        tmp = c.probT[:, 0:2, :].rearrange("p i (t n) -> p (i t) n", t=2)
        gT = c.prob
        s0 = after(start, {"sb": KD, "ln": 1}, 1)
        block = st.enter_context(nc.Block())
        loaded = c.loaded + 5 * 16

        @block.sync
        def _(sp):
            sp.dma_start(wr[:, :, :], d["wrouter"].rearrange("(k p) n -> p k n", p=P)).then_inc(c.s["load"], 16)
            sp.dma_start(gains[:, :], d["moe_ln"]).then_inc(c.s["load"], 16)
            sp.dma_start(w1[:, :, :, :], d["we1"].rearrange("e (k p) n -> p e k n", p=P)).then_inc(c.s["load"], 16)
            sp.dma_start(w2[:, :, :, :], d["we2"].rearrange("e (k p) n -> p e k n", p=P)).then_inc(c.s["load"], 16)
            sp.dma_start(gate[:, :, :], mod_rows(c, 1, "gb")).then_inc(c.s["load"], 16)
            with sp.Fori(0, B) as b:
                sp.wait_ge(c.s["finished"], b + 1)
                sp.dma_start(out[b].rearrange("(t p) n -> p t n", p=P), c.x[:, b]).then_inc(c.s["stored"], 16)
            sp.wait_ge(c.s["stored"], 16 * B)

        @block.gpsimd
        def _(pool):
            ln_rstd(c, pool, start["ln"])
            chain(c, pool, c.s["p_chain"], nc.gpsimd.memset(ones[:, :], 1.0))
            nc.gpsimd.memset(base[:, 0:1, :], 0.0)
            nc.gpsimd.affine_select(out=tri[:, :], in_=ones[:, :], compare_op=ALU.is_gt, fill=0.0, base=0,
                                    pattern=[[1, P]], channel_multiplier=-1)
            nc.gpsimd.iota(expert[:, 0, :], pattern=[[1, E]], base=0, channel_multiplier=0,
                           allow_small_or_imprecise_dtypes=True).then_inc(c.s["aux"], 1)
            pool.wait_ge(c.s["load"], loaded)

            def turn(b, more):
                n = Span(s0, MOE, b)
                if more:
                    ln_rstd(c, pool, n("ln"))
                pool.wait_ge(c.s["vbank_empty"], n("vb", MOE["vb"]))
                nc.gpsimd.tensor_tensor(tmp, c.y[:, b], row_of(gate, b).to_broadcast([P, NT, D]), ALU.mult)\
                  .then_inc(c.s["gated"], 1)
            loop(c, pool, B, turn)

        @block.vector
        def _(dve):
            v = c.s["v_chain"]
            ln_stats(c, dve, start["ln"], c.y[:, 0])
            ln_norm(c, dve, start["ln"], c.y[:, 0], start["sb"])
            dve.wait_ge(c.s["aux"], 7)

            def over_experts(x):
                return x.unsqueeze(2).to_broadcast([P, NT, E])

            def turn(b, more):
                n = Span(s0, MOE, b)
                dve.wait_ge(c.s["vbank_full"], n("vb", 1))
                nc.vector.tensor_copy(lg[:, :, :], c.vbank[0][:, 0:NT * E].rearrange("p (t e) -> p t e", e=E))\
                  .then_inc(c.s["vbank_empty"], 1)
                dve.wait_ge(c.s["vbank_empty"], n("vb", 1))
                chain(c, dve, v, nc.vector.tensor_reduce(total[:, :], lg[:, :, :], AX.X, ALU.max))
                nc.vector.tensor_tensor(lg[:, :, :], lg[:, :, :], over_experts(total[:, :]), ALU.subtract)\
                  .then_inc(c.s["logits_shifted"], 1)
                dve.wait_ge(c.s["logits_exped"], n("mo", 1))
                chain(c, dve, v, nc.vector.tensor_reduce(total[:, :], lg[:, :, :], AX.X, ALU.add))
                chain(c, dve, v, nc.vector.reciprocal(total[:, :], total[:, :]))
                chain(c, dve, v, nc.vector.tensor_tensor(lg[:, :, :], lg[:, :, :], over_experts(total[:, :]),
                                                         ALU.mult))
                for t in range(NT):
                    ins = nc.vector.max(top[:, t, :], lg[:, t, :])
                chain(c, dve, v, ins)
                for t in range(NT):
                    ins = nc.vector.max_index(index[:, t, :], top[:, t, :], lg[:, t, :])
                chain(c, dve, v, ins)
                chain(c, dve, v, nc.vector.tensor_copy(indexf[:, :, :], index[:, :, 0:2]))
                for i in range(TOPK):
                    ins = nc.vector.tensor_tensor(hot[:, i, :, :], expert[:, :, :].to_broadcast([P, NT, E]),
                                                  over_experts(indexf[:, :, i]), ALU.is_equal)
                chain(c, dve, v, ins)
                nc.vector.tensor_tensor(chosen[:, :, :], hot[:, 0], hot[:, 1], ALU.add)\
                  .then_inc(c.s["chosen"], 1)
                chain(c, dve, v, nc.vector.tensor_tensor(total[:, :], top[:, :, 0], top[:, :, 1], ALU.add))
                chain(c, dve, v, nc.vector.reciprocal(total[:, :], total[:, :]))
                for i in range(TOPK):
                    ins = nc.vector.tensor_tensor(indexf[:, :, i], top[:, :, i], total[:, :], ALU.mult)
                chain(c, dve, v, ins)
                for i in range(TOPK):
                    ins = nc.vector.tensor_tensor(hot[:, i], hot[:, i], over_experts(indexf[:, :, i]), ALU.mult)
                chain(c, dve, v, ins)
                nc.vector.tensor_tensor(w[:, :, :], hot[:, 0], hot[:, 1], ALU.add)
                dve.wait_ge(c.s["vbank_full"], n("vb", 2))
                for t in range(NT):
                    at = NT * E + t * E
                    chain(c, dve, v, nc.vector.tensor_tensor(base[:, t + 1, :], base[:, t, :],
                                                             c.vbank[1][:, at:at + E], ALU.add))
                nc.vector.tensor_tensor(rank[:, :, :], base[:, 0:NT, :],
                                        c.vbank[1][:, 0:NT * E].rearrange("p (t e) -> p t e", e=E), ALU.add)\
                  .then_inc(c.s["vbank_empty"], 1)
                dve.wait_ge(c.s["vbank_empty"], n("vb", 2))
                chain(c, dve, v, nc.vector.tensor_copy(base[:, 0, :], base[:, NT, :]))
                chain(c, dve, v, nc.vector.scalar_tensor_tensor(out=w[:, :, :], in0=rank[:, :, :], scalar=float(CAP),
                                                                in1=w[:, :, :], op0=ALU.is_lt, op1=ALU.mult))
                if more:
                    ln_stats(c, dve, n("ln"), c.y[:, b + 1])
                    ln_norm(c, dve, n("ln"), c.y[:, b + 1], n("sb"))
                for e in range(E):
                    for i in range(2):
                        dve.wait_ge(c.s["vbank_full"], n("vb", 2 * e + i + 3))
                        for t in range(2):
                            y = c.y[:, b, 2 * i + t, :]
                            ins = nc.vector.scalar_tensor_tensor(out=y, in0=c.vbank[i][:, t * D:(t + 1) * D],
                                                                 scalar=w[:, 2 * i + t, e:e + 1], in1=y,
                                                                 op0=ALU.mult, op1=ALU.add)
                        ins.then_inc(c.s["vbank_empty"], 1)
                    dve.wait_ge(c.s["vbank_empty"], n("vb", 2 * e + 4))
                dve.wait_ge(c.s["gated"], gated0 + 1 + b)
                nc.vector.tensor_tensor(c.x[:, b], c.x[:, b], tmp, ALU.add).then_inc(c.s["finished"], 1)
            gated0 = B
            loop(c, dve, B, turn)

        @block.scalar
        def _(act):
            act.wait_ge(c.s["load"], loaded)
            g = (lambda k: gains[:, k:k + 1], lambda k: gains[:, 2 + k:3 + k])
            ln_gain(c, act, start["sb"], *g)

            def turn(b, more):
                n = Span(s0, MOE, b)
                act.wait_ge(c.s["logits_shifted"], n("mo", 1))
                nc.scalar.activation(lg[:, :, :], lg[:, :, :], ACT.Exp).then_inc(c.s["logits_exped"], 1)
                for e in range(E):
                    for m in range(KF):
                        act.wait_ge(c.s["sbank_full"], n("sb", KF * e + m + 1))
                        if e >= 2:
                            act.wait_ge(c.s["vbank_full"], n("vb", 2 * e))
                        nc.scalar.activation(gT[:, KF * (e % 2) + m, :], c.sbank[m % 2][:, :],
                                             ACT.Gelu_apprx_tanh).then_inc(c.s["sbank_empty"], 1)
                if more:
                    ln_gain(c, act, n("sb", KF * E), *g)
            loop(c, act, B, turn)

        @block.tensor
        def _(pe):
            pe.wait_ge(c.s["load"], loaded)
            pe.wait_ge(c.s["aux"], 7)
            ln_turn(c, pe, start["ln"], start["sb"])

            def turn(b, more):
                n = Span(s0, MOE, b)
                pe.wait_ge(c.s["sbank_empty"], n("sb"))
                pe.wait_ge(c.s["vbank_empty"], n("vb", -1))
                for t in range(NT):
                    for k in range(KD):
                        ins = nc.tensor.matmul(c.vbank[0][:, t * E:(t + 1) * E], c.hT[:, k, 1 + t * P:1 + (t + 1) * P],
                                               wr[:, k, :], start=(k == 0), stop=(k == KD - 1))
                ins.then_inc(c.s["vbank_full"], 1)

                def up(e):
                    for m in range(KF):
                        pe.wait_ge(c.s["sbank_empty"], n("sb", KF * e + m - 1))
                        for k in range(KD):
                            ins = nc.tensor.matmul(c.sbank[m % 2][:, :], w1[:, e, k, m * P:(m + 1) * P],
                                                   c.hT[:, k, 1:T + 1], start=(k == 0), stop=(k == KD - 1))
                        ins.then_inc(c.s["sbank_full"], 1)

                def down(e):
                    pe.wait_ge(c.s["sbank_empty"], n("sb", KF * (e + 1)))
                    for i in range(2):
                        pe.wait_ge(c.s["vbank_empty"], n("vb", 2 * e + 1 + i))
                        for t in range(2 * i, 2 * i + 2):
                            for k in range(KF):
                                ins = nc.tensor.matmul(c.vbank[i][:, (t % 2) * D:(t % 2 + 1) * D],
                                                       gT[:, KF * (e % 2) + k, t * P:(t + 1) * P], w2[:, e, k, :],
                                                       start=(k == 0), stop=(k == KF - 1))
                        ins.then_inc(c.s["vbank_full"], 1)

                up(0)
                pe.wait_ge(c.s["chosen"], n("mo", 1))
                pe.wait_ge(c.s["vbank_empty"], n("vb", 0))
                for i, m in enumerate((tri, ones)):
                    ins = nc.tensor.matmul(c.vbank[1][:, i * NT * E:(i + 1) * NT * E], m[:, :],
                                           chosen[:, :, :].rearrange("p t e -> p (t e)"), start=True, stop=True)
                ins.then_inc(c.s["vbank_full"], 1)
                for e in range(1, E):
                    up(e)
                    down(e - 1)
                if more:
                    ln_turn(c, pe, n("ln"), n("sb", KF * E))
                down(E - 1)
            loop(c, pe, B, turn)


def build(nc, d, outs):
    with ExitStack() as st:
        c = Chip()
        c.nc = nc
        c.s = {name: st.enter_context(nc.semaphore(name)) for name in SEMS}

        def sb(name, shape, dt=F32):
            return st.enter_context(nc.sbuf_tensor(name, shape, dt))

        def pair(name):
            return [st.enter_context(nc.psum_tensor(f"{name}{i}", [P, T], F32)) for i in range(2)]

        c.x = sb("x", [P, B, NT, D])
        c.y = sb("y", [P, B, NT, D])
        c.hT = sb("hT", [P, KD, T + 1])
        c.xn = sb("xn", [P, NT, D])
        c.ident = sb("ident", [P, P])
        c.modT = sb("modT", [P, 4, KD, B])
        c.bn = sb("bn", [P, NT, 6])
        c.mv = sb("mv", [P, NT, 2])
        c.ve = sb("ve", [P, NT])
        c.rstd = sb("rstd", [P, NT])
        c.mhalf = sb("mhalf", [P, NT])
        c.score = sb("score", [P, 4, T])
        c.prob = sb("prob", [P, 8, T])
        c.probT = sb("probT", [P, 8, T])
        c.least = sb("least", [P, 8])
        c.psum_of = sb("psum_of", [P, 8])
        c.rsum = sb("rsum", [P, 8])
        c.vbank, c.pbank, c.sbank, c.obank = pair("vbank"), pair("pbank"), pair("sbank"), pair("obank")
        c.mod_dram = nc.dram_tensor("modulation", (2, B, 6 * D), F32).ap()
        c.loaded = 64
        opening(c, d)
        n = layer0(c, d, dict(OPENING))
        n = remix(c, d, n, None, "ca", "sa")
        n = layer1(c, d, n)
        n = remix(c, d, n, "ga", "cb", "sb")
        n = cross(c, d, n)
        moe(c, d, n, outs[0])


def kernel(**inputs):
    import numpy as np
    import concourse.bacc as bacc
    from concourse.bass_utils import run_bass_kernel_spmd

    inputs = {k: np.asarray(v) for k, v in inputs.items()}
    arrays = {"x": inputs["L0_attn_x"]}
    for short, name in (("qw", "q_w"), ("kw", "k_w"), ("vw", "v_w"), ("ow", "o_w")):
        arrays[short] = inputs[f"L0_attn_{name}"]
    for l in range(2):
        arrays[f"c{l}"] = inputs[f"L{l}_c"].T
        arrays[f"wmod{l}"] = inputs[f"L{l}_wmod"]
    for short, name in (("Wr", "W_r"), ("Wk", "W_k"), ("Wv", "W_v")):
        arrays[short] = inputs[f"L0_ffn_{name}"].T
    for name in ("mu_r", "mu_k"):
        arrays[name] = inputs[f"L0_ffn_{name}"].reshape(KD, P).T
    for short, name in (("Aq", "Wq"), ("Ak", "Wk"), ("Ao", "Wo"), ("W1", "W1"), ("W2", "W2"), ("bo", "bo"), ("b2", "b2")):
        arrays[short] = inputs[f"L1_attn_{name}"]
    wide = [inputs[f"L1_attn_{name}"] for name in ("Wq", "Wk", "Wv")]
    arrays["wtok"] = np.concatenate([wide[0][:, :, P:], wide[1][:, :, P:], wide[2]], axis=2)
    by_feature = [inputs[f"L1_attn_{name}"].reshape(DEPTH, -1, P) for name in ("ln1_g", "ln1_b", "ln2_g", "ln2_b", "b1")]
    arrays["vec"] = np.concatenate(by_feature, axis=1).transpose(2, 0, 1)
    for short, name in (("wqkv", "qkv_weight"), ("wproj", "proj_weight")):
        arrays[short] = inputs[f"L1_ffn_{name}"].T
    for short, ln in (("cross_ln", "ln1"), ("moe_ln", "ln2")):
        both = [inputs[f"L1_ffn_{ln}_{name}"].reshape(KD, P) for name in ("weight", "bias")]
        arrays[short] = np.concatenate(both).T
    for short, name in (("wrouter", "router_weight"), ("we1", "moe_w1"), ("we2", "moe_w2")):
        arrays[short] = inputs[f"L1_ffn_{name}"]
    arrays = {k: np.ascontiguousarray(v) for k, v in arrays.items()}
    nc = bacc.Bacc("TRN2", target_bir_lowering=False, num_devices=1)
    d = {k: nc.dram_tensor(f"in_{k}", v.shape, mybir.dt.from_np(v.dtype), kind="ExternalInput").ap()
         for k, v in arrays.items()}
    out = nc.dram_tensor("out_x", (B, T, D), F32, kind="ExternalOutput").ap()
    build(nc, d, [out])
    r = run_bass_kernel_spmd(nc, [{f"in_{k}": v for k, v in arrays.items()}], core_ids=[0])
    return r.results[0]["out_x"]
```

```python
from contextlib import ExitStack

import concourse.bass as bass
from concourse import mybir

F32 = mybir.dt.float32
U32 = mybir.dt.uint32
ALU = mybir.AluOpType
ACT = mybir.ActivationFunctionType
AX = mybir.AxisListType

P = 128
B = 8
T = 512
NT = T // P
D = 256
KD = D // P
EPS = 1e-5
BIG = 1e30
GATE_MIN = 0.25
H0, HD0 = 16, 16
DEPTH = 4
H1, HD1 = 8, 32
BUCKET = 64
NU = T // BUCKET
FF = 4 * D
MF = FF // P
NH, NKV, E, TOPK = 16, 4, 8, 2
HDM = D // NH
QKV = NKV * (NH // NKV + 2) * HDM
FM = 512
CAP = -(-(B * T * TOPK * 5) // (E * 4))
SEMS = ("load aux store resid_ready mod_ready vbank_full vbank_empty pbank_full pbank_empty sbank_full "
        "sbank_empty obank_full obank_empty stats_ready rstd_ready normed_ready scores_exped "
        "sums_inverted q_ready probs_ready diff_ready mixed_ready squared_ready v_chain p_chain settled "
        "attn_weights mlp_weights attn_biased mlp_biased mlp_full mlp_added lin_turned lin_qT_ready "
        "lin_shifted lin_exped lin_inverted lin_q_ready lin_k_ready context_ready lin_full gated "
        "products_ready products_used cross_shifted cross_exped cross_probs logits_shifted logits_exped "
        "chosen finished stored expert_weights0 expert_weights1 rows_ready scattered0 scattered1 "
        "scattered2 scattered3 chunk_in0 chunk_in1 result_stored rows_copied gathered0 gathered1 cleared "
        "normed_free result_free").split()


class Span:

    def __init__(self, start, turn, i):
        self.start, self.turn, self.i = start, turn, i

    def __call__(self, name, k=0):
        return self.start.get(name, 0) + self.i * self.turn.get(name, 0) + k


def after(start, turn, n):
    return {k: start.get(k, 0) + n * turn.get(k, 0) for k in {*start, *turn}}


class Chip:
    pass


def alone(c, eng):
    eng.sem_inc(c.s["settled"], 1)


def chain(c, eng, sem, ins):
    ins.then_inc(sem, 1)
    eng.wait_ge(sem, 1)
    eng.sem_clear(sem)



def ln_stats(c, dve, n, src):
    nc = c.nc
    dve.wait_ge(c.s["normed_ready"], n)
    alone(c, dve)
    for t in range(NT):
        ins = nc.vector.bn_stats(c.bn[:, t, :], src[:, t, :])
    chain(c, dve, c.s["v_chain"], ins)
    for t in range(NT):
        ins = nc.vector.bn_aggr(c.mv[:, t, :], c.bn[:, t, :])
    ins.then_inc(c.s["stats_ready"], 1)


def ln_rstd(c, pool, n):
    nc = c.nc
    pool.wait_ge(c.s["stats_ready"], n + 1)
    alone(c, pool)
    chain(c, pool, c.s["p_chain"], nc.gpsimd.tensor_scalar(c.ve[:, :], c.mv[:, :, 1], EPS, None, ALU.add))
    nc.gpsimd.tensor_tensor(c.rstd[:, :], c.ve[:, :], c.mhalf[:, :], ALU.pow).then_inc(c.s["rstd_ready"], 1)


def ln_norm(c, dve, n, src, sbank_before, dst=None):
    nc = c.nc
    dve.wait_ge(c.s["rstd_ready"], n + 1)
    if dst is None:
        dst = c.xn
        dve.wait_ge(c.s["sbank_full"], sbank_before)
    for t in range(NT):
        ins = nc.vector.tensor_scalar(dst[:, t, :], src[:, t, :], c.mv[:, t, 0:1], c.rstd[:, t:t + 1],
                                      ALU.subtract, ALU.mult)
    ins.then_inc(c.s["normed_ready"], 1)


def ln_turn(c, pe, n, sb):
    nc = c.nc
    pe.wait_ge(c.s["normed_ready"], n + 1)
    for half in range(KD):
        pe.wait_ge(c.s["sbank_empty"], sb + half - 1)
        for t in range(NT):
            ins = nc.tensor.transpose(c.sbank[half][:, t * P:(t + 1) * P], c.xn[:, t, half * P:(half + 1) * P],
                                      c.ident[:, :])
        ins.then_inc(c.s["sbank_full"], 1)


def ln_gain(c, act, sb, gain, shift, dst=None):
    nc = c.nc
    dst = c.hT if dst is None else dst
    for half in range(KD):
        act.wait_ge(c.s["sbank_full"], sb + half + 1)
        alone(c, act)
        nc.scalar.activation(dst[:, half, 1:T + 1], c.sbank[half][:, :], ACT.Identity, bias=shift(half),
                             scale=gain(half)).then_inc(c.s["sbank_empty"], 1)



LAG_N, LAG_T, LAG_PT, LAG_AV = 5, 8, 9, 10


class Heads:

    def __init__(self, quads, q_of, k_of, keys_of, mask_of, v_of, out_of, vb, opens=lambda q: True,
                 closes=lambda q: True, q_needed=lambda q, j: None):
        self.quads, self.q_of, self.k_of, self.keys_of = quads, q_of, k_of, keys_of
        self.mask_of, self.v_of, self.out_of, self.vb = mask_of, v_of, out_of, vb
        self.opens, self.closes, self.q_needed = opens, closes, q_needed
        self.items = 4 * quads
        self.steps = self.items + LAG_AV + 4


def heads_pe(c, pe, n, h, mid):
    nc = c.nc

    def score(k):
        q, j = divmod(k, 4)
        keys = h.keys_of(q)
        needed = h.q_needed(q, j)
        if needed is not None:
            pe.wait_ge(c.s["q_ready"], n("qr", needed))
        pe.wait_ge(c.s["vbank_empty"], n("vb", h.vb + k - 1))
        nc.tensor.matmul(c.vbank[k % 2][:, 0:P * len(keys)], h.q_of(q, j), h.k_of(q, j, keys[0], keys[-1] + 1),
                         start=True, stop=True).then_inc(c.s["vbank_full"], 1)

    def turn(k):
        q, j = divmod(k, 4)
        if k >= 2:
            pe.wait_ge(c.s["pbank_empty"], n("pb", k - 1))
        pe.wait_ge(c.s["probs_ready"], n("pb", k + 1))
        for m in range(len(h.keys_of(q))):
            ins = nc.tensor.transpose(c.pbank[k % 2][:, m * P:(m + 1) * P], c.prob[:, k % 8, m * P:(m + 1) * P],
                                      c.ident[:, :])
        ins.then_inc(c.s["pbank_full"], 1)

    def values(q):
        pe.wait_ge(c.s["pbank_empty"], n("pb", 4 * q + 4))
        keys = h.keys_of(q)
        bank, cols = h.out_of(q)
        for m, key in enumerate(keys):
            for j in range(4):
                ins = nc.tensor.matmul(bank[32 * j:32 * j + 32, cols], h.v_of(q, j, key),
                                       c.probT[:, (4 * q + j) % 8, m * P:(m + 1) * P],
                                       start=(m == 0 and h.opens(q)), stop=(m == len(keys) - 1 and h.closes(q)),
                                       tile_position=(0, 32 * j))
        ins.then_inc(c.s["obank_full"], 1)

    for t in range(h.steps):
        if t < h.items:
            score(t)
        if 0 <= t - LAG_T < h.items:
            turn(t - LAG_T)
        q, r = divmod(t - LAG_AV - 3, 4)
        if r == 0 and 0 <= q < h.quads:
            values(q)
        mid(t)


def heads_dve(c, dve, n, h, mid):
    nc = c.nc
    for t in range(h.steps):
        k = t - LAG_PT
        if 0 <= k < h.items:
            q = k // 4
            width = P * len(h.keys_of(q))
            dve.wait_ge(c.s["pbank_full"], n("pb", k + 1))
            if q >= 2:
                dve.wait_ge(c.s["obank_full"], n("av", q - 1))
            nc.vector.tensor_copy(c.probT[:, k % 8, 0:width], c.pbank[k % 2][:, 0:width])\
              .then_inc(c.s["pbank_empty"], 1)
        if t < h.items:
            q, j = divmod(t, 4)
            width = P * len(h.keys_of(q))
            if t >= 4:
                dve.wait_ge(c.s["scores_exped"], n("pb", t - 3))
            dve.wait_ge(c.s["vbank_full"], n("vb", h.vb + t + 1))
            alone(c, dve)
            nc.vector.tensor_tensor_reduce(out=c.score[:, t % 4, 0:width], in0=c.vbank[t % 2][:, 0:width],
                                           in1=h.mask_of(q, j), scale=1.0, scalar=3e38, op0=ALU.add, op1=ALU.min,
                                           accum_out=c.least[:, t % 8:t % 8 + 1]).then_inc(c.s["vbank_empty"], 1)
        q, r = divmod(t - LAG_N, 4)
        if r == 0 and 0 <= q < h.quads:
            dve.wait_ge(c.s["scores_exped"], n("pb", 4 * q + 4))
            lo = 4 * (q % 2)
            nc.vector.reciprocal(c.rsum[:, lo:lo + 4], c.psum_of[:, lo:lo + 4]).then_inc(c.s["sums_inverted"], 1)
        mid(t)


def heads_pool(c, pool, n, h, mid):
    nc = c.nc
    for q in range(h.quads):
        width = P * len(h.keys_of(q))
        pool.wait_ge(c.s["sums_inverted"], n("av", q + 1))
        for lo in (4 * (q % 2), 4 * (q % 2) + 2):
            two = c.prob[:, lo:lo + 2, 0:width]
            nc.gpsimd.tensor_tensor(two, two, c.rsum[:, lo:lo + 2].unsqueeze(2).to_broadcast([P, 2, width]), ALU.mult)\
              .then_inc(c.s["probs_ready"], 2)
        mid(q)


def heads_act(c, act, n, h, mid):
    nc = c.nc
    for k in range(h.items):
        q, j = divmod(k, 4)
        width = P * len(h.keys_of(q))
        if k >= 8:
            act.wait_ge(c.s["pbank_full"], n("pb", k - 7))
        act.wait_ge(c.s["vbank_empty"], n("vb", h.vb + k + 1))
        nc.scalar.activation(c.prob[:, k % 8, 0:width], c.score[:, k % 4, 0:width], ACT.Exp,
                             bias=c.least[:, k % 8:k % 8 + 1], scale=-1.0,
                             accum_out=c.psum_of[:, k % 8:k % 8 + 1]).then_inc(c.s["scores_exped"], 1)
        mid(k)


def nothing(t):
    pass


def loop(c, eng, n, body):
    alone(c, eng)
    with eng.Fori(0, n - 1) as i:
        body(i, True)
    body(n - 1, False)


def grouped(c, eng, n, size, body):
    def group(i, more):
        for z in range(size):
            body(size * i + z, z, more or z < size - 1)
    loop(c, eng, n // size, group)



CHUNK = {"sa": 0, "ca": 1, "ga": 2, "sb": 3, "cb": 4, "gb": 5}
BEGIN = {"vb": 2, "sb": 2, "ln": 1}
OPENING = {"vb": BEGIN["vb"] + 8, "sb": BEGIN["sb"], "ln": BEGIN["ln"]}


def opening(c, d):
    nc = c.nc
    with ExitStack() as st:
        def sb(name, shape, dt=F32):
            return st.enter_context(nc.sbuf_tensor(name, shape, dt))

        cT = sb("cT", [P, 2, KD, B])
        wm = sb("wm", [P, 2, KD, 6 * D])
        rows = sb("rows", [B, 2, 6 * D])
        sign = sb("sign", [B, D])
        ones = sb("ones", [P, P])
        block = st.enter_context(nc.Block())

        @block.sync
        def _(sp):
            for name, count in (("vbank_full", BEGIN["vb"]), ("vbank_empty", BEGIN["vb"]), ("sbank_full", BEGIN["sb"]),
                                ("sbank_empty", BEGIN["sb"]), ("stats_ready", BEGIN["ln"]), ("rstd_ready", BEGIN["ln"]),
                                ("normed_ready", BEGIN["ln"])):
                sp.sem_inc(c.s[name], count)
            for l in range(2):
                sp.dma_start(cT[:, l, :, :], d[f"c{l}"].rearrange("(k p) b -> p k b", p=P)).then_inc(c.s["load"], 16)
                sp.dma_start(wm[:, l, :, :], d[f"wmod{l}"].rearrange("(k p) n -> p k n", p=P))\
                  .then_inc(c.s["load"], 16)
            for b in range(B):
                sp.dma_start(c.x[:, b, :, :], d["x"][b].rearrange("(t p) n -> p t n", p=P))\
                  .then_inc(c.s["resid_ready"], 16)
            sp.wait_ge(c.s["mod_ready"], 2)
            sp.dma_start(c.mod_dram.rearrange("l b n -> b l n"), rows[:, :, :]).then_inc(c.s["store"], 16)
            sp.wait_ge(c.s["store"], 16)
            sp.wait_ge(c.s["resid_ready"], 16 * B)

        @block.scalar
        def _(act):
            act.wait_ge(c.s["load"], 64)
            nc.scalar.activation(cT[:, :, :, :], cT[:, :, :, :], ACT.Silu).then_inc(c.s["aux"], 1)

        @block.gpsimd
        def _(pool):
            nc.gpsimd.memset(c.mhalf[:, :], -0.5)
            chain(c, pool, c.s["p_chain"], nc.gpsimd.memset(ones[:, :], 1.0))
            nc.gpsimd.affine_select(out=c.ident[:, :], in_=ones[:, :], compare_op=ALU.is_equal, fill=0.0, base=0,
                                    pattern=[[-1, P]], channel_multiplier=1).then_inc(c.s["aux"], 1)

        @block.tensor
        def _(pe):
            pe.wait_ge(c.s["aux"], 2)
            n = BEGIN["vb"]
            for l in range(2):
                for m in range(3):
                    pe.wait_ge(c.s["vbank_empty"], n - 1)
                    for k in range(KD):
                        ins = nc.tensor.matmul(c.vbank[n % 2][0:B, :], cT[:, l, k, :], wm[:, l, k, m * T:(m + 1) * T],
                                               start=(k == 0), stop=(k == KD - 1))
                    ins.then_inc(c.s["vbank_full"], 1)
                    n += 1
            pe.wait_ge(c.s["mod_ready"], 2)
            for pair in (("sa", "ca"), ("sb", "cb")):
                pe.wait_ge(c.s["vbank_empty"], n - 1)
                for i, name in enumerate(pair):
                    for k in range(KD):
                        at = CHUNK[name] * D + k * P
                        ins = nc.tensor.transpose(c.vbank[n % 2][:, (i * KD + k) * B:(i * KD + k + 1) * B],
                                                  rows[:, 0, at:at + P], c.ident[0:B, 0:B])
                ins.then_inc(c.s["vbank_full"], 1)
                n += 1

        @block.vector
        def _(dve):
            n = BEGIN["vb"]
            for l in range(2):
                for m in range(3):
                    dve.wait_ge(c.s["vbank_full"], n + 1)
                    ins = nc.vector.tensor_copy(rows[:, l, m * T:(m + 1) * T], c.vbank[n % 2][0:B, :])
                    ins.then_inc(c.s["vbank_empty"], 1)
                    n += 1
                dve.wait_ge(c.s["vbank_empty"], n)
                for name in ("ca", "cb"):
                    at = CHUNK[name] * D
                    v = rows[:, l, at:at + D]
                    chain(c, dve, c.s["v_chain"], nc.vector.tensor_scalar(v, v, 1.0, None, ALU.add))
                for name in ("ga", "gb"):
                    at = CHUNK[name] * D
                    v = rows[:, l, at:at + D]
                    chain(c, dve, c.s["v_chain"], nc.vector.tensor_scalar(sign[:, :], v, 0.0, 2.0, ALU.is_ge, ALU.mult))
                    chain(c, dve, c.s["v_chain"], nc.vector.tensor_scalar(sign[:, :], sign[:, :], -1.0, None, ALU.add))
                    chain(c, dve, c.s["v_chain"], nc.vector.tensor_tensor(v, v, sign[:, :], ALU.mult))
                    ins = nc.vector.scalar_tensor_tensor(out=v, in0=v, scalar=GATE_MIN, in1=sign[:, :], op0=ALU.max,
                                                         op1=ALU.mult)
                    if name == "gb":
                        ins.then_inc(c.s["mod_ready"], 1)
                        dve.wait_ge(c.s["mod_ready"], l + 1)
                    else:
                        chain(c, dve, c.s["v_chain"], ins)
            for i in range(2):
                dve.wait_ge(c.s["vbank_full"], n + 1)
                nc.vector.tensor_copy(c.modT[:, 2 * i:2 * i + 2, :, :],
                                      c.vbank[n % 2][:, 0:2 * KD * B].rearrange("p (i k b) -> p i k b", k=KD, b=B))\
                  .then_inc(c.s["vbank_empty"], 1)
                n += 1
            dve.wait_ge(c.s["vbank_empty"], n)


def mod_rows(c, l, name):
    at = CHUNK[name] * D
    return c.mod_dram[l, :, at:at + D].partition_broadcast(P)



PROJ0 = {"vb": KD + 2, "sb": KD}
HEADS0 = {"vb": 4 * 16 + 2, "sb": 2, "pb": 64, "av": 16, "ob": KD, "ln": 1, "qr": H0}
ATTN0 = after(HEADS0, PROJ0, 1)
FFN0 = {"vb": 2, "sb": 6, "ln": 1, "mx": 1}


def one(ap, i):
    return ap[:, i:i + 1] if isinstance(i, int) else ap[:, bass.ds(i, 1)]


def layer0(c, d, start):
    nc = c.nc
    with ExitStack() as st:
        def sb(name, shape, dt=F32):
            return st.enter_context(nc.sbuf_tensor(name, shape, dt))

        gates = sb("gates0", [P, 2, B, D])
        wqkv = sb("wqkv0", [P, 3, KD, D])
        wo = sb("wo0", [P, KD, D])
        wf = sb("wf0", [P, 3, KD, D])
        mu = sb("mu0", [P, 2, KD])
        scale = sb("scale0", [P, H0 // KD])
        qT = sb("qT0", [P, H0, T])
        kT = sb("kT0", [P, KD, T])
        vt = sb("vt0", [P, NT, H0 // 2, 2, 32])
        aoT = sb("aoT0", [P, KD, T])
        mixT = qT[:, 0:2 * KD, :].rearrange("p (i k) t -> p i k t", k=KD)
        diff = qT[:, 2 * KD:3 * KD, :]
        krelu, kact = qT[:, 4 * KD:5 * KD, :], qT[:, 5 * KD:6 * KD, :]
        rsig = qT[:, 6 * KD:7 * KD, :].rearrange("p i (t n) -> p (i t) n", n=D)
        slope_mask = c.y[:, :, :, :].rearrange("p (h b) t n -> p h (b t n)", h=2)\
            .rearrange("p h (i n) -> p (h i) n", n=T)
        tmp = sb("tmp0", [P, 2, D])
        norm = after(start, {"sb": 2, "ln": 1}, 1)
        s0 = after(after(norm, PROJ0, 1), {"qr": 4}, 1)
        s1 = after(after(after(s0, ATTN0, B - 1), HEADS0, 1), {"qr": -4}, 1)
        end = after(after(s1, FFN0, B), {"sb": -2, "ln": -1}, 1)

        block = st.enter_context(nc.Block())

        def mod(i, b):
            return lambda k: one(c.modT[:, i, k, :], b)

        def head(s, j):
            return 8 * (s // 2) + 2 * j + s % 2

        def place(q):
            return 2 * (q // 8) + q % 2, (q % 8) // 2

        def of(f):
            return lambda q, *rest: f(*place(q), *rest)

        h = Heads(
            quads=H0,
            q_of=of(lambda s, tile, j: qT[:, head(s, j), tile * P:(tile + 1) * P]),
            k_of=of(lambda s, tile, j, lo, hi: kT[:, s // 2, lo * P:hi * P]),
            keys_of=of(lambda s, tile: list(range(tile + 1))),
            mask_of=of(lambda s, tile, j: slope_mask[:, head(s, j), (3 - tile) * P:T]),
            v_of=of(lambda s, tile, j, key: vt[:, key, head(s, j) // 2, s % 2, :]),
            out_of=of(lambda s, tile: (c.obank[s // 2], slice(tile * P, (tile + 1) * P))),
            vb=0,
            opens=lambda q: q % 2 == 0,
            closes=lambda q: q % 2 == 1,
            q_needed=of(lambda s, tile, j: 4 * (s - 1) + j + 1 if tile == 0 else None))
        L = c.loaded

        @block.sync
        def _(sp):
            for i, name in enumerate(("qw", "kw", "vw")):
                sp.dma_start(wqkv[:, i, :, :], d[name].rearrange("(k p) n -> p k n", p=P)).then_inc(c.s["load"], 16)
            sp.dma_start(wo[:, :, :], d["ow"].rearrange("(k p) n -> p k n", p=P)).then_inc(c.s["load"], 16)
            for i, name in enumerate(("Wr", "Wk", "Wv")):
                sp.dma_start(wf[:, i, :, :], d[name].rearrange("(k p) n -> p k n", p=P)).then_inc(c.s["load"], 16)
            for i, name in enumerate(("mu_r", "mu_k")):
                sp.dma_start(mu[:, i, :], d[name]).then_inc(c.s["load"], 16)
            for i, name in enumerate(("ga", "gb")):
                sp.dma_start(gates[:, i, :, :], mod_rows(c, 0, name)).then_inc(c.s["load"], 16)
        loaded0 = L + 11 * 16

        @block.gpsimd
        def _(pool):
            nc.gpsimd.memset(vt[:, :, :, :, :], 0.0)
            nc.gpsimd.memset(c.hT[:, :, 0:1], 0.0)
            chain(c, pool, c.s["p_chain"], nc.gpsimd.memset(scale[:, :], -float(HD0) ** -0.5))
            for base, step in ((0, 1), (HD0 - 1, -1)):
                ins = nc.gpsimd.affine_select(out=scale[:, :], in_=scale[:, :], compare_op=ALU.is_ge, fill=0.0,
                                              base=base, pattern=[[-HD0 * step, H0 // KD]], channel_multiplier=step)
                if step == 1:
                    chain(c, pool, c.s["p_chain"], ins)
            ins.then_inc(c.s["aux"], 1)
            ln_rstd(c, pool, start["ln"])
            dist = slope_mask[:, H0 - 1, :]
            chain(c, pool, c.s["p_chain"], nc.gpsimd.iota(dist, pattern=[[-1, T]], base=T - P, channel_multiplier=1,
                                                          allow_small_or_imprecise_dtypes=True))
            chain(c, pool, c.s["p_chain"], nc.gpsimd.affine_select(out=dist, in_=dist, compare_op=ALU.is_ge, fill=BIG,
                                                                   base=T - P, pattern=[[-1, T]],
                                                                   channel_multiplier=1))
            for i in range(H0):
                slope = float((2.0 ** (-8.0 / H0)) ** (i + 1))
                ins = nc.gpsimd.tensor_scalar(slope_mask[:, i, :], dist, slope, None, ALU.mult)
            ins.then_inc(c.s["aux"], 1)

            def attn(b, more):
                n = Span(s0, ATTN0, b)

                def mid(q):
                    if q == 2:
                        ln_rstd(c, pool, n("ln"))
                heads_pool(c, pool, n, h, mid)
            loop(c, pool, B, attn)
            pool.wait_ge(c.s["vbank_full"], s1["vb"])

            def differ(n, sb):
                pool.wait_ge(c.s["sbank_empty"], n("sb", sb))
                nc.gpsimd.tensor_tensor(diff, c.hT[:, :, 1:T + 1], c.hT[:, :, 0:T], ALU.subtract)\
                  .then_inc(c.s["diff_ready"], 1)
            differ(Span(s1, FFN0, 0), 0)

            def ffn(b, more):
                n = Span(s1, FFN0, b)
                if more:
                    ln_rstd(c, pool, n("ln"))
                pool.wait_ge(c.s["sbank_empty"], n("sb", 2))
                for k in range(KD):
                    ins = nc.gpsimd.tensor_tensor(kact[:, k, :], krelu[:, k, :], krelu[:, k, :], ALU.mult)
                ins.then_inc(c.s["squared_ready"], 1)
                if more:
                    differ(n, 6)
            loop(c, pool, B, ffn)

        @block.vector
        def _(dve):
            ln_stats(c, dve, start["ln"], c.x[:, 0])
            ln_norm(c, dve, start["ln"], c.x[:, 0], start["sb"])
            dve.wait_ge(c.s["load"], loaded0)
            dve.wait_ge(c.s["aux"], 4)

            def keys_out(n, k, vb):
                dve.wait_ge(c.s["vbank_full"], n("vb", vb + k + 1))
                nc.vector.tensor_copy(kT[:, k, :], c.vbank[k][:, :]).then_inc(c.s["vbank_empty"], 1)

            def values_out(n, vb):
                for i in range(2):
                    dve.wait_ge(c.s["vbank_full"], n("vb", vb + i + 1))
                    for odd in range(2):
                        src = c.vbank[i][:, :].rearrange("p (t h z e) -> p t h z e", t=2, z=2, e=HD0)
                        ins = nc.vector.tensor_copy(vt[:, 2 * i:2 * i + 2, :, odd, HD0 * odd:HD0 * odd + HD0],
                                                    src[:, :, :, odd, :])
                    ins.then_inc(c.s["vbank_empty"], 1)

            first = Span(norm, PROJ0, 0)
            for k in range(KD):
                keys_out(first, k, 0)
            values_out(first, KD)

            def attn(b, more):
                n = Span(s0, ATTN0, b)

                def mid(t):
                    nxt = c.x[:, b + 1] if more else c.x[:, 0]
                    if t == 16:
                        ln_stats(c, dve, n("ln"), nxt)
                    if t == 20:
                        ln_norm(c, dve, n("ln"), nxt, n("sb"))
                    if more and t in (66, 68):
                        keys_out(n, (t - 66) // 2, 64)
                heads_dve(c, dve, n, h, mid)
                if more:
                    dve.wait_ge(c.s["obank_full"], n("av", 16))
                    values_out(n, 66)
                out = 68 if more else 64
                for i in range(2):
                    dve.wait_ge(c.s["vbank_full"], n("vb", out + 1 + i))
                    gate = one_row(gates[:, 0], b)
                    chain(c, dve, c.s["v_chain"],
                          nc.vector.tensor_tensor(tmp[:, :, :], c.vbank[i][:, :].rearrange("p (t n) -> p t n", t=2),
                                                  gate, ALU.mult))
                    xs = c.x[:, b, 2 * i:2 * i + 2, :]
                    nc.vector.tensor_tensor(xs, xs, tmp[:, :, :], ALU.add).then_inc(c.s["vbank_empty"], 1)
                    dve.wait_ge(c.s["vbank_empty"], n("vb", out + 1 + i))
            loop(c, dve, B, attn)

            def mix(count):
                dve.wait_ge(c.s["diff_ready"], count)
                alone(c, dve)
                for i in range(2):
                    for k in range(KD):
                        ins = nc.vector.scalar_tensor_tensor(out=mixT[:, i, k, :], in0=diff[:, k, :],
                                                             scalar=mu[:, i, k:k + 1], in1=c.hT[:, k, 0:T],
                                                             op0=ALU.mult, op1=ALU.add)
                ins.then_inc(c.s["mixed_ready"], 1)
            mix(1)

            def ffn(b, more):
                n = Span(s1, FFN0, b)
                if more:
                    ln_stats(c, dve, n("ln"), c.x[:, b + 1])
                    ln_norm(c, dve, n("ln"), c.x[:, b + 1], n("sb"))
                    mix(n("mx", 2))
                dve.wait_ge(c.s["sbank_empty"], n("sb", 4))
                for i in range(2):
                    dve.wait_ge(c.s["vbank_full"], n("vb", 1 + i))
                    chain(c, dve, c.s["v_chain"],
                          nc.vector.tensor_tensor(tmp[:, :, :], c.vbank[i][:, :].rearrange("p (t n) -> p t n", t=2),
                                                  rsig[:, 2 * i:2 * i + 2, :], ALU.mult))
                    chain(c, dve, c.s["v_chain"], nc.vector.tensor_tensor(tmp[:, :, :], tmp[:, :, :],
                                                                          one_row(gates[:, 1], b), ALU.mult))
                    xs = c.x[:, b, 2 * i:2 * i + 2, :]
                    nc.vector.tensor_tensor(xs, xs, tmp[:, :, :], ALU.add).then_inc(c.s["vbank_empty"], 1)
                    dve.wait_ge(c.s["vbank_empty"], n("vb", 1 + i))
            loop(c, dve, B, ffn)

        @block.scalar
        def _(act):
            ln_gain(c, act, start["sb"], mod(1, 0), mod(0, 0))

            def q_out(k, full):
                hd = head(k // 4, k % 4)
                if k % 8 == 0:
                    act.wait_ge(c.s["sbank_full"], full)
                    alone(c, act)
                nc.scalar.activation(qT[:, hd, :], c.sbank[k // 8][:, :], ACT.Identity,
                                     scale=scale[:, hd % 8:hd % 8 + 1]).then_inc(c.s["q_ready"], 1)

            for k in range(4):
                q_out(k, norm["sb"] + 1)

            def attn(b, more):
                n = Span(s0, ATTN0, b)

                def out(g):
                    act.wait_ge(c.s["obank_full"], n("av", 8 * g + 8))
                    nc.scalar.copy(aoT[:, g, :], c.obank[g][:, :]).then_inc(c.s["obank_empty"], 1)

                def mid(k):
                    if k < 12:
                        q_out(k + 4, n("sb"))
                        if k + 4 in (7, 15):
                            act.wait_ge(c.s["q_ready"], n("qr", k + 1))
                            act.sem_inc(c.s["sbank_empty"], 1)
                    if k == 48:
                        out(0)
                    if k == 44:
                        if more:
                            ln_gain(c, act, n("sb"), mod(1, b + 1), mod(0, b + 1))
                        else:
                            ln_gain(c, act, n("sb"), mod(3, 0), mod(2, 0))
                heads_act(c, act, n, h, mid)
                if more:
                    for k in range(4):
                        q_out(k, n("sb", 3))
                out(1)
            loop(c, act, B, attn)

            def ffn(b, more):
                n = Span(s1, FFN0, b)
                for i in range(KD):
                    act.wait_ge(c.s["sbank_full"], n("sb", 1 + i))
                    nc.scalar.activation(krelu[:, i, :], c.sbank[i][:, :], ACT.Relu).then_inc(c.s["sbank_empty"], 1)
                act.wait_ge(c.s["vbank_empty"], n("vb"))
                alone(c, act)
                for i in range(2):
                    act.wait_ge(c.s["sbank_full"], n("sb", 3 + i))
                    nc.scalar.activation(rsig[:, 2 * i:2 * i + 2, :],
                                         c.sbank[i][:, :].rearrange("p (t n) -> p t n", t=2),
                                         ACT.Sigmoid).then_inc(c.s["sbank_empty"], 1)
                if more:
                    ln_gain(c, act, n("sb", 4), mod(3, b + 1), mod(2, b + 1))
            loop(c, act, B, ffn)

        @block.tensor
        def _(pe):
            ln_turn(c, pe, start["ln"], start["sb"])
            pe.wait_ge(c.s["load"], loaded0)

            def queries_and_keys(n, g, sb, vb):
                for i, (bank, full, empty, job) in enumerate(
                        ((c.sbank, "sbank_full", "sbank_empty", n("sb", sb)),
                         (c.vbank, "vbank_full", "vbank_empty", n("vb", vb)))):
                    pe.wait_ge(c.s[empty], job + g - 1)
                    for k in range(KD):
                        ins = nc.tensor.matmul(bank[g][:, :], wqkv[:, i, k, g * P:(g + 1) * P],
                                               c.hT[:, k, 1:T + 1], start=(k == 0), stop=(k == KD - 1))
                    ins.then_inc(c.s[full], 1)

            def values(n, i, vb):
                pe.wait_ge(c.s["vbank_empty"], n("vb", vb + i - 1))
                for t in range(2 * i, 2 * i + 2):
                    for k in range(KD):
                        ins = nc.tensor.matmul(c.vbank[i][:, (t % 2) * D:(t % 2 + 1) * D],
                                               c.hT[:, k, 1 + t * P:1 + (t + 1) * P], wqkv[:, 2, k, :],
                                               start=(k == 0), stop=(k == KD - 1))
                ins.then_inc(c.s["vbank_full"], 1)

            first = Span(norm, PROJ0, 0)
            pe.wait_ge(c.s["sbank_empty"], norm["sb"])
            for g in range(KD):
                queries_and_keys(first, g, 0, 0)
            for i in range(2):
                values(first, i, KD)
            pe.wait_ge(c.s["vbank_empty"], s0["vb"])

            def attn(b, more):
                n = Span(s0, ATTN0, b)

                def mid(t):
                    if t == 32:
                        ln_turn(c, pe, n("ln"), n("sb"))
                    if more and t in (64, 66):
                        if t == 64:
                            pe.wait_ge(c.s["sbank_empty"], n("sb", 2))
                        queries_and_keys(n, (t - 64) // 2, 2, 64)
                    if more and t in (69, 71):
                        values(n, (t - 69) // 2, 66)
                heads_pe(c, pe, n, h, mid)
                pe.wait_ge(c.s["obank_empty"], n("ob", KD))
                out = 68 if more else 64
                for i in range(2):
                    pe.wait_ge(c.s["vbank_empty"], n("vb", out - 1 + i))
                    for t in range(2 * i, 2 * i + 2):
                        for g in range(KD):
                            ins = nc.tensor.matmul(c.vbank[i][:, (t % 2) * D:(t % 2 + 1) * D],
                                                   aoT[:, g, t * P:(t + 1) * P], wo[:, g, :],
                                                   start=(g == 0), stop=(g == KD - 1))
                    ins.then_inc(c.s["vbank_full"], 1)
            loop(c, pe, B, attn)

            def ffn(b, more):
                n = Span(s1, FFN0, b)
                pe.wait_ge(c.s["mixed_ready"], n("mx", 1))
                for i in range(KD):
                    pe.wait_ge(c.s["sbank_empty"], n("sb", i - 1))
                    for k in range(KD):
                        ins = nc.tensor.matmul(c.sbank[i][:, :], wf[:, 1, k, i * P:(i + 1) * P], mixT[:, 1, k, :],
                                               start=(k == 0), stop=(k == KD - 1))
                    ins.then_inc(c.s["sbank_full"], 1)
                for i in range(2):
                    pe.wait_ge(c.s["sbank_empty"], n("sb", 1 + i))
                    for t in range(2 * i, 2 * i + 2):
                        for k in range(KD):
                            ins = nc.tensor.matmul(c.sbank[i][:, (t % 2) * D:(t % 2 + 1) * D],
                                                   mixT[:, 0, k, t * P:(t + 1) * P], wf[:, 0, k, :],
                                                   start=(k == 0), stop=(k == KD - 1))
                    ins.then_inc(c.s["sbank_full"], 1)
                if more:
                    ln_turn(c, pe, n("ln"), n("sb", 4))
                pe.wait_ge(c.s["squared_ready"], n("mx", 1))
                for i in range(2):
                    pe.wait_ge(c.s["vbank_empty"], n("vb", i - 1))
                    for t in range(2 * i, 2 * i + 2):
                        for k in range(KD):
                            ins = nc.tensor.matmul(c.vbank[i][:, (t % 2) * D:(t % 2 + 1) * D],
                                                   kact[:, k, t * P:(t + 1) * P], wf[:, 2, k, :],
                                                   start=(k == 0), stop=(k == KD - 1))
                    ins.then_inc(c.s["vbank_full"], 1)
            loop(c, pe, B, ffn)
    c.loaded = loaded0
    return end


def one_row(rows, b):
    r = rows[:, b:b + 1, :] if isinstance(b, int) else rows[:, bass.ds(b, 1), :]
    return r.to_broadcast([P, 2, D])


def row_of(rows, b):
    return rows[:, b:b + 1, :] if isinstance(b, int) else rows[:, bass.ds(b, 1), :]



REMIX = {"ln": 1}


def remix(c, d, start, gate, scale, shift):
    nc = c.nc
    end = after(start, REMIX, B)
    names = [gate, scale, shift] if gate else [scale, shift]
    with ExitStack() as st:
        def sb(name, shape):
            return st.enter_context(nc.sbuf_tensor(f"{name}_{scale}", shape, F32))

        rows = sb("rows", [P, 3, B, D])
        mean_var = sb("mean_var", [P, B, NT, 2])
        inv_std = sb("inv_std", [P, B, NT])
        neg_half = sb("neg_half", [P, B, NT])
        block = st.enter_context(nc.Block())
        loaded = c.loaded + 16 * len(names)

        def row(i, b):
            return row_of(rows[:, i], b).to_broadcast([P, NT, D])

        def tile_row(i, b):
            return row_of(rows[:, i], b).rearrange("p a n -> p (a n)")

        @block.sync
        def _(sp):
            for i, name in enumerate(names):
                sp.dma_start(rows[:, i + (not gate), :, :], mod_rows(c, 1, name)).then_inc(c.s["load"], 16)

        @block.gpsimd
        def _(pool):
            nc.gpsimd.memset(neg_half[:, :, :], -0.5)
            pool.wait_ge(c.s["load"], loaded)
            if gate:
                with pool.Fori(0, B) as b:
                    nc.gpsimd.tensor_tensor(c.y[:, b], c.y[:, b], row(0, b), ALU.mult).then_inc(c.s["gated"], 1)
            pool.wait_ge(c.s["stats_ready"], start["ln"] + B)
            chain(c, pool, c.s["p_chain"], nc.gpsimd.tensor_scalar(inv_std[:, :, :], mean_var[:, :, :, 1], EPS, None,
                                                                   ALU.add))
            nc.gpsimd.tensor_tensor(inv_std[:, :, :], inv_std[:, :, :], neg_half[:, :, :], ALU.pow)\
              .then_inc(c.s["rstd_ready"], B)

        @block.vector
        def _(dve):
            with dve.Fori(0, B) as b:
                if gate:
                    dve.wait_ge(c.s["gated"], b + 1)
                    chain(c, dve, c.s["v_chain"], nc.vector.tensor_tensor(c.x[:, b], c.x[:, b], c.y[:, b], ALU.add))
                for t in range(NT):
                    ins = nc.vector.bn_stats(c.bn[:, t, :], c.x[:, b, t, :])
                chain(c, dve, c.s["v_chain"], ins)
                for t in range(NT):
                    ins = nc.vector.bn_aggr(c.mv[:, t, :], c.bn[:, t, :])
                chain(c, dve, c.s["v_chain"], ins)
                nc.vector.tensor_copy(mean_var[:, b], c.mv[:, :, :]).then_inc(c.s["stats_ready"], 1)
                dve.wait_ge(c.s["stats_ready"], start["ln"] + b + 1)
                alone(c, dve)
            dve.wait_ge(c.s["load"], loaded)
            dve.wait_ge(c.s["rstd_ready"], start["ln"] + B)
            alone(c, dve)
            with dve.Fori(0, B) as b:
                for t in range(NT):
                    ins = nc.vector.scalar_tensor_tensor(out=c.y[:, b, t, :], in0=c.x[:, b, t, :],
                                                         scalar=mean_var[:, b, t, 0:1], in1=tile_row(1, b),
                                                         op0=ALU.subtract, op1=ALU.mult)
                chain(c, dve, c.s["v_chain"], ins)
                for t in range(NT):
                    ins = nc.vector.scalar_tensor_tensor(out=c.y[:, b, t, :], in0=c.y[:, b, t, :],
                                                         scalar=inv_std[:, b, t:t + 1], in1=tile_row(2, b),
                                                         op0=ALU.mult, op1=ALU.add)
                ins.then_inc(c.s["normed_ready"], 1)
    c.loaded = loaded
    return end



ATTN1 = {"vb": 26, "pb": 16, "av": 4, "ob": 2, "at": 1}
VL = 2 * P
LIN = VL + P
CTX = HD1 + 1
CTXW = P + 4


KEPT = 8


CLEARED = 2048


class Turn:

    def __init__(self, attn, mlp, more):
        self.attn, self.mlp, self.more = attn, mlp, more
        self.qk = 0
        self.mlp_norm = 2 * attn
        self.hidden = self.mlp_norm + 2 * mlp
        self.next_norm = self.hidden + MF * mlp
        self.adds = {"sb": self.next_norm + 2 * more, "ln": mlp + more, "ml": mlp}
        if attn:
            self.adds.update(ATTN1)


FIRST, INNER, LAST, TAIL = Turn(1, 0, 1), Turn(1, 1, 1), Turn(1, 1, 0), Turn(0, 1, 1)
DEPTH_ADDS = {}
for _turn, _times in ((FIRST, 1), (INNER, B - 2), (LAST, 1), (TAIL, 1)):
    DEPTH_ADDS = after(DEPTH_ADDS, _turn.adds, _times)


def depth_turns(c, eng, start, body):
    body(0, FIRST, Span(start, FIRST.adds, 0))
    start = after(start, FIRST.adds, 1)
    alone(c, eng)
    with eng.Fori(0, B - 2) as i:
        body(i + 1, INNER, Span(start, INNER.adds, i))
    start = after(start, INNER.adds, B - 2)
    body(B - 1, LAST, Span(start, LAST.adds, 0))
    start = after(start, LAST.adds, 1)
    body(B, TAIL, Span(start, TAIL.adds, 0))


def layer1(c, d, start):
    nc = c.nc
    begin = after(start, {"sb": KD, "ln": 1}, 1)
    end = after(begin, DEPTH_ADDS, DEPTH)
    with ExitStack() as st:
        def sb(name, shape, dt=F32):
            return st.enter_context(nc.sbuf_tensor(name, shape, dt))

        wq = sb("wq1", [P, KD, P])
        wk = sb("wk1", [P, KD, P])
        wtok = sb("wtok", [P, KD, 2 * P + D])
        wo = sb("wo1", [P, KD, D])
        w1 = sb("w1", [P, KD, FF])
        w2 = sb("w2", [P, MF, D])
        bo = sb("bo", [P, 1, D])
        b2 = sb("b2", [P, 1, D])
        vec = sb("vec", [P, DEPTH + 1, 8 + MF])
        qT = sb("qT1", [P, T])
        kT = sb("kT1", [P, T])
        tok = sb("tok", [P, NT, LIN + P + 4])
        kneg = sb("kneg", [P, NT, P])
        qmax = sb("qmax", [P, NT, 4])
        qinv = sb("qinv", [P, NT, 4])
        qlT = sb("qlT", [P, T])
        ctx = sb("ctx", [P, NU - 1, CTX])
        kcum = sb("kcum", [P, NU - 1])
        bd = sb("bd", [P, NU - 1, P])
        mask = sb("mask", [P, 2 * P])
        aoT = sb("aoT1", [P, KD, T])
        h2T = sb("h2T", [P, KD, T + 1])
        gT = sb("gT", [P, MF, T])
        zeros = sb("zeros", [P, CLEARED])
        block = st.enter_context(nc.Block())

        def depth_start(e):
            return {k: begin.get(k, 0) + e * DEPTH_ADDS.get(k, 0) for k in {*begin, *DEPTH_ADDS}}

        h = Heads(
            quads=4,
            q_of=lambda q, j: qT[32 * j:32 * j + 32, q * P:(q + 1) * P],
            k_of=lambda q, j, lo, hi: kT[32 * j:32 * j + 32, lo * P:hi * P],
            keys_of=lambda q: [q - 1, q] if q else [q],
            mask_of=lambda q, j: mask[:, 0:2 * P] if q else mask[:, P:2 * P],
            v_of=lambda q, j, key: tok[:, key, VL + 32 * j:VL + 32 * j + 32],
            out_of=lambda q: (c.obank[0], slice(q * P, (q + 1) * P)),
            vb=4)
        all_wa, all_wm = 5 * 16, 3 * 16

        @block.sync
        def _(sp):
            sp.dma_start(vec[:, 0:DEPTH, :], d["vec"]).then_inc(c.s["load"], 16)

            def attn_weights(e):
                sp.dma_start(wtok[:, :, :], d["wtok"][e].rearrange("(k p) n -> p k n", p=P))\
                  .then_inc(c.s["attn_weights"], 16)
                for w, name in ((wq, "Aq"), (wk, "Ak")):
                    sp.dma_start(w[:, :, :], d[name][e].rearrange("(k p) n -> p k n", p=P)[:, :, 0:P])\
                      .then_inc(c.s["attn_weights"], 16)
                sp.dma_start(wo[:, :, :], d["Ao"][e].rearrange("(k p) n -> p k n", p=P))\
                  .then_inc(c.s["attn_weights"], 16)
                sp.dma_start(bo[:, :, :], row(d["bo"], e)).then_inc(c.s["attn_weights"], 16)

            def mlp_weights(e):
                sp.dma_start(w1[:, :, :], d["W1"][e].rearrange("(k p) n -> p k n", p=P))\
                  .then_inc(c.s["mlp_weights"], 16)
                sp.dma_start(w2[:, :, :], d["W2"][e].rearrange("(k p) n -> p k n", p=P))\
                  .then_inc(c.s["mlp_weights"], 16)
                sp.dma_start(b2[:, :, :], row(d["b2"], e)).then_inc(c.s["mlp_weights"], 16)

            def row(bias, e):
                return (bias[e:e + 1, :] if isinstance(e, int) else bias[bass.ds(e, 1), :]).partition_broadcast(P)

            attn_weights(0)
            mlp_weights(0)
            sp.wait_ge(c.s["aux"], 5)
            parts = SLOTS_X * D // (P * CLEARED)
            by_part = c.expert_in.rearrange("(p r) n -> p (r n)", p=P)
            for i in range(parts):
                sp.dma_start(by_part[:, i * CLEARED:(i + 1) * CLEARED], zeros[:, :]).then_inc(c.s["cleared"], 16)
            with sp.Fori(0, DEPTH - 1) as e:
                n = Span(begin, DEPTH_ADDS, e)
                sp.wait_ge(c.s["vbank_empty"], n("vb", DEPTH_ADDS["vb"]))
                attn_weights(e + 1)
                sp.wait_ge(c.s["mlp_added"], 2 * B * (e + 1))
                mlp_weights(e + 1)
            sp.wait_ge(c.s["cleared"], 16 * parts)

        @block.gpsimd
        def _(pool):
            nc.gpsimd.memset(zeros[:, :], 0.0)
            nc.gpsimd.memset(bd[:, :, :], 0.0)
            nc.gpsimd.memset(aoT[:, 1, 0:BUCKET], 0.0)
            nc.gpsimd.memset(tok[:, :, LIN + P:LIN + P + 1], 1.0)
            nc.gpsimd.memset(vec[:, DEPTH, :], 0.0)
            chain(c, pool, c.s["p_chain"], nc.gpsimd.memset(mask[:, :], 0.0))
            cur = mask[:, P:2 * P]
            nc.gpsimd.affine_select(out=cur, in_=cur, compare_op=ALU.is_ge, fill=BIG, base=0, pattern=[[-1, P]],
                                    channel_multiplier=1).then_inc(c.s["aux"], 1)
            ln_rstd(c, pool, start["ln"])
            with pool.Fori(0, DEPTH) as e:
                pool.wait_ge(c.s["attn_weights"], (e + 1) * all_wa)
                alone(c, pool)
                pool.wait_ge(c.s["mlp_weights"], (e + 1) * all_wm)
                alone(c, pool)

                def body(b, turn, n):
                    if turn.mlp:
                        ln_rstd(c, pool, n("ln"))
                    if turn.attn:
                        pool.wait_ge(c.s["normed_ready"], n("ln"))
                        yb = c.y[:, b]
                        nc.gpsimd.tensor_tensor(yb, yb, bo[:, :, :].to_broadcast([P, NT, D]), ALU.add)\
                          .then_inc(c.s["attn_biased"], 1)
                    if turn.mlp:
                        pool.wait_ge(c.s["normed_ready"], n("ln", 1))
                        yb = c.y[:, b - 1]
                        nc.gpsimd.tensor_tensor(yb, yb, b2[:, :, :].to_broadcast([P, NT, D]), ALU.add)\
                          .then_inc(c.s["mlp_biased"], 1)
                    if turn.attn:
                        pool.wait_ge(c.s["lin_inverted"], n("at", 1))
                        ql = tok[:, :, 0:P].rearrange("p t (h e) -> p t h e", e=HD1)
                        nc.gpsimd.tensor_tensor(ql, ql, qinv[:, :, :].unsqueeze(3).to_broadcast([P, NT, 4, HD1]),
                                                ALU.mult).then_inc(c.s["lin_q_ready"], 1)

                        def mid(q):
                            if q == 1 and turn.more:
                                ln_rstd(c, pool, n("ln", turn.mlp))
                        heads_pool(c, pool, n, h, mid)
                    elif turn.more:
                        ln_rstd(c, pool, n("ln", turn.mlp))
                depth_turns(c, pool, depth_start(e), body)

        @block.vector
        def _(dve):
            ln_stats(c, dve, start["ln"], c.y[:, 0])
            ln_norm(c, dve, start["ln"], c.y[:, 0], start["sb"])
            dve.wait_ge(c.s["aux"], 5)
            with dve.Fori(0, DEPTH) as e:

                def body(b, turn, n):
                    if turn.mlp:
                        ln_stats(c, dve, n("ln"), c.y[:, b - 1])
                    if turn.attn:
                        for t in range(NT):
                            dve.wait_ge(c.s["vbank_full"], n("vb", t + 1))
                            nc.vector.tensor_copy(tok[:, t, 0:LIN + P], c.vbank[t % 2][:, :])\
                              .then_inc(c.s["vbank_empty"], 1)
                            if t == 1 and turn.mlp:
                                ln_norm(c, dve, n("ln"), c.y[:, b - 1], n("sb"))
                        dve.wait_ge(c.s["vbank_empty"], n("vb", NT))
                        attention(b, turn, n)
                    else:
                        ln_norm(c, dve, n("ln"), c.y[:, b - 1], n("sb"))
                        ln_stats(c, dve, n("ln", 1), c.y[:, 0])
                        ln_norm(c, dve, n("ln", 1), c.y[:, 0], n("sb", turn.hidden))
                        mlp_sum(b, n, 0)
                        mlp_sum(b, n, 1)

                def mlp_sum(b, n, i):
                    dve.wait_ge(c.s["mlp_biased"], n("ml", 1))
                    dve.wait_ge(c.s["mlp_full"], 2 * n("ml") + i + 1)
                    ys = c.y[:, b - 1, 2 * i:2 * i + 2, :]
                    nc.vector.tensor_tensor(ys, ys, c.sbank[i][:, :].rearrange("p (t n) -> p t n", t=2), ALU.add)\
                      .then_inc(c.s["mlp_added"], 1)

                def attention(b, turn, n):
                    ql = tok[:, :, 0:P].rearrange("p t (h e) -> p t h e", e=HD1)
                    kl = tok[:, :, P:2 * P]
                    nc.vector.tensor_scalar(kneg[:, :, :], kl, 0.0, None, ALU.min)
                    chain(c, dve, c.s["v_chain"],
                          nc.vector.tensor_reduce(qmax[:, :, :], ql, AX.X, ALU.max))
                    nc.vector.tensor_tensor(ql, ql, qmax[:, :, :].unsqueeze(3).to_broadcast([P, NT, 4, HD1]),
                                            ALU.subtract).then_inc(c.s["lin_shifted"], 1)

                    def context(i):
                        dve.wait_ge(c.s["vbank_full"], n("vb", 21 + i))
                        us = min(2, NU - 1 - 2 * i)
                        src = c.vbank[i % 2][:, 0:us * CTXW].rearrange("p (u n) -> p u n", u=us)
                        for j in range(4):
                            nc.vector.tensor_copy(ctx[32 * j:32 * j + 32, 2 * i:2 * i + us, 0:HD1],
                                                  src[32 * j:32 * j + 32, :, 32 * j:32 * j + 32])
                        nc.vector.tensor_copy(ctx[:, 2 * i:2 * i + us, HD1:CTX], src[:, :, P:P + 1])\
                          .then_inc(c.s["vbank_empty"], 1)

                    def mid(t):
                        if t == 2:
                            dve.wait_ge(c.s["lin_exped"], n("at", 0) * 2 + 1)
                            chain(c, dve, c.s["v_chain"],
                                  nc.vector.tensor_reduce(qmax[:, :, :], ql, AX.X, ALU.add))
                            nc.vector.reciprocal(qinv[:, :, :], qmax[:, :, :]).then_inc(c.s["lin_inverted"], 1)
                        if t == 4:
                            dve.wait_ge(c.s["lin_exped"], n("at", 0) * 2 + 2)
                            nc.vector.scalar_tensor_tensor(out=kl, in0=kl, scalar=0.0, in1=kneg[:, :, :],
                                                           op0=ALU.max, op1=ALU.add).then_inc(c.s["lin_k_ready"], 1)
                        if turn.more and t == 9:
                            ln_stats(c, dve, n("ln", turn.mlp), c.y[:, b + 1])
                        if turn.more and t == 12:
                            ln_norm(c, dve, n("ln", turn.mlp), c.y[:, b + 1], n("sb", turn.hidden))
                        if t >= 20 and t % 2 == 0 and t < 28:
                            context((t - 20) // 2)
                    heads_dve(c, dve, n, h, mid)
                    dve.wait_ge(c.s["vbank_empty"], n("vb", 24))
                    for u in range(2, NU - 1, 2):
                        to = slice(u, min(u + 2, NU - 1))
                        before = ctx[:, u - 1:u, :].to_broadcast([P, to.stop - to.start, CTX])
                        chain(c, dve, c.s["v_chain"], nc.vector.tensor_tensor(ctx[:, to, :], ctx[:, to, :], before,
                                                                              ALU.add))
                    chain(c, dve, c.s["v_chain"], nc.vector.tensor_scalar(kcum[:, :], ctx[:, :, HD1], 1e-6, None,
                                                                          ALU.add))
                    chain(c, dve, c.s["v_chain"], nc.vector.reciprocal(kcum[:, :], kcum[:, :]))
                    for j in range(4):
                        q = slice(32 * j, 32 * j + 32)
                        ins = nc.vector.tensor_tensor(bd[q, :, q], ctx[q, :, 0:HD1],
                                                      kcum[q, :].unsqueeze(2).to_broadcast([32, NU - 1, HD1]),
                                                      ALU.mult)
                    ins.then_inc(c.s["context_ready"], 1)
                    if turn.mlp:
                        mlp_sum(b, n, 0)
                        mlp_sum(b, n, 1)
                    dve.wait_ge(c.s["attn_biased"], n("at", 1))
                    for i in range(2):
                        dve.wait_ge(c.s["vbank_full"], n("vb", 25 + i))
                        ys = c.y[:, b, 2 * i:2 * i + 2, :]
                        nc.vector.tensor_tensor(ys, ys, c.vbank[i][:, :].rearrange("p (t n) -> p t n", t=2), ALU.add)\
                          .then_inc(c.s["vbank_empty"], 1)
                    dve.wait_ge(c.s["vbank_empty"], n("vb", 26))
                depth_turns(c, dve, depth_start(e), body)

        @block.scalar
        def _(act):
            act.wait_ge(c.s["load"], c.loaded + 16)
            ln_gain(c, act, start["sb"], lambda k: vec[:, 0, k:k + 1], lambda k: vec[:, 0, 2 + k:3 + k])
            with act.Fori(0, DEPTH) as e:
                v = vec[:, e, :]

                def body(b, turn, n):
                    if turn.attn:
                        act.wait_ge(c.s["sbank_full"], n("sb", 1))
                        nc.scalar.mul(qT[:, :], c.sbank[0][:, :], -float(HD1) ** -0.5).then_inc(c.s["sbank_empty"], 1)
                        act.wait_ge(c.s["sbank_full"], n("sb", 2))
                        nc.scalar.copy(kT[:, :], c.sbank[1][:, :]).then_inc(c.s["sbank_empty"], 1)
                    if turn.mlp:
                        ln_gain(c, act, n("sb", turn.mlp_norm), lambda k: v[:, 4 + k:5 + k],
                                lambda k: v[:, 6 + k:7 + k], h2T)
                        for m in range(MF):
                            act.wait_ge(c.s["sbank_full"], n("sb", turn.hidden + m + 1))
                            alone(c, act)
                            nc.scalar.activation(gT[:, m, :], c.sbank[m % 2][:, :], ACT.Gelu, bias=v[:, 8 + m:9 + m])\
                              .then_inc(c.s["sbank_empty"], 1)
                    if turn.attn:
                        act.wait_ge(c.s["lin_shifted"], n("at", 1))
                        nc.scalar.activation(tok[:, :, 0:P], tok[:, :, 0:P], ACT.Exp).then_inc(c.s["lin_exped"], 1)
                        nc.scalar.activation(kneg[:, :, :], kneg[:, :, :], ACT.Exp).then_inc(c.s["lin_exped"], 1)

                        def mid(k):
                            if k == 11:
                                act.wait_ge(c.s["lin_turned"], n("at", 1))
                                nc.scalar.copy(qlT[:, :], c.obank[1][:, :]).then_inc(c.s["lin_qT_ready"], 1)
                        heads_act(c, act, n, h, mid)
                        act.wait_ge(c.s["obank_full"], n("av", 4))
                        nc.scalar.copy(aoT[:, 0, :], c.obank[0][:, :]).then_inc(c.s["obank_empty"], 1)
                        act.wait_ge(c.s["lin_full"], n("at", 1))
                        nc.scalar.copy(aoT[:, 1, BUCKET:T], c.obank[1][:, BUCKET:T]).then_inc(c.s["obank_empty"], 1)
                    if turn.more:
                        w = v if turn.attn else vec[:, e + 1, :]
                        ln_gain(c, act, n("sb", turn.next_norm), lambda k: w[:, k:k + 1], lambda k: w[:, 2 + k:3 + k])
                depth_turns(c, act, depth_start(e), body)

        @block.tensor
        def _(pe):
            ln_turn(c, pe, start["ln"], start["sb"])
            with pe.Fori(0, DEPTH) as e:
                pe.wait_ge(c.s["attn_weights"], (e + 1) * all_wa)
                alone(c, pe)

                def body(b, turn, n):
                    if turn.attn:
                        project(n)
                    if turn.mlp:
                        pe.wait_ge(c.s["mlp_weights"], (e + 1) * all_wm)
                        ln_turn(c, pe, n("ln"), n("sb", turn.mlp_norm))
                        pe.wait_ge(c.s["sbank_empty"], n("sb", turn.hidden))
                        for m in range(MF):
                            pe.wait_ge(c.s["sbank_empty"], n("sb", turn.hidden + m - 1))
                            for k in range(KD):
                                ins = nc.tensor.matmul(c.sbank[m % 2][:, :], w1[:, k, m * P:(m + 1) * P],
                                                       h2T[:, k, 1:T + 1], start=(k == 0), stop=(k == KD - 1))
                            ins.then_inc(c.s["sbank_full"], 1)
                    pieces = [(i, t, m) for i in range(2) for t in (2 * i, 2 * i + 1) for m in range(MF)] \
                        if turn.mlp else []

                    def down(count, kept=0):
                        count = min(count, max(0, len(pieces) - kept))
                        for i, t, m in pieces[:count]:
                            if m == 0 and t == 2 * i:
                                pe.wait_ge(c.s["sbank_empty"], n("sb", turn.next_norm + i - 1))
                                if i == 0:
                                    pe.wait_ge(c.s["sbank_empty"], n("sb", turn.next_norm))
                            ins = nc.tensor.matmul(c.sbank[i][:, (t % 2) * D:(t % 2 + 1) * D],
                                                   gT[:, m, t * P:(t + 1) * P], w2[:, m, :],
                                                   start=(m == 0), stop=(m == MF - 1))
                            if m == MF - 1 and t == 2 * i + 1:
                                ins.then_inc(c.s["mlp_full"], 1)
                        del pieces[:count]

                    if turn.attn:
                        attention(turn, n, down)
                    else:
                        down(4 * MF)
                        next_norm(turn, n)

                def next_norm(turn, n):
                    if turn.mlp:
                        pe.wait_ge(c.s["mlp_added"], 2 * n("ml", 1))
                    ln_turn(c, pe, n("ln", turn.mlp), n("sb", turn.next_norm))

                def project(n):
                    pe.wait_ge(c.s["sbank_empty"], n("sb"))
                    for t in range(NT):
                        pe.wait_ge(c.s["vbank_empty"], n("vb", t - 1))
                        for k in range(KD):
                            ins = nc.tensor.matmul(c.vbank[t % 2][:, :], c.hT[:, k, 1 + t * P:1 + (t + 1) * P],
                                                   wtok[:, k, :], start=(k == 0), stop=(k == KD - 1))
                        ins.then_inc(c.s["vbank_full"], 1)
                        if t % 2 == 1:
                            i = t // 2
                            pe.wait_ge(c.s["sbank_empty"], n("sb", i - 1))
                            for k in range(KD):
                                ins = nc.tensor.matmul(c.sbank[i][:, :], (wq, wk)[i][:, k, :], c.hT[:, k, 1:T + 1],
                                                       start=(k == 0), stop=(k == KD - 1))
                            ins.then_inc(c.s["sbank_full"], 1)

                def attention(turn, n, down):
                    pe.wait_ge(c.s["sbank_empty"], n("sb", 2))

                    def context(i):
                        pe.wait_ge(c.s["vbank_empty"], n("vb", 19 + i))
                        for u in range(2 * i, min(2 * i + 2, NU - 1)):
                            rows = slice(0, BUCKET if u % 2 == 0 else P)
                            at = (u % 2) * CTXW
                            ins = nc.tensor.matmul(c.vbank[i % 2][:, at:at + P + 1], tok[rows, u // 2, P:2 * P],
                                                   tok[rows, u // 2, LIN:LIN + P + 1], start=True, stop=True)
                        ins.then_inc(c.s["vbank_full"], 1)

                    def mid(t):
                        if t >= 2:
                            down(2, KEPT)
                        if t == 9:
                            pe.wait_ge(c.s["lin_q_ready"], n("at", 1))
                            for r in range(NT):
                                ins = nc.tensor.transpose(c.obank[1][:, r * P:(r + 1) * P], tok[:, r, 0:P],
                                                          c.ident[:, :])
                            ins.then_inc(c.s["lin_turned"], 1)
                        if t == 16:
                            pe.wait_ge(c.s["lin_k_ready"], n("at", 1))
                            context(0)
                            context(1)
                        if t == 22:
                            context(2)
                        if t == 24:
                            context(3)
                    heads_pe(c, pe, n, h, mid)
                    down(4 * MF)
                    pe.wait_ge(c.s["lin_qT_ready"], n("at", 1))
                    pe.wait_ge(c.s["context_ready"], n("at", 1))
                    for u in range(NU - 1):
                        cols = slice(BUCKET * (u + 1), BUCKET * (u + 2))
                        ins = nc.tensor.matmul(c.obank[1][:, cols], bd[:, u, :], qlT[:, cols], start=True, stop=True)
                    ins.then_inc(c.s["lin_full"], 1)
                    if turn.more:
                        next_norm(turn, n)
                    pe.wait_ge(c.s["obank_empty"], n("ob", 2))
                    for i in range(2):
                        pe.wait_ge(c.s["vbank_empty"], n("vb", 23 + i))
                        for t in range(2 * i, 2 * i + 2):
                            for k in range(KD):
                                ins = nc.tensor.matmul(c.vbank[i][:, (t % 2) * D:(t % 2 + 1) * D],
                                                       aoT[:, k, t * P:(t + 1) * P], wo[:, k, :],
                                                       start=(k == 0), stop=(k == KD - 1))
                        ins.then_inc(c.s["vbank_full"], 1)
                depth_turns(c, pe, depth_start(e), body)
    c.loaded += 16
    return end



NEXT_QKV = {"vb": B, "sb": 4, "ln": 2}
ATTEND = {"vb": 4, "sb": 4, "cr": 1, "pr": 16}
CROSS = after(NEXT_QKV, ATTEND, 1)
GW = QKV // NKV
QH = NH // NKV
POOL_G = 2


def cross(c, d, start):
    nc = c.nc
    begin = after(start, NEXT_QKV, 1)
    end = after(after(begin, CROSS, NT - 1), ATTEND, 1)
    with ExitStack() as st:
        def sb(name, shape, dt=F32):
            return st.enter_context(nc.sbuf_tensor(name, shape, dt))

        wqkv = sb("wqkv", [P, KD, QKV])
        wp = sb("wproj", [P, KD, D])
        g1 = sb("cross_gain", [P, 2 * KD])
        qkv = [sb(f"qkv{z}", [P, B, QKV]) for z in range(2)]
        prod = sb("prod", [P, 2, NKV * B * QH * HDM])
        sc = sb("cross_scores", [P, NH, B, B])
        pr = sb("cross_probs", [P, NH, B, B])
        mx = sb("cross_max", [P, NH, B])
        ao = sb("cross_out", [P, B, D])
        aoT = sb("cross_outT", [P, KD, B, P])
        block = st.enter_context(nc.Block())
        loaded = c.loaded + 3 * 16

        def part(z, s, g, at, n):
            return qkv[z][:, s, g * GW + at:g * GW + at + n]

        def scores_of(z, s, g):
            out = prod[:, s % 2, g * (s + 1) * QH * HDM:(g + 1) * (s + 1) * QH * HDM]\
                .rearrange("p (t h e) -> p t h e", h=QH, e=HDM)
            q = part(z, s, g, 0, QH * HDM).rearrange("p (h e) -> p h e", h=QH).unsqueeze(1)\
                .to_broadcast([P, s + 1, QH, HDM])
            k = part(z, slice(0, s + 1), g, QH * HDM, HDM).unsqueeze(2).to_broadcast([P, s + 1, QH, HDM])
            return out, q, k

        def values_of(z, s, g):
            out = prod[:, s % 2, g * (s + 1) * QH * HDM:(g + 1) * (s + 1) * QH * HDM]\
                .rearrange("p (h e t) -> p h e t", h=QH, e=HDM)
            a = pr[:, g * QH:(g + 1) * QH, s, 0:s + 1].unsqueeze(2).to_broadcast([P, QH, HDM, s + 1])
            v = part(z, slice(0, s + 1), g, (QH + 1) * HDM, HDM).rearrange("p t e -> p e t").unsqueeze(1)\
                .to_broadcast([P, QH, HDM, s + 1])
            return out, a, v

        @block.sync
        def _(sp):
            sp.dma_start(wqkv[:, :, :], d["wqkv"].rearrange("(k p) n -> p k n", p=P)).then_inc(c.s["load"], 16)
            sp.dma_start(wp[:, :, :], d["wproj"].rearrange("(k p) n -> p k n", p=P)).then_inc(c.s["load"], 16)
            sp.dma_start(g1[:, :], d["cross_ln"]).then_inc(c.s["load"], 16)

        @block.gpsimd
        def _(pool):
            nc.gpsimd.memset(sc[:, :, :, :], -BIG).then_inc(c.s["aux"], 1)
            for half in range(2):
                ln_rstd(c, pool, start["ln"] + half)

            def turn(p, z, more):
                n = Span(begin, CROSS, p)
                pool.wait_ge(c.s["vbank_empty"], n("vb"))
                for s in range(B):
                    pool.wait_ge(c.s["products_used"], n("pr", s + 1))
                    for g in range(POOL_G):
                        ins = nc.gpsimd.tensor_tensor(*scores_of(z, s, g), ALU.mult)
                    ins.then_inc(c.s["products_ready"], 1)
                    if more and s in (4, 6):
                        ln_rstd(c, pool, n("ln", (s - 4) // 2))
                pool.wait_ge(c.s["cross_probs"], n("cr", 1))
                for s in range(B):
                    pool.wait_ge(c.s["products_used"], n("pr", B + s + 1))
                    for g in range(POOL_G):
                        ins = nc.gpsimd.tensor_tensor(*values_of(z, s, g), ALU.mult)
                    ins.then_inc(c.s["products_ready"], 1)
            grouped(c, pool, NT, 2, turn)

        @block.vector
        def _(dve):
            dve.wait_ge(c.s["aux"], 6)
            dve.sem_inc(c.s["products_used"], 2)

            def four_rows(half, p):
                return c.y[:, 4 * half:4 * half + 4, p, :]

            def qkv_out(z, half, n):
                for s in range(4 * half, 4 * half + 4):
                    dve.wait_ge(c.s["vbank_full"], n("vb", s + 1))
                    nc.vector.tensor_copy(qkv[z][:, s, :], c.vbank[s % 2][:, 0:QKV]).then_inc(c.s["vbank_empty"], 1)

            first = Span(start, NEXT_QKV, 0)
            for half in range(2):
                ln_stats(c, dve, first("ln", half), four_rows(half, 0))
                ln_norm(c, dve, first("ln", half), four_rows(half, 0), first("sb", 2 * half))
                qkv_out(0, half, first)

            def turn(p, z, more):
                n = Span(begin, CROSS, p)
                dve.wait_ge(c.s["vbank_empty"], n("vb"))
                alone(c, dve)
                for s in range(B):
                    for g in range(POOL_G, NKV):
                        ins = nc.vector.tensor_tensor(*scores_of(z, s, g), ALU.mult)
                    chain(c, dve, c.s["v_chain"], ins)
                    dve.wait_ge(c.s["products_ready"], n("pr", s + 1))
                    src = prod[:, s % 2, 0:(s + 1) * D].rearrange("p (g t h e) -> p g t h e", g=NKV, h=QH, e=HDM)
                    to = sc[:, :, s, 0:s + 1].rearrange("p (g h) t -> p g t h", g=NKV)
                    if s == 0:
                        src, to = src[:, :, 0], to[:, :, 0]
                    nc.vector.tensor_reduce(to, src, AX.X, ALU.add).then_inc(c.s["products_used"], 1)
                    if more and s in (2, 5):
                        ln_stats(c, dve, n("ln", s // 4), four_rows(s // 4, p + 1))
                    if more and s == 4:
                        ln_norm(c, dve, n("ln"), four_rows(0, p + 1), n("sb"))
                    if more and s == 6:
                        qkv_out(1 - z, 0, n)
                        ln_norm(c, dve, n("ln", 1), four_rows(1, p + 1), n("sb", 2))
                dve.wait_ge(c.s["products_used"], n("pr", B + 2))
                chain(c, dve, c.s["v_chain"], nc.vector.tensor_reduce(mx[:, :, :], sc[:, :, :, :], AX.X, ALU.max))
                nc.vector.tensor_tensor(pr[:, :, :, :], sc[:, :, :, :], mx[:, :, :].unsqueeze(3)
                                        .to_broadcast([P, NH, B, B]), ALU.subtract).then_inc(c.s["cross_shifted"], 1)
                if more:
                    qkv_out(1 - z, 1, n)
                dve.wait_ge(c.s["cross_exped"], n("cr", 1))
                chain(c, dve, c.s["v_chain"], nc.vector.tensor_reduce(mx[:, :, :], pr[:, :, :, :], AX.X, ALU.add))
                chain(c, dve, c.s["v_chain"], nc.vector.reciprocal(mx[:, :, :], mx[:, :, :]))
                nc.vector.tensor_tensor(pr[:, :, :, :], pr[:, :, :, :], mx[:, :, :].unsqueeze(3)
                                        .to_broadcast([P, NH, B, B]), ALU.mult).then_inc(c.s["cross_probs"], 1)
                dve.wait_ge(c.s["cross_probs"], n("cr", 1))
                alone(c, dve)
                for s in range(B):
                    for g in range(POOL_G, NKV):
                        ins = nc.vector.tensor_tensor(*values_of(z, s, g), ALU.mult)
                    chain(c, dve, c.s["v_chain"], ins)
                    dve.wait_ge(c.s["products_ready"], n("pr", B + s + 1))
                    src = prod[:, s % 2, 0:(s + 1) * D].rearrange("p (n t) -> p n t", t=s + 1)
                    nc.vector.tensor_reduce(ao[:, s, :], src, AX.X, ALU.add).then_inc(c.s["products_used"], 1)
                before = B if more else 0
                for i in range(4):
                    dve.wait_ge(c.s["vbank_full"], n("vb", before + i + 1))
                    ys = c.y[:, 2 * i:2 * i + 2, p, :]
                    nc.vector.tensor_tensor(ys, ys, c.vbank[i % 2][:, :].rearrange("p (t n) -> p t n", t=2), ALU.add)\
                      .then_inc(c.s["vbank_empty"], 1)
            grouped(c, dve, NT, 2, turn)

        @block.scalar
        def _(act):
            act.wait_ge(c.s["load"], loaded)

            def gain(n):
                for half in range(2):
                    if half:
                        act.wait_ge(c.s["vbank_full"], n("vb", 4))
                    ln_gain(c, act, n("sb", 2 * half), lambda k: g1[:, k:k + 1], lambda k: g1[:, 2 + k:3 + k])
            gain(Span(start, NEXT_QKV, 0))

            def turn(p, z, more):
                n = Span(begin, CROSS, p)
                if more:
                    gain(n)
                act.wait_ge(c.s["cross_shifted"], n("cr", 1))
                nc.scalar.activation(pr[:, :, :, :], pr[:, :, :, :], ACT.Exp, scale=float(HDM) ** -0.5)\
                  .then_inc(c.s["cross_exped"], 1)
                before = 4 if more else 0
                for i in range(4):
                    act.wait_ge(c.s["sbank_full"], n("sb", before + 1 + i))
                    nc.scalar.copy(aoT[:, i // 2, 4 * (i % 2):4 * (i % 2) + 4, :].rearrange("p s t -> p (s t)"),
                                   c.sbank[i % 2][:, :]).then_inc(c.s["sbank_empty"], 1)
            grouped(c, act, NT, 2, turn)

        @block.tensor
        def _(pe):
            pe.wait_ge(c.s["load"], loaded)

            def project(n):
                for half in range(2):
                    ln_turn(c, pe, n("ln", half), n("sb", 2 * half))
                    pe.wait_ge(c.s["sbank_empty"], n("sb", 2 * half + 2))
                    for t in range(4):
                        pe.wait_ge(c.s["vbank_empty"], n("vb", 4 * half + t - 1))
                        for k in range(KD):
                            ins = nc.tensor.matmul(c.vbank[t % 2][:, 0:QKV], c.hT[:, k, 1 + t * P:1 + (t + 1) * P],
                                                   wqkv[:, k, :], start=(k == 0), stop=(k == KD - 1))
                        ins.then_inc(c.s["vbank_full"], 1)
            project(Span(start, NEXT_QKV, 0))

            def turn(p, z, more):
                n = Span(begin, CROSS, p)
                if more:
                    project(n)
                sb_before, vb_before = (4, B) if more else (0, 0)
                pe.wait_ge(c.s["products_used"], n("pr", 2 * B + 2))
                for i in range(4):
                    pe.wait_ge(c.s["sbank_empty"], n("sb", sb_before + i - 1))
                    for r in range(4):
                        s = 4 * (i % 2) + r
                        ins = nc.tensor.transpose(c.sbank[i % 2][:, r * P:(r + 1) * P],
                                                  ao[:, s, (i // 2) * P:(i // 2 + 1) * P], c.ident[:, :])
                    ins.then_inc(c.s["sbank_full"], 1)
                pe.wait_ge(c.s["sbank_empty"], n("sb", sb_before + 4))
                for i in range(4):
                    pe.wait_ge(c.s["vbank_empty"], n("vb", vb_before + i - 1))
                    for r in range(2):
                        for k in range(KD):
                            ins = nc.tensor.matmul(c.vbank[i % 2][:, r * D:(r + 1) * D], aoT[:, k, 2 * i + r, :],
                                                   wp[:, k, :], start=(k == 0), stop=(k == KD - 1))
                    ins.then_inc(c.s["vbank_full"], 1)
            grouped(c, pe, NT, 2, turn)
    c.loaded = loaded
    return end



ROUTE = {"vb": 2, "sb": 2, "ln": 1, "mo": 1}
KF = FM // P
CHUNK_T = 256
CHUNKS = CAP // CHUNK_T
EXPERTS = {"vb": 2 * CHUNKS, "sb": 6 * CHUNKS, "ck": 2 * CHUNKS}
SLOTS_X = E * CAP
IN_FLIGHT = 4
FAR = 1e6


def moe(c, d, start, out):
    nc = c.nc
    with ExitStack() as st:
        def sb(name, shape, dt=F32):
            return st.enter_context(nc.sbuf_tensor(name, shape, dt))

        c.w1 = [sb(f"we1_{z}", [P, KD, FM]) for z in range(2)]
        c.w2 = [sb(f"we2_{z}", [P, KF, D]) for z in range(2)]
        c.gains = sb("moe_gain", [P, 2 * KD])
        c.gate = sb("gate1", [P, B, D])
        c.rows_of = sb("rows_of", [P, B, TOPK, NT], U32)
        c.share = sb("share", [P, B, TOPK, NT])
        n = routing(c, d, start)
        n = experts(c, d, n)
        combine(c, out)


def routing(c, d, start):
    nc = c.nc
    with ExitStack() as st:
        def sb(name, shape, dt=F32):
            return st.enter_context(nc.sbuf_tensor(name, shape, dt))

        wr = sb("wrouter", [P, KD, E])
        tri = sb("tri", [P, P])
        ones = sb("ones_moe", [P, P])
        expert = sb("expert", [P, 1, E])
        mean_var = sb("mean_var", [P, B, NT, 2])
        inv_std = sb("inv_std", [P, B, NT])
        neg_half = sb("neg_half", [P, B, NT])
        lg = sb("logits", [P, NT, E])
        top = sb("top", [P, NT, 8])
        index = sb("index", [P, NT, 8], U32)
        chosen_by = sb("chosen_by", [P, TOPK, NT])
        total = sb("total", [P, NT])
        hot = sb("hot", [P, TOPK, NT, E])
        chosen = sb("chosen", [P, NT, E])
        rank = sb("rank", [P, NT, E])
        base = sb("base", [P, NT + 1, E])
        place = sb("place", [P, TOPK, NT])
        kept = sb("kept", [P, TOPK, NT])
        weight = sb("weight", [P, TOPK, NT])
        first_row = sb("first_row", [P, TOPK, NT])
        row_f = sb("row_f", [P, 2, TOPK, NT])
        to_row = [sb(f"to_row{z}", [P, TOPK, NT], U32) for z in range(IN_FLIGHT)]
        normed = [c.prob[:, 2 * z:2 * z + 2, :].rearrange("p i (t n) -> p (i t) n", n=D) for z in range(IN_FLIGHT)]
        block = st.enter_context(nc.Block())
        loaded = c.loaded + 3 * 16

        @block.sync
        def _(sp):
            sp.dma_start(wr[:, :, :], d["wrouter"].rearrange("(k p) n -> p k n", p=P)).then_inc(c.s["load"], 16)
            sp.dma_start(c.gains[:, :], d["moe_ln"]).then_inc(c.s["load"], 16)
            sp.dma_start(c.gate[:, :, :], mod_rows(c, 1, "gb")).then_inc(c.s["load"], 16)
            for z in range(2):
                sp.dma_start(c.w1[z][:, :, :], d["we1"][z].rearrange("(k p) n -> p k n", p=P))\
                  .then_inc(c.s[f"expert_weights{z}"], 16)
                sp.dma_start(c.w2[z][:, :, :], d["we2"][z].rearrange("(k p) n -> p k n", p=P))\
                  .then_inc(c.s[f"expert_weights{z}"], 16)
            sp.sem_inc(c.s["normed_free"], IN_FLIGHT)
            with sp.Fori(0, B // IN_FLIGHT) as g:
                for z in range(IN_FLIGHT):
                    sp.wait_ge(c.s[f"scattered{z}"], 16 * TOPK * NT * (g + 1))
                    sp.sem_inc(c.s["normed_free"], 1)

        @block.gpsimd
        def _(pool):
            chain(c, pool, c.s["p_chain"], nc.gpsimd.memset(ones[:, :], 1.0))
            nc.gpsimd.memset(base[:, 0:1, :], 0.0)
            nc.gpsimd.memset(neg_half[:, :, :], -0.5)
            nc.gpsimd.affine_select(out=tri[:, :], in_=ones[:, :], compare_op=ALU.is_gt, fill=0.0, base=0,
                                    pattern=[[1, P]], channel_multiplier=-1)
            nc.gpsimd.iota(expert[:, 0, :], pattern=[[1, E]], base=0, channel_multiplier=0,
                           allow_small_or_imprecise_dtypes=True).then_inc(c.s["aux"], 1)
            pool.wait_ge(c.s["stats_ready"], start["ln"] + B)
            chain(c, pool, c.s["p_chain"], nc.gpsimd.tensor_scalar(inv_std[:, :, :], mean_var[:, :, :, 1], EPS, None,
                                                                   ALU.add))
            nc.gpsimd.tensor_tensor(inv_std[:, :, :], inv_std[:, :, :], neg_half[:, :, :], ALU.pow)\
              .then_inc(c.s["rstd_ready"], 1)

            def turn(b, z, more):
                pool.wait_ge(c.s["rows_ready"], b + 1)
                alone(c, pool)
                for i in range(TOPK):
                    for t in range(NT):
                        nc.gpsimd.indirect_dma_start(c.expert_in[:, :],
                                                     bass.IndirectOffsetOnAxis(ap=to_row[z][:, i, t:t + 1], axis=0),
                                                     normed[z][:, t, :], None, bounds_check=SLOTS_X - 1,
                                                     oob_is_err=False).then_inc(c.s[f"scattered{z}"], 16)
            grouped(c, pool, B, IN_FLIGHT, turn)

        @block.vector
        def _(dve):
            v = c.s["v_chain"]
            with dve.Fori(0, B) as b:
                for t in range(NT):
                    ins = nc.vector.bn_stats(c.bn[:, t, :], c.y[:, b, t, :])
                chain(c, dve, v, ins)
                for t in range(NT):
                    ins = nc.vector.bn_aggr(c.mv[:, t, :], c.bn[:, t, :])
                chain(c, dve, v, ins)
                nc.vector.tensor_copy(mean_var[:, b], c.mv[:, :, :]).then_inc(c.s["stats_ready"], 1)
                dve.wait_ge(c.s["stats_ready"], start["ln"] + b + 1)
                alone(c, dve)
            dve.wait_ge(c.s["rstd_ready"], start["ln"] + 1)
            dve.wait_ge(c.s["aux"], 7)

            def norm(b, z):
                dve.wait_ge(c.s["normed_free"], b + 1)
                alone(c, dve)
                for t in range(NT):
                    ins = nc.vector.tensor_scalar(normed[z][:, t, :], c.y[:, b, t, :], mean_var[:, b, t, 0:1],
                                                  inv_std[:, b, t:t + 1], ALU.subtract, ALU.mult)
                ins.then_inc(c.s["normed_ready"], 1)

            def over_experts(x):
                return x.unsqueeze(2).to_broadcast([P, NT, E])

            def turn(b, z, more):
                n = Span(start, ROUTE, b)
                if more:
                    norm(b + 1, (z + 1) % IN_FLIGHT)
                dve.wait_ge(c.s["vbank_full"], n("vb", 1))
                nc.vector.tensor_copy(lg[:, :, :], c.vbank[0][:, 0:NT * E].rearrange("p (t e) -> p t e", e=E))\
                  .then_inc(c.s["vbank_empty"], 1)
                dve.wait_ge(c.s["vbank_empty"], n("vb", 1))
                chain(c, dve, v, nc.vector.tensor_reduce(total[:, :], lg[:, :, :], AX.X, ALU.max))
                nc.vector.tensor_tensor(lg[:, :, :], lg[:, :, :], over_experts(total[:, :]), ALU.subtract)\
                  .then_inc(c.s["logits_shifted"], 1)
                dve.wait_ge(c.s["logits_exped"], n("mo", 1))
                chain(c, dve, v, nc.vector.tensor_reduce(total[:, :], lg[:, :, :], AX.X, ALU.add))
                chain(c, dve, v, nc.vector.reciprocal(total[:, :], total[:, :]))
                chain(c, dve, v, nc.vector.tensor_tensor(lg[:, :, :], lg[:, :, :], over_experts(total[:, :]),
                                                         ALU.mult))
                for t in range(NT):
                    ins = nc.vector.max(top[:, t, :], lg[:, t, :])
                chain(c, dve, v, ins)
                for t in range(NT):
                    ins = nc.vector.max_index(index[:, t, :], top[:, t, :], lg[:, t, :])
                chain(c, dve, v, ins)
                chain(c, dve, v, nc.vector.tensor_copy(chosen_by[:, :, :],
                                                       index[:, :, 0:TOPK].rearrange("p t i -> p i t")))
                for i in range(TOPK):
                    ins = nc.vector.tensor_tensor(hot[:, i, :, :], expert[:, :, :].to_broadcast([P, NT, E]),
                                                  over_experts(chosen_by[:, i, :]), ALU.is_equal)
                chain(c, dve, v, ins)
                nc.vector.tensor_tensor(chosen[:, :, :], hot[:, 0], hot[:, 1], ALU.add)\
                  .then_inc(c.s["chosen"], 1)
                chain(c, dve, v, nc.vector.tensor_tensor(total[:, :], top[:, :, 0], top[:, :, 1], ALU.add))
                chain(c, dve, v, nc.vector.reciprocal(total[:, :], total[:, :]))
                for i in range(TOPK):
                    nc.vector.tensor_tensor(weight[:, i, :], top[:, :, i], total[:, :], ALU.mult)
                nc.vector.tensor_scalar(first_row[:, :, :], chosen_by[:, :, :], float(CAP), None, ALU.mult)
                dve.wait_ge(c.s["vbank_full"], n("vb", 2))
                for t in range(NT):
                    at = NT * E + t * E
                    chain(c, dve, v, nc.vector.tensor_tensor(base[:, t + 1, :], base[:, t, :],
                                                             c.vbank[1][:, at:at + E], ALU.add))
                nc.vector.tensor_tensor(rank[:, :, :], base[:, 0:NT, :],
                                        c.vbank[1][:, 0:NT * E].rearrange("p (t e) -> p t e", e=E), ALU.add)\
                  .then_inc(c.s["vbank_empty"], 1)
                dve.wait_ge(c.s["vbank_empty"], n("vb", 2))
                nc.vector.tensor_copy(base[:, 0, :], base[:, NT, :])
                for i in range(TOPK):
                    ins = nc.vector.tensor_tensor(hot[:, i], hot[:, i], rank[:, :, :], ALU.mult)
                chain(c, dve, v, ins)
                chain(c, dve, v, nc.vector.tensor_reduce(place[:, :, :], hot[:, :, :, :], AX.X, ALU.add))
                chain(c, dve, v, nc.vector.tensor_scalar(kept[:, :, :], place[:, :, :], float(CAP), None, ALU.is_lt))
                nc.vector.tensor_tensor(c.share[:, b], weight[:, :, :], kept[:, :, :], ALU.mult)
                nc.vector.scalar_tensor_tensor(out=row_f[:, 0], in0=place[:, :, :], scalar=float(CAP - 1),
                                               in1=first_row[:, :, :], op0=ALU.min, op1=ALU.add)
                chain(c, dve, v, nc.vector.scalar_tensor_tensor(out=row_f[:, 1], in0=kept[:, :, :], scalar=-FAR,
                                                                in1=place[:, :, :], op0=ALU.mult, op1=ALU.add))
                nc.vector.tensor_copy(c.rows_of[:, b], row_f[:, 0])
                chain(c, dve, v, nc.vector.scalar_tensor_tensor(out=row_f[:, 1], in0=row_f[:, 1], scalar=FAR,
                                                                in1=first_row[:, :, :], op0=ALU.add, op1=ALU.add))
                nc.vector.tensor_copy(to_row[z][:, :, :], row_f[:, 1]).then_inc(c.s["rows_ready"], 1)
                dve.wait_ge(c.s["rows_ready"], b + 1)
                alone(c, dve)
            norm(0, 0)
            grouped(c, dve, B, IN_FLIGHT, turn)

        @block.scalar
        def _(act):
            act.wait_ge(c.s["load"], loaded)

            def gain(sbs):
                ln_gain(c, act, sbs, lambda k: c.gains[:, k:k + 1], lambda k: c.gains[:, 2 + k:3 + k])
            gain(start["sb"])

            def turn(b, z, more):
                n = Span(start, ROUTE, b)
                if more:
                    gain(n("sb", 2))
                act.wait_ge(c.s["logits_shifted"], n("mo", 1))
                nc.scalar.activation(lg[:, :, :], lg[:, :, :], ACT.Exp).then_inc(c.s["logits_exped"], 1)
            grouped(c, act, B, IN_FLIGHT, turn)

        @block.tensor
        def _(pe):
            pe.wait_ge(c.s["load"], loaded)
            pe.wait_ge(c.s["aux"], 7)

            def turned(n, z, row):
                pe.wait_ge(c.s["normed_ready"], n("ln", row + 1))
                for half in range(KD):
                    pe.wait_ge(c.s["sbank_empty"], n("sb", 2 * row + half - 1))
                    for t in range(NT):
                        ins = nc.tensor.transpose(c.sbank[half][:, t * P:(t + 1) * P],
                                                  normed[z][:, t, half * P:(half + 1) * P], c.ident[:, :])
                    ins.then_inc(c.s["sbank_full"], 1)
            turned(Span(start, ROUTE, 0), 0, 0)

            def turn(b, z, more):
                n = Span(start, ROUTE, b)
                pe.wait_ge(c.s["sbank_empty"], n("sb", 2))
                pe.wait_ge(c.s["vbank_empty"], n("vb", -1))
                for t in range(NT):
                    for k in range(KD):
                        ins = nc.tensor.matmul(c.vbank[0][:, t * E:(t + 1) * E], c.hT[:, k, 1 + t * P:1 + (t + 1) * P],
                                               wr[:, k, :], start=(k == 0), stop=(k == KD - 1))
                ins.then_inc(c.s["vbank_full"], 1)
                if more:
                    turned(n, (z + 1) % IN_FLIGHT, 1)
                pe.wait_ge(c.s["chosen"], n("mo", 1))
                pe.wait_ge(c.s["vbank_empty"], n("vb", 0))
                for i, m in enumerate((tri, ones)):
                    ins = nc.tensor.matmul(c.vbank[1][:, i * NT * E:(i + 1) * NT * E], m[:, :],
                                           chosen[:, :, :].rearrange("p t e -> p (t e)"), start=True, stop=True)
                ins.then_inc(c.s["vbank_full"], 1)
            grouped(c, pe, B, IN_FLIGHT, turn)
    c.loaded = loaded
    return after(start, ROUTE, B)


def experts(c, d, start):
    nc = c.nc
    n0 = after(start, {"sb": 1}, 1)
    with ExitStack() as st:
        def sb(name, shape, dt=F32):
            return st.enter_context(nc.sbuf_tensor(name, shape, dt))

        TT = CHUNK_T // P
        xin = [sb(f"xin{z}", [P, TT, D]) for z in range(2)]
        inT = [sb(f"inT{z}", [P, KD, CHUNK_T]) for z in range(2)]
        gT = [c.prob[:, 2 * z:2 * z + 2, :].rearrange("p i (m t) -> p (i m) t", t=CHUNK_T) for z in range(2)]
        yout = [sb(f"yout{z}", [P, TT, D]) for z in range(2)]
        block = st.enter_context(nc.Block())

        def rows(dram, at):
            return dram[bass.ds(at * CHUNK_T, CHUNK_T) if not isinstance(at, int)
                        else slice(at * CHUNK_T, (at + 1) * CHUNK_T), :].rearrange("(t p) n -> p t n", p=P)

        @block.sync
        def _(sp):
            for j in range(2):
                sp.dma_start(xin[j][:, :, :], rows(c.expert_in, j)).then_inc(c.s[f"chunk_in{j}"], 16)

            def pair(g, more):
                n = Span(n0, EXPERTS, g)
                for j in range(2, 2 * CHUNKS + 2 * more):
                    sp.wait_ge(c.s["sbank_full"], n("sb", 3 * (j - 2)))
                    sp.dma_start(xin[j % 2][:, :, :], rows(c.expert_in, 2 * CHUNKS * g + j))\
                      .then_inc(c.s[f"chunk_in{j % 2}"], 16)
                    if more and j == CHUNKS + 2:
                        weights(g, 0, n, CHUNKS)
                if more:
                    weights(g, 1, n, 2 * CHUNKS)

            def weights(g, z, n, done):
                sp.wait_ge(c.s["vbank_full"], n("vb", done))
                for to, name in ((c.w1, "we1"), (c.w2, "we2")):
                    src = d[name][2 * g + 2 + z] if isinstance(g, int) else d[name][bass.ds(2 * g + 2 + z, 1)]\
                        .rearrange("a k n -> (a k) n")
                    sp.dma_start(to[z][:, :, :], src.rearrange("(k p) n -> p k n", p=P))\
                      .then_inc(c.s[f"expert_weights{z}"], 16)
            loop(c, sp, E // 2, pair)

        @block.gpsimd
        def _(pool):
            pool.sem_inc(c.s["result_free"], 2)

            def pair(g, more):
                n = Span(n0, EXPERTS, g)
                for j in range(2 * CHUNKS):
                    pool.wait_ge(c.s["vbank_empty"], n("vb", j + 1))
                    alone(c, pool)
                    pool.dma_start(rows(c.expert_out, 2 * CHUNKS * g + j), yout[j % 2][:, :, :])\
                        .then_inc(c.s["result_stored"], 16)
                    pool.wait_ge(c.s["result_stored"], 16 * n("ck", j + 1))
                    pool.sem_inc(c.s["result_free"], 1)
            loop(c, pool, E // 2, pair)

        @block.vector
        def _(dve):
            def pair(g, more):
                n = Span(n0, EXPERTS, g)
                for j in range(2 * CHUNKS):
                    dve.wait_ge(c.s["result_free"], n("ck", j + 1))
                    dve.wait_ge(c.s["vbank_full"], n("vb", j + 1))
                    nc.vector.tensor_copy(yout[j % 2][:, :, :], c.vbank[j % 2][:, :].rearrange("p (t n) -> p t n", n=D))\
                      .then_inc(c.s["vbank_empty"], 1)
            loop(c, dve, E // 2, pair)

        @block.scalar
        def _(act):
            def gain(z, bank, job):
                act.wait_ge(c.s["sbank_full"], job + 1)
                for k in range(KD):
                    ins = nc.scalar.activation(inT[z][:, k, :], c.sbank[bank][:, k * CHUNK_T:(k + 1) * CHUNK_T],
                                               ACT.Identity, bias=c.gains[:, 2 + k:3 + k],
                                               scale=c.gains[:, k:k + 1])
                ins.then_inc(c.s["sbank_empty"], 1)
            gain(0, 0, start["sb"])

            def pair(g, more):
                n = Span(n0, EXPERTS, g)
                for j in range(2 * CHUNKS):
                    for i in range(2):
                        act.wait_ge(c.s["sbank_full"], n("sb", 3 * j + i + 1))
                        nc.scalar.activation(gT[j % 2][:, 2 * i:2 * i + 2, :],
                                             c.sbank[(3 * j + i + 1) % 2][:, :].rearrange("p (m t) -> p m t", m=2),
                                             ACT.Gelu_apprx_tanh).then_inc(c.s["sbank_empty"], 1)
                    if more or j < 2 * CHUNKS - 1:
                        act.wait_ge(c.s["sbank_full"], n("sb", 3 * j + 3))
                        alone(c, act)
                        gain((j + 1) % 2, (3 * j + 3) % 2, n("sb", 3 * j + 2))
            loop(c, act, E // 2, pair)

        @block.tensor
        def _(pe):
            def turned(z, bank, count, job):
                pe.wait_ge(c.s[f"chunk_in{z}"], 16 * count)
                pe.wait_ge(c.s["sbank_empty"], job - 1)
                for k in range(KD):
                    for t in range(TT):
                        at = k * CHUNK_T + t * P
                        ins = nc.tensor.transpose(c.sbank[bank][:, at:at + P], xin[z][:, t, k * P:(k + 1) * P],
                                                  c.ident[:, :])
                ins.then_inc(c.s["sbank_full"], 1)
            turned(0, 0, 1, start["sb"])

            def pair(g, more):
                n = Span(n0, EXPERTS, g)

                def up(j):
                    z = j // CHUNKS
                    if j % CHUNKS == 0:
                        pe.wait_ge(c.s[f"expert_weights{z}"], 32 * (g + 1))
                        alone(c, pe)
                    pe.wait_ge(c.s["sbank_empty"], n("sb", 3 * j))
                    for i in range(2):
                        pe.wait_ge(c.s["sbank_empty"], n("sb", 3 * j + i - 1))
                        for m in (2 * i, 2 * i + 1):
                            for k in range(KD):
                                ins = nc.tensor.matmul(
                                    c.sbank[(3 * j + i + 1) % 2][:, (m % 2) * CHUNK_T:(m % 2 + 1) * CHUNK_T],
                                    c.w1[z][:, k, m * P:(m + 1) * P], inT[j % 2][:, k, :],
                                    start=(k == 0), stop=(k == KD - 1))
                        ins.then_inc(c.s["sbank_full"], 1)

                def down(j):
                    z = j // CHUNKS
                    pe.wait_ge(c.s["sbank_empty"], n("sb", 3 * j + 2))
                    pe.wait_ge(c.s["vbank_empty"], n("vb", j - 1))
                    for t in range(TT):
                        for k in range(KF):
                            ins = nc.tensor.matmul(c.vbank[j % 2][:, t * D:(t + 1) * D],
                                                   gT[j % 2][:, k, t * P:(t + 1) * P], c.w2[z][:, k, :],
                                                   start=(k == 0), stop=(k == KF - 1))
                    ins.then_inc(c.s["vbank_full"], 1)

                for j in range(2 * CHUNKS):
                    up(j)
                    if more or j < 2 * CHUNKS - 1:
                        turned((j + 1) % 2, (3 * j + 3) % 2, CHUNKS * g + (j + 1) // 2 + 1, n("sb", 3 * j + 2))
                    if j:
                        down(j - 1)
                down(2 * CHUNKS - 1)
            loop(c, pe, E // 2, pair)
    return n0


def combine(c, out):
    nc = c.nc
    with ExitStack() as st:
        def sb(name, shape, dt=F32):
            return st.enter_context(nc.sbuf_tensor(name, shape, dt))

        got = [sb(f"got{z}", [P, TOPK, NT, D]) for z in range(2)]
        from_row = [sb(f"from_row{z}", [P, TOPK, NT], U32) for z in range(2)]
        share = [sb(f"share{z}", [P, TOPK, NT]) for z in range(2)]
        block = st.enter_context(nc.Block())
        each = 16 * TOPK * NT

        @block.sync
        def _(sp):
            with sp.Fori(0, B) as b:
                sp.wait_ge(c.s["finished"], b + 1)
                sp.dma_start(out[b].rearrange("(t p) n -> p t n", p=P), c.x[:, b]).then_inc(c.s["stored"], 16)
            sp.wait_ge(c.s["stored"], 16 * B)

        @block.gpsimd
        def _(pool):
            def turn(b, z, more):
                pool.wait_ge(c.s["rows_copied"], b + 1)
                alone(c, pool)
                for t in range(NT):
                    for i in range(TOPK):
                        nc.gpsimd.indirect_dma_start(got[z][:, i, t, :], None, c.expert_out[:, :],
                                                     bass.IndirectOffsetOnAxis(ap=from_row[z][:, i, t:t + 1], axis=0))\
                          .then_inc(c.s[f"gathered{z}"], 16)
            grouped(c, pool, B, 2, turn)

        @block.vector
        def _(dve):
            v = c.s["v_chain"]

            def places(b, z):
                nc.vector.tensor_copy(share[z][:, :, :], c.share[:, b])
                nc.vector.tensor_copy(from_row[z][:, :, :], c.rows_of[:, b]).then_inc(c.s["rows_copied"], 1)
            for z in range(2):
                places(z, z)

            def turn(g, z, more):
                b = 2 * g + z
                dve.wait_ge(c.s[f"gathered{z}"], each * (g + 1))
                alone(c, dve)
                for i in range(TOPK):
                    for t in range(NT):
                        y = c.y[:, b, t, :]
                        ins = nc.vector.scalar_tensor_tensor(out=y, in0=got[z][:, i, t, :], scalar=share[z][:, i, t:t + 1],
                                                             in1=y, op0=ALU.mult, op1=ALU.add)
                    chain(c, dve, v, ins)
                if more:
                    places(b + 2, z)
                chain(c, dve, v, nc.vector.tensor_tensor(c.y[:, b], c.y[:, b], row_of(c.gate, b).to_broadcast([P, NT, D]),
                                                         ALU.mult))
                nc.vector.tensor_tensor(c.x[:, b], c.x[:, b], c.y[:, b], ALU.add).then_inc(c.s["finished"], 1)

            def both(i, more):
                for z in range(2):
                    turn(i, z, more)
            loop(c, dve, B // 2, both)


def build(nc, d, outs):
    with ExitStack() as st:
        c = Chip()
        c.nc = nc
        c.s = {name: st.enter_context(nc.semaphore(name)) for name in SEMS}

        def sb(name, shape, dt=F32):
            return st.enter_context(nc.sbuf_tensor(name, shape, dt))

        def pair(name):
            return [st.enter_context(nc.psum_tensor(f"{name}{i}", [P, T], F32)) for i in range(2)]

        c.x = sb("x", [P, B, NT, D])
        c.y = sb("y", [P, B, NT, D])
        c.hT = sb("hT", [P, KD, T + 1])
        c.xn = sb("xn", [P, NT, D])
        c.ident = sb("ident", [P, P])
        c.modT = sb("modT", [P, 4, KD, B])
        c.bn = sb("bn", [P, NT, 6])
        c.mv = sb("mv", [P, NT, 2])
        c.ve = sb("ve", [P, NT])
        c.rstd = sb("rstd", [P, NT])
        c.mhalf = sb("mhalf", [P, NT])
        c.score = sb("score", [P, 4, T])
        c.prob = sb("prob", [P, 8, T])
        c.probT = sb("probT", [P, 8, T])
        c.least = sb("least", [P, 8])
        c.psum_of = sb("psum_of", [P, 8])
        c.rsum = sb("rsum", [P, 8])
        c.vbank, c.pbank, c.sbank, c.obank = pair("vbank"), pair("pbank"), pair("sbank"), pair("obank")
        c.mod_dram = nc.dram_tensor("modulation", (2, B, 6 * D), F32).ap()
        c.expert_in = nc.dram_tensor("expert_in", (SLOTS_X, D), F32).ap()
        c.expert_out = nc.dram_tensor("expert_out", (SLOTS_X, D), F32).ap()
        c.loaded = 64
        opening(c, d)
        n = layer0(c, d, dict(OPENING))
        n = remix(c, d, n, None, "ca", "sa")
        n = layer1(c, d, n)
        n = remix(c, d, n, "ga", "cb", "sb")
        n = cross(c, d, n)
        moe(c, d, n, outs[0])


def kernel(**inputs):
    import numpy as np
    import concourse.bacc as bacc
    from concourse.bass_utils import run_bass_kernel_spmd

    inputs = {k: np.asarray(v) for k, v in inputs.items()}
    arrays = {"x": inputs["L0_attn_x"]}
    for short, name in (("qw", "q_w"), ("kw", "k_w"), ("vw", "v_w"), ("ow", "o_w")):
        arrays[short] = inputs[f"L0_attn_{name}"]
    for l in range(2):
        arrays[f"c{l}"] = inputs[f"L{l}_c"].T
        arrays[f"wmod{l}"] = inputs[f"L{l}_wmod"]
    for short, name in (("Wr", "W_r"), ("Wk", "W_k"), ("Wv", "W_v")):
        arrays[short] = inputs[f"L0_ffn_{name}"].T
    for name in ("mu_r", "mu_k"):
        arrays[name] = inputs[f"L0_ffn_{name}"].reshape(KD, P).T
    for short, name in (("Aq", "Wq"), ("Ak", "Wk"), ("Ao", "Wo"), ("W1", "W1"), ("W2", "W2"), ("bo", "bo"), ("b2", "b2")):
        arrays[short] = inputs[f"L1_attn_{name}"]
    wide = [inputs[f"L1_attn_{name}"] for name in ("Wq", "Wk", "Wv")]
    arrays["wtok"] = np.concatenate([wide[0][:, :, P:], wide[1][:, :, P:], wide[2]], axis=2)
    by_feature = [inputs[f"L1_attn_{name}"].reshape(DEPTH, -1, P) for name in ("ln1_g", "ln1_b", "ln2_g", "ln2_b", "b1")]
    arrays["vec"] = np.concatenate(by_feature, axis=1).transpose(2, 0, 1)
    for short, name in (("wqkv", "qkv_weight"), ("wproj", "proj_weight")):
        arrays[short] = inputs[f"L1_ffn_{name}"].T
    for short, ln in (("cross_ln", "ln1"), ("moe_ln", "ln2")):
        both = [inputs[f"L1_ffn_{ln}_{name}"].reshape(KD, P) for name in ("weight", "bias")]
        arrays[short] = np.concatenate(both).T
    for short, name in (("wrouter", "router_weight"), ("we1", "moe_w1"), ("we2", "moe_w2")):
        arrays[short] = inputs[f"L1_ffn_{name}"]
    arrays = {k: np.ascontiguousarray(v) for k, v in arrays.items()}
    nc = bacc.Bacc("TRN2", target_bir_lowering=False, num_devices=1)
    d = {k: nc.dram_tensor(f"in_{k}", v.shape, mybir.dt.from_np(v.dtype), kind="ExternalInput").ap()
         for k, v in arrays.items()}
    out = nc.dram_tensor("out_x", (B, T, D), F32, kind="ExternalOutput").ap()
    build(nc, d, [out])
    r = run_bass_kernel_spmd(nc, [{f"in_{k}": v for k, v in arrays.items()}], core_ids=[0])
    return r.results[0]["out_x"]
```
